# Optimizing a Trainium2 kernel written in Bass

```python
import numpy as np
import jax
import jax.numpy as jnp

def _softmax(x, axis=-1):
    return jax.nn.softmax(x, axis=axis)

def _gelu(x):
    return jax.nn.gelu(x, approximate=True)

def _silu(x):
    return jax.nn.silu(x)

def _sigmoid(x):
    return jax.nn.sigmoid(x)

def _layernorm(x, axis=-1, eps=1e-05):
    m = jnp.mean(x, axis=axis, keepdims=True)
    v = jnp.var(x, axis=axis, keepdims=True)
    return (x - m) / jnp.sqrt(v + eps)

def _scatter_add(tgt, idx, src, axis=0):
    return tgt.at[idx].add(src)

def _segment_sum(src, seg, n):
    return jax.ops.segment_sum(src, seg, n)
kernel_name = 'mk_xattn_ffn_d2_seqx_r4_6098ec'

def setup_inputs(seed: int=0):
    np.random.seed(seed)
    _w = jnp.asarray

    def _rec_inputs():
        import jax
        import jax.numpy as jnp
        _rk = jax.random.key(seed)
        x = 7.22e-05 + 1 * jax.random.normal(jax.random.fold_in(_rk, 1), (8, 512, 256), jnp.float32)
        _lenS = 512 - jax.random.randint(jax.random.fold_in(_rk, 7), (8,), 0, max(1, 512 // 4) + 1, jnp.int32)
        _lenS2 = 64 - jax.random.randint(jax.random.fold_in(_rk, 8), (8,), 0, max(1, 64 // 4) + 1, jnp.int32)
        _ctx_768P = jax.random.normal(jax.random.fold_in(_rk, 11), (8, 16, 192), jnp.float32)
        _ctx_768c = jax.random.dirichlet(jax.random.fold_in(_rk, 511), 0.3 * jnp.ones((16,), jnp.float32), (8, 64))
        _ctx_768t = jnp.einsum('bsk,bkd->bsd', _ctx_768c, _ctx_768P)
        _ctx_768t = _ctx_768t * jax.lax.rsqrt(jnp.mean(jnp.square(_ctx_768t)) + 1e-12) * 0.953939
        ctx_768 = -0.000191848 + 0.999787 * (_ctx_768t + 0.3 * jax.random.normal(jax.random.fold_in(_rk, 611), (8, 64, 192), jnp.float32))
        _validS = jnp.arange(512)[None, :] < _lenS[:, None]
        _validS2 = jnp.arange(64)[None, :] < _lenS2[:, None]
        _causal = jnp.tril(jnp.ones((512, 512), dtype=bool))
        mask_BxS2_bk0 = jnp.logical_not(jnp.broadcast_to(_validS2[:, :], (8, 64)))
        mask_BxS_bf1 = jnp.ones((8, 512), dtype=bool)
        mask_BxS2_bf1 = jnp.ones((8, 64), dtype=bool)
        return (x, ctx_768, mask_BxS2_bk0, mask_BxS_bf1, mask_BxS2_bf1)
    x, ctx_768, mask_BxS2_bk0, mask_BxS_bf1, mask_BxS2_bf1 = _rec_inputs()

    def _L0_xattn_setup():
        import jax, jax.numpy as jnp
        import numpy as np
        HEADS = 8
        DIM_HEAD = 64
        QUERY_DIM = 256
        CONTEXT_DIM = 192
        INNER = HEADS * DIM_HEAD
        key = jax.random.key(seed)
        ks = jax.random.split(key, 8)
        b, n, j = (4, 512, 512)
        x = jax.random.normal(ks[0], (b, n, QUERY_DIM), dtype=jnp.float32)
        context = jax.random.normal(ks[1], (b, j, CONTEXT_DIM), dtype=jnp.float32)
        mask = jax.random.randint(ks[2], (b, j), 0, 2).astype(jnp.bool_)
        W_q = jax.random.normal(ks[3], (QUERY_DIM, INNER), dtype=jnp.float32) / np.sqrt(QUERY_DIM)
        W_k = jax.random.normal(ks[4], (CONTEXT_DIM, INNER), dtype=jnp.float32) / np.sqrt(CONTEXT_DIM)
        W_v = jax.random.normal(ks[5], (CONTEXT_DIM, INNER), dtype=jnp.float32) / np.sqrt(CONTEXT_DIM)
        W_o = jax.random.normal(ks[6], (INNER, QUERY_DIM), dtype=jnp.float32) / np.sqrt(INNER)
        b_o = jax.random.normal(ks[7], (QUERY_DIM,), dtype=jnp.float32) * 0.01
        return {'x': x, 'context': context, 'mask': mask, 'W_q': W_q, 'W_k': W_k, 'W_v': W_v, 'W_o': W_o, 'b_o': b_o}
    _L0_xattn_all = _L0_xattn_setup()
    _L0_xattn_in = {k: v for k, v in _L0_xattn_all.items() if k in ('W_q', 'W_k', 'W_v', 'W_o', 'b_o')}
    del _L0_xattn_all

    def _L0_ffn_setup():
        import jax, jax.numpy as jnp
        import numpy as np
        DMODEL = 256
        N_EXPERTS = 16
        EXPERT_SIZE = 64
        K = 4
        key = jax.random.key(seed)
        k1, k2, k3, k4 = jax.random.split(key, 4)
        std_sel = 1.0 / np.sqrt(DMODEL)
        std_val = 1.0 / np.sqrt(N_EXPERTS * EXPERT_SIZE)
        return {'x': jax.random.normal(k1, (4, 512, DMODEL), dtype=jnp.float32), 'expert_sel': jax.random.normal(k2, (N_EXPERTS, DMODEL), dtype=jnp.float32) * std_sel, 'keys': jax.random.normal(k3, (N_EXPERTS, DMODEL, EXPERT_SIZE), dtype=jnp.float32) * std_sel, 'values': jax.random.normal(k4, (N_EXPERTS, EXPERT_SIZE, DMODEL), dtype=jnp.float32) * std_val, 'route_scale': jnp.ones((1,), dtype=jnp.float32)}
    _L0_ffn_all = _L0_ffn_setup()
    _L0_ffn_in = {k: v for k, v in _L0_ffn_all.items() if k in ('expert_sel', 'keys', 'values', 'route_scale')}
    del _L0_ffn_all

    def _L1_xattn_setup():
        import jax, jax.numpy as jnp
        import numpy as np
        B, T, DT, G, DV = (16, 128, 256, 144, 192)
        H, DH = (4, 32)
        INNER = H * DH
        HID = 4 * DT
        N_STATE = 64
        K_TOP = 32

        def layernorm(x, g, b, eps=1e-05):
            m = x.mean(-1, keepdims=True)
            v = x.var(-1, keepdims=True)
            return (x - m) * jax.lax.rsqrt(v + eps) * g + b

        def s4d(x, log_dt, A_re, A_im, C_re, C_im, D_skip):
            Bb, L, D = x.shape
            dt = jnp.exp(log_dt)
            A = A_re + 1j * A_im
            C = C_re + 1j * C_im
            dtA = dt[:, None] * A
            dC = C * (jnp.exp(dtA) - 1.0) / A
            powers = jnp.exp(dtA[:, :, None] * jnp.arange(L))
            K = 2.0 * jnp.einsum('dn,dnl->dl', dC, powers).real
            n = 2 * L
            Kf = jnp.fft.rfft(K, n=n, axis=-1)
            xf = jnp.fft.rfft(x, n=n, axis=1)
            y = jnp.fft.irfft(xf * Kf.T[None], n=n, axis=1)[:, :L]
            return y + x * D_skip
        key = jax.random.key(seed)
        ks = jax.random.split(key, 16)
        s = 0.02
        inp = {'x_text': jax.random.normal(ks[0], (B, T, DT), jnp.float32), 'x_vision': jax.random.normal(ks[1], (B, G, DV), jnp.float32), 'text_mask': jnp.ones((B, T), bool), 'vision_mask': jnp.ones((B, G), bool), 'Wq': jax.random.normal(ks[2], (DT, INNER), jnp.float32) * s, 'Wk': jax.random.normal(ks[3], (DV, INNER), jnp.float32) * s, 'Wv': jax.random.normal(ks[4], (DV, DT), jnp.float32) * s, 'W_film_in': jax.random.normal(ks[5], (DT, 2 * DT), jnp.float32) * s, 'b_film_in': jnp.zeros((2 * DT,), jnp.float32), 'W_film_out': jax.random.normal(ks[6], (DT, 2 * DT), jnp.float32) * s, 'b_film_out': jnp.zeros((2 * DT,), jnp.float32), 'g_norm_in': jnp.ones((DT,), jnp.float32), 'b_norm_in': jnp.zeros((DT,), jnp.float32), 'g_norm_out': jnp.ones((DT,), jnp.float32), 'b_norm_out': jnp.zeros((DT,), jnp.float32), 'g_ffn': jnp.ones((DT,), jnp.float32), 'b_ffn': jnp.zeros((DT,), jnp.float32), 'W1': jax.random.normal(ks[7], (DT, HID), jnp.float32) * s, 'b1': jnp.zeros((HID,), jnp.float32), 'W2': jax.random.normal(ks[8], (HID, DT), jnp.float32) * s, 'b2': jnp.zeros((DT,), jnp.float32), 'log_dt': jnp.log(0.001) + jax.random.uniform(ks[9], (DT,), jnp.float32) * (jnp.log(0.1) - jnp.log(0.001)), 'A_re': -0.5 * jnp.ones((DT, N_STATE), jnp.float32), 'A_im': jnp.tile(jnp.pi * jnp.arange(N_STATE, dtype=jnp.float32), (DT, 1)), 'C_re': jax.random.normal(ks[10], (DT, N_STATE), jnp.float32) * 0.5 ** 0.5, 'C_im': jax.random.normal(ks[11], (DT, N_STATE), jnp.float32) * 0.5 ** 0.5, 'D_skip': jax.random.normal(ks[12], (DT,), jnp.float32), 'mod_gate': jnp.array(0.5, jnp.float32)}
        return inp
    _L1_xattn_all = _L1_xattn_setup()
    _L1_xattn_in = {k: v for k, v in _L1_xattn_all.items() if k in ('Wq', 'Wk', 'Wv', 'W_film_in', 'b_film_in', 'W_film_out', 'b_film_out', 'g_norm_in', 'b_norm_in', 'g_norm_out', 'b_norm_out', 'g_ffn', 'b_ffn', 'W1', 'b1', 'W2', 'b2', 'log_dt', 'A_re', 'A_im', 'C_re', 'C_im', 'D_skip', 'mod_gate')}
    del _L1_xattn_all

    def _L1_ffn_setup():
        import jax, jax.numpy as jnp
        import numpy as np
        EMBED_DIM = 256
        MLP_RATIO = 4
        NUM_EXPERTS = 8
        CAPACITY = 1.0
        LN_EPS = 1e-05

        def _layernorm(y, gamma, beta):
            mu = jnp.mean(y, axis=-1, keepdims=True)
            var = jnp.mean(jnp.square(y - mu), axis=-1, keepdims=True)
            return (y - mu) * jax.lax.rsqrt(var + LN_EPS) * gamma + beta
        key = jax.random.key(seed)
        k0, k1, k2, k3, k4, k5 = jax.random.split(key, 6)
        d = EMBED_DIM
        dd = EMBED_DIM * MLP_RATIO
        n = NUM_EXPERTS
        x = jax.random.normal(k0, (4, 512, d), dtype=jnp.float32)
        gate_w = jax.random.normal(k1, (n, d), dtype=jnp.float32) * 0.02
        ln_gamma = jnp.ones((d,), dtype=jnp.float32)
        ln_beta = jnp.zeros((d,), dtype=jnp.float32)
        fc1s = jax.random.normal(k2, (n, dd, d), dtype=jnp.float32) * (1.0 / np.sqrt(d))
        b1s = jax.random.normal(k3, (n, dd), dtype=jnp.float32) * 0.02
        fc2s = jax.random.normal(k4, (n, d, dd), dtype=jnp.float32) * (1.0 / np.sqrt(dd))
        b2s = jax.random.normal(k5, (n, d), dtype=jnp.float32) * 0.02
        return {'x': x, 'gate_w': gate_w, 'ln_gamma': ln_gamma, 'ln_beta': ln_beta, 'fc1s': fc1s, 'b1s': b1s, 'fc2s': fc2s, 'b2s': b2s}
    _L1_ffn_all = _L1_ffn_setup()
    _L1_ffn_in = {k: v for k, v in _L1_ffn_all.items() if k in ('gate_w', 'ln_gamma', 'ln_beta', 'fc1s', 'b1s', 'fc2s', 'b2s')}
    del _L1_ffn_all
    return {'x': x, 'ctx_768': ctx_768, 'mask_BxS2_bk0': mask_BxS2_bk0, 'mask_BxS_bf1': mask_BxS_bf1, 'mask_BxS2_bf1': mask_BxS2_bf1, 'L0_xattn_W_q': _L0_xattn_in['W_q'], 'L0_xattn_W_k': _L0_xattn_in['W_k'], 'L0_xattn_W_v': _L0_xattn_in['W_v'], 'L0_xattn_W_o': _L0_xattn_in['W_o'], 'L0_xattn_b_o': _L0_xattn_in['b_o'], 'L0_ffn_expert_sel': _L0_ffn_in['expert_sel'], 'L0_ffn_keys': _L0_ffn_in['keys'], 'L0_ffn_values': _L0_ffn_in['values'], 'L0_ffn_route_scale': _L0_ffn_in['route_scale'], 'L1_xattn_Wq': _L1_xattn_in['Wq'], 'L1_xattn_Wk': _L1_xattn_in['Wk'], 'L1_xattn_Wv': _L1_xattn_in['Wv'], 'L1_xattn_W_film_in': _L1_xattn_in['W_film_in'], 'L1_xattn_b_film_in': _L1_xattn_in['b_film_in'], 'L1_xattn_W_film_out': _L1_xattn_in['W_film_out'], 'L1_xattn_b_film_out': _L1_xattn_in['b_film_out'], 'L1_xattn_g_norm_in': _L1_xattn_in['g_norm_in'], 'L1_xattn_b_norm_in': _L1_xattn_in['b_norm_in'], 'L1_xattn_g_norm_out': _L1_xattn_in['g_norm_out'], 'L1_xattn_b_norm_out': _L1_xattn_in['b_norm_out'], 'L1_xattn_g_ffn': _L1_xattn_in['g_ffn'], 'L1_xattn_b_ffn': _L1_xattn_in['b_ffn'], 'L1_xattn_W1': _L1_xattn_in['W1'], 'L1_xattn_b1': _L1_xattn_in['b1'], 'L1_xattn_W2': _L1_xattn_in['W2'], 'L1_xattn_b2': _L1_xattn_in['b2'], 'L1_xattn_log_dt': _L1_xattn_in['log_dt'], 'L1_xattn_A_re': _L1_xattn_in['A_re'], 'L1_xattn_A_im': _L1_xattn_in['A_im'], 'L1_xattn_C_re': _L1_xattn_in['C_re'], 'L1_xattn_C_im': _L1_xattn_in['C_im'], 'L1_xattn_D_skip': _L1_xattn_in['D_skip'], 'L1_xattn_mod_gate': _L1_xattn_in['mod_gate'], 'L1_ffn_gate_w': _L1_ffn_in['gate_w'], 'L1_ffn_ln_gamma': _L1_ffn_in['ln_gamma'], 'L1_ffn_ln_beta': _L1_ffn_in['ln_beta'], 'L1_ffn_fc1s': _L1_ffn_in['fc1s'], 'L1_ffn_b1s': _L1_ffn_in['b1s'], 'L1_ffn_fc2s': _L1_ffn_in['fc2s'], 'L1_ffn_b2s': _L1_ffn_in['b2s']}

def reference(x, ctx_768, mask_BxS2_bk0, mask_BxS_bf1, mask_BxS2_bf1, L0_xattn_W_q, L0_xattn_W_k, L0_xattn_W_v, L0_xattn_W_o, L0_xattn_b_o, L0_ffn_expert_sel, L0_ffn_keys, L0_ffn_values, L0_ffn_route_scale, L1_xattn_Wq, L1_xattn_Wk, L1_xattn_Wv, L1_xattn_W_film_in, L1_xattn_b_film_in, L1_xattn_W_film_out, L1_xattn_b_film_out, L1_xattn_g_norm_in, L1_xattn_b_norm_in, L1_xattn_g_norm_out, L1_xattn_b_norm_out, L1_xattn_g_ffn, L1_xattn_b_ffn, L1_xattn_W1, L1_xattn_b1, L1_xattn_W2, L1_xattn_b2, L1_xattn_log_dt, L1_xattn_A_re, L1_xattn_A_im, L1_xattn_C_re, L1_xattn_C_im, L1_xattn_D_skip, L1_xattn_mod_gate, L1_ffn_gate_w, L1_ffn_ln_gamma, L1_ffn_ln_beta, L1_ffn_fc1s, L1_ffn_b1s, L1_ffn_fc2s, L1_ffn_b2s):
    import jax
    import jax.numpy as jnp

    def _L0_xattn_ref(x, context, mask, W_q, W_k, W_v, W_o, b_o):
        import jax, jax.numpy as jnp
        import numpy as np
        HEADS = 8
        DIM_HEAD = 64
        QUERY_DIM = 256
        CONTEXT_DIM = 192
        INNER = HEADS * DIM_HEAD
        b, n, _ = x.shape
        j = context.shape[1]
        scale = DIM_HEAD ** (-0.5)
        q = (x @ W_q).reshape(b, n, HEADS, DIM_HEAD)
        k = (context @ W_k).reshape(b, j, HEADS, DIM_HEAD)
        v = (context @ W_v).reshape(b, j, HEADS, DIM_HEAD)
        sim = jnp.einsum('bihd,bjhd->bhij', q, k) * scale
        max_neg = -jnp.finfo(sim.dtype).max
        sim = jnp.where(mask[:, None, None, :], sim, max_neg)
        attn = jax.nn.softmax(sim, axis=-1)
        out = jnp.einsum('bhij,bjhd->bihd', attn, v).reshape(b, n, INNER)
        return out @ W_o + b_o

    def _L0_ffn_ref(x, expert_sel, keys, values, route_scale):
        import jax, jax.numpy as jnp
        import numpy as np
        DMODEL = 256
        N_EXPERTS = 16
        EXPERT_SIZE = 64
        K = 4
        sel_logits = jnp.einsum('btd,ed->bte', x, expert_sel)
        sel_probs = jax.nn.sigmoid(sel_logits)
        _, sel_index = jax.lax.top_k(sel_probs, K)
        sel_val = jnp.take_along_axis(sel_probs, sel_index, axis=-1)
        sel_val = sel_val / jnp.clip(sel_val.sum(-1, keepdims=True), 1e-09)
        sel_val = sel_val * route_scale
        scores_all = jax.nn.relu(jnp.einsum('btd,edh->bteh', x, keys))
        values_all = jnp.einsum('bteh,ehv->btev', scores_all, values)
        sel_idx_exp = sel_index[..., None]
        selected = jnp.take_along_axis(values_all, sel_idx_exp, axis=2)
        out = (selected * sel_val[..., None]).sum(axis=2)
        return out

    def _L1_xattn_ref(x_text, x_vision, text_mask, vision_mask, Wq, Wk, Wv, W_film_in, b_film_in, W_film_out, b_film_out, g_norm_in, b_norm_in, g_norm_out, b_norm_out, g_ffn, b_ffn, W1, b1, W2, b2, log_dt, A_re, A_im, C_re, C_im, D_skip, mod_gate):
        import jax, jax.numpy as jnp
        import numpy as np
        B, T, DT, G, DV = (16, 128, 256, 144, 192)
        H, DH = (4, 32)
        INNER = H * DH
        HID = 4 * DT
        N_STATE = 64
        K_TOP = 32

        def layernorm(x, g, b, eps=1e-05):
            m = x.mean(-1, keepdims=True)
            v = x.var(-1, keepdims=True)
            return (x - m) * jax.lax.rsqrt(v + eps) * g + b

        def s4d(x, log_dt, A_re, A_im, C_re, C_im, D_skip):
            Bb, L, D = x.shape
            dt = jnp.exp(log_dt)
            A = A_re + 1j * A_im
            C = C_re + 1j * C_im
            dtA = dt[:, None] * A
            dC = C * (jnp.exp(dtA) - 1.0) / A
            powers = jnp.exp(dtA[:, :, None] * jnp.arange(L))
            K = 2.0 * jnp.einsum('dn,dnl->dl', dC, powers).real
            n = 2 * L
            Kf = jnp.fft.rfft(K, n=n, axis=-1)
            xf = jnp.fft.rfft(x, n=n, axis=1)
            y = jnp.fft.irfft(xf * Kf.T[None], n=n, axis=1)[:, :L]
            return y + x * D_skip
        Bb, Tt, D = x_text.shape
        Gg = x_vision.shape[1]
        Q = (x_text @ Wq).reshape(Bb, Tt, H, DH)
        K = (x_vision @ Wk).reshape(Bb, Gg, H, DH)
        scores = jnp.einsum('bthd,bghd->bhtg', Q, K) / np.sqrt(DH).astype(np.float32)
        scores = jnp.where(vision_mask[:, None, None, :], scores, -jnp.inf)
        topv, topi = jax.lax.top_k(scores, K_TOP)
        probs = jax.nn.softmax(topv, axis=-1)
        bi = jnp.arange(Bb)[:, None, None, None]
        hi = jnp.arange(H)[None, :, None, None]
        ti = jnp.arange(Tt)[None, None, :, None]
        attn = jnp.zeros_like(scores).at[bi, hi, ti, topi].set(probs)
        attn_mean = attn.mean(axis=1)
        V = x_vision @ Wv
        c_t = jnp.einsum('btg,bgd->btd', attn_mean, V)
        c_t = c_t * text_mask[..., None]
        x = layernorm(x_text, g_norm_in, b_norm_in)
        scale_in, shift_in = jnp.split(c_t @ W_film_in + b_film_in, 2, axis=-1)
        x = x * (1.0 + mod_gate * scale_in) + mod_gate * shift_in
        y = s4d(x, log_dt, A_re, A_im, C_re, C_im, D_skip)
        scale_out, shift_out = jnp.split(c_t @ W_film_out + b_film_out, 2, axis=-1)
        y = y * (1.0 + mod_gate * scale_out) + mod_gate * shift_out
        xt = x_text + y
        h = layernorm(xt, g_ffn, b_ffn)
        h = jax.nn.gelu(h @ W1 + b1, approximate=False) @ W2 + b2
        xt = xt + h
        return layernorm(xt, g_norm_out, b_norm_out)

    def _L1_ffn_ref(x, gate_w, ln_gamma, ln_beta, fc1s, b1s, fc2s, b2s):
        import jax, jax.numpy as jnp
        import numpy as np
        EMBED_DIM = 256
        MLP_RATIO = 4
        NUM_EXPERTS = 8
        CAPACITY = 1.0
        LN_EPS = 1e-05

        def _layernorm(y, gamma, beta):
            mu = jnp.mean(y, axis=-1, keepdims=True)
            var = jnp.mean(jnp.square(y - mu), axis=-1, keepdims=True)
            return (y - mu) * jax.lax.rsqrt(var + LN_EPS) * gamma + beta
        og_shape = x.shape
        d = og_shape[-1]
        xf = x.reshape(-1, d)
        bs = xf.shape[0]
        n = gate_w.shape[0]
        k = int(bs * CAPACITY) // n
        scores = xf @ gate_w.T
        scores = (jnp.tanh(scores) + 1.0) * 0.5
        vals, idx = jax.lax.top_k(scores.T, k)
        kept_w = vals.T
        flat_idx = idx.T.reshape(-1)
        y = xf[flat_idx].reshape(k, n, d)
        y = _layernorm(y, ln_gamma, ln_beta)
        h = jnp.einsum('knd,nfd->knf', y, fc1s) + b1s
        h = jax.nn.gelu(h, approximate=True)
        o = jnp.einsum('knf,ndf->knd', h, fc2s) + b2s
        o = o * kept_w[:, :, None]
        out = xf.at[flat_idx].add(o.reshape(k * n, d))
        return out.reshape(og_shape)
    x = x + _L0_xattn_ref(_layernorm(x, axis=-1), ctx_768, mask_BxS2_bk0, L0_xattn_W_q, L0_xattn_W_k, L0_xattn_W_v, L0_xattn_W_o, L0_xattn_b_o)
    x = x + _L0_ffn_ref(_layernorm(x, axis=-1), L0_ffn_expert_sel, L0_ffn_keys, L0_ffn_values, L0_ffn_route_scale)
    x = x + _L1_xattn_ref(_layernorm(x, axis=-1), ctx_768, mask_BxS_bf1, mask_BxS2_bf1, L1_xattn_Wq, L1_xattn_Wk, L1_xattn_Wv, L1_xattn_W_film_in, L1_xattn_b_film_in, L1_xattn_W_film_out, L1_xattn_b_film_out, L1_xattn_g_norm_in, L1_xattn_b_norm_in, L1_xattn_g_norm_out, L1_xattn_b_norm_out, L1_xattn_g_ffn, L1_xattn_b_ffn, L1_xattn_W1, L1_xattn_b1, L1_xattn_W2, L1_xattn_b2, L1_xattn_log_dt, L1_xattn_A_re, L1_xattn_A_im, L1_xattn_C_re, L1_xattn_C_im, L1_xattn_D_skip, L1_xattn_mod_gate)
    x = x + _L1_ffn_ref(_layernorm(x, axis=-1), L1_ffn_gate_w, L1_ffn_ln_gamma, L1_ffn_ln_beta, L1_ffn_fc1s, L1_ffn_b1s, L1_ffn_fc2s, L1_ffn_b2s)
    return x

_drawn_inputs = setup_inputs


def setup_inputs(seed=0):
    import zlib

    import numpy as np

    out = dict(_drawn_inputs(seed))
    spreads = {'L1_xattn_b_film_in': (0.0, 0.1),
     'L1_xattn_b_film_out': (0.0, 0.1),
     'L1_xattn_g_norm_in': (1.0, 0.2),
     'L1_xattn_b_norm_in': (0.0, 0.1),
     'L1_xattn_g_norm_out': (1.0, 0.2),
     'L1_xattn_b_norm_out': (0.0, 0.1),
     'L1_xattn_g_ffn': (1.0, 0.6),
     'L1_xattn_b_ffn': (0.0, 0.79),
     'L1_xattn_b1': (0.0, 0.522),
     'L1_xattn_b2': (0.0, 0.276),
     'L1_xattn_A_re': (-0.5, 0.2),
     'L1_ffn_ln_gamma': (1.0, 0.2),
     'L1_ffn_ln_beta': (0.0, 0.483)}
    factors = {'L0_xattn_b_o': 3.838,
     'L1_xattn_Wq': 5.854,
     'L1_xattn_Wk': 5.943,
     'L1_xattn_W_film_out': 2.744,
     'L1_ffn_b1s': 8.0,
     'L1_ffn_b2s': 8.0}
    for name, (base, spread) in spreads.items():
        noise = np.random.default_rng([zlib.crc32(name.encode()), seed]).standard_normal(out[name].shape)
        drawn = base * np.exp(spread * noise) if base else spread * noise
        out[name] = jnp.asarray(drawn.astype(out[name].dtype))
    for name, factor in factors.items():
        out[name] = (out[name] * factor).astype(out[name].dtype)
    return out
```

```python
from contextlib import ExitStack

import concourse.bass as bass
from concourse import mybir

F32 = mybir.dt.float32
BF16 = mybir.dt.bfloat16
I32 = mybir.dt.int32
U8 = mybir.dt.uint8
U32 = mybir.dt.uint32
ALU = mybir.AluOpType
ACT = mybir.ActivationFunctionType
AX = mybir.AxisListType.X

P = 128
B, T, D = 8, 512, 256
NT = T // P
DC = D // P
N = B * T
J, CD = 64, 192
CK = CD // 2
H0, DH0 = 8, 64
H1, DH1 = 4, 32
C0 = H0 * DH0 // P
E0, ES = 16, 64
HID = 1024
HC = HID // P
KTOP0 = 4
ROUNDS = 4
NS = 64
FQ = 4
LI, LJ = 32, 16
E1, CAP = 8, N // 8
CC = CAP // P
EPS = 1e-5
FAR = -1e30
OUT_OF_RANGE = -3e38
MAGIC = 1.5 * 2.0 ** 23
TWO_PI = 6.2831845
TABLE_W = D + E1
PSUM_BANKS = 8


class Tally:

    def __init__(self, ctx, nc):
        self.ctx, self.nc = ctx, nc
        self.sems, self.place, self.per, self.base, self.by, self.next = {}, {}, {}, {}, {}, {}

    def declare(self, sem, events, base=0, by=1):
        self.sems[sem] = self.ctx.enter_context(self.nc.semaphore(sem))
        self.per[sem], self.base[sem], self.by[sem], self.next[sem] = len(events), base, by, 0
        for n, e in enumerate(events):
            assert e not in self.place, e
            self.place[e] = (sem, n)

    def at(self, b, *event):
        sem, n = self.place[event]
        by = self.by[sem]
        fixed = self.base[sem] + (n + 1) * by
        return self.sems[sem], (fixed if isinstance(b, int) and b == 0 else b * (self.per[sem] * by) + fixed)

    def last(self, b, *event):
        sem, n = self.place[event]
        fixed = self.base[sem] + (n + 1 - self.per[sem]) * self.by[sem]
        assert fixed > 0
        return self.sems[sem], b * (self.per[sem] * self.by[sem]) + fixed

    def tick(self, *event):
        sem, n = self.place[event]
        if event[0] == "emptied":
            return self.sems[sem], 1
        assert n == self.next[sem] % self.per[sem], (event, self.next[sem])
        self.next[sem] += 1
        return self.sems[sem], self.by[sem]


class Banks(Tally):

    def plan(self, uses, banks, tag):
        self.bank, self.before = {}, {}
        filled, emptied = {k: [] for k in banks}, {k: [] for k in banks}
        for n, u in enumerate(uses):
            k = banks[n % len(banks)]
            self.bank[u] = k
            self.before[u] = len(emptied[k])
            filled[k].append(("filled", *u))
            emptied[k].append(("emptied", *u))
        for k in banks:
            self.declare(f"{tag}_bank{k}_filled", filled[k])
            self.declare(f"{tag}_bank{k}_emptied", emptied[k], base=1)
        self.tag = tag

    def open_(self, b, *use):
        sem = f"{self.tag}_bank{self.bank[use]}_emptied"
        return self.sems[sem], b * self.per[sem] + (self.base[sem] + self.before[use])


def setup_block(nc, ctx, S, A, tally):
    with ExitStack() as tmp:
        def sb(name, shape, dt=F32):
            return tmp.enter_context(nc.sbuf_tensor(f"setup_{name}", shape, dt))

        def sem(name):
            return tmp.enter_context(nc.semaphore(name))

        QD = D // 4
        are, aim, cre, cim, ldt = (sb(n, [P, D]) for n in ("are", "aim", "cre", "cim", "ldt"))
        decay, turn, mag, den = (sb(n, [P, D]) for n in ("decay", "turn", "mag", "den"))
        alpha, beta = sb("alpha", [P, D]), sb("beta", [P, D])
        offA, offB, signA, signB = (sb(n, [P, 1]) for n in ("offA", "offB", "signA", "signB"))
        it_i, it_j = sb("it_i", [P, LI]), sb("it_j", [P, LJ])
        U, UE, US = (sb(n, [P, QD, LI]) for n in ("U", "UE", "US"))
        g = [UE[:].rearrange("p d i -> p (d i)")[:, k * D:(k + 1) * D] for k in range(6)]
        mf = US[0:1].rearrange("p d i -> p (d i)")[:, 0:2 * B * J].rearrange("p (a s) -> p a s", a=2)
        W, WA, WB, WE, WS = (sb(n, [P, QD, LJ]) for n in ("W", "WA", "WB", "WE", "WS"))
        kq = sb("kq", [P, QD, LJ])
        kd = sb("kd", [QD, 4, T])
        KT = sb("KTaps", [P, NT, D])
        dskip = sb("dskip", [1, D])
        m8w = sb("m8", [1, 2, B * J // 4], U32)
        m8 = m8w[:].bitcast(U8)
        tm8w = sb("tm8", [P, B * NT // 4], U32)
        tm8 = tm8w[:].bitcast(U8)
        pk = tmp.enter_context(nc.psum_tensor("pk", [P, 2, QD * LJ // 2], F32))
        pt = tmp.enter_context(nc.psum_tensor("pt", [P, 4, 512], F32))

        par_in, mask_in, skip_in = sem("par_in"), sem("mask_in"), sem("skip_in")
        iota_made, vec, act, pool = sem("iota_made"), sem("vec_step"), sem("act_step"), sem("pool_step")
        u_made, w_made, taps_filled, kq_made = sem("u_made"), sem("w_made"), sem("taps_filled"), sem("kq_made")
        tr_filled, tr_copied, film_in = sem("tr_filled"), sem("tr_copied"), sem("film_in")
        kt_filled, kt_copied, kf_filled, kf_copied = sem("kt_filled"), sem("kt_copied"), sem("kf_filled"), sem("kf_copied")
        w_in, ident_made = sem("w_in"), sem("ident_made")
        pi_filled, phased = sem("pi_filled"), sem("phased")

        loads = []

        block = tmp.enter_context(nc.Block())

        @block.sync
        def _(sp):
            for half in (0, NS):
                for dst, src in ((are, A["A_reT"]), (aim, A["A_imT"]), (cre, A["C_reT"]), (cim, A["C_imT"])):
                    sp.dma_start(dst[half:half + NS, :], src).then_inc(par_in, 16)
            sp.dma_start(ldt[:], A["log_dt"].partition_broadcast(P)).then_inc(par_in, 16)
            sp.dma_start(S["fd"][:], A["dft_in"].rearrange("(c p) f -> p c f", p=P)).then_inc(w_in, 16)
            sp.dma_start(dskip[:], A["D_skip"]).then_inc(skip_in, 16)
            sp.dma_start(m8w[:, 0, :], A["mask_k0"]).then_inc(mask_in, 16)
            sp.dma_start(m8w[:, 1, :], A["mask_k1"]).then_inc(mask_in, 16)
            sp.dma_start(tm8w[:], A["mask_t"]).then_inc(mask_in, 16)
            sp.dma_start(S["mgate"][:], A["mod_gate"].partition_broadcast(P)).then_inc(film_in, 16)
            sp.dma_start(S["vf"][J:J + 1, 0:2 * D], A["b_film_in"]).then_inc(film_in, 16)
            sp.dma_start(S["vf"][J:J + 1, 2 * D:4 * D], A["b_film_out"]).then_inc(film_in, 16)
            n = 0
            for dst, src in S["weight_loads"]:
                sp.dma_start(dst, src).then_inc(w_in, 16)
                n += 1
            sp.wait_ge(w_in, 16 * (n + 1))

        @block.gpsimd
        def _(g_):
            ident = S["ident"]
            g_.memset(ident[:], 0.0).then_inc(ident_made, 1)
            g_.wait_ge(ident_made, 1)
            g_.affine_select(out=ident[:], in_=ident[:], compare_op=ALU.not_equal, fill=1.0, base=0,
                             pattern=[[-1, P]], channel_multiplier=1).then_inc(ident_made, 1)
            made = [0]

            def step(ins):
                made[0] += 1
                ins.then_inc(iota_made, 1)
                g_.wait_ge(iota_made, made[0])

            g_.wait_ge(ident_made, 2)
            step(g_.iota(it_i[:], [[LJ, LI]], base=0, channel_multiplier=0, allow_small_or_imprecise_dtypes=True))
            step(g_.iota(it_j[:], [[1, LJ]], base=0, channel_multiplier=0, allow_small_or_imprecise_dtypes=True))
            for tile, first, second in ((offA, 0.25, 0.0), (offB, 0.0, 0.25), (signA, 1.0, -1.0), (signB, -1.0, -1.0)):
                step(g_.memset(tile[0:NS, :], first))
                step(g_.memset(tile[NS:P, :], second))
            step(g_.memset(S["power"][:], -0.5))
            step(g_.memset(S["ones_bf"][:], 1.0))
            step(g_.memset(S["amT"][J:J + 1, :], 1.0))
            for name in ("ktbd", "vtbd", "k1bd"):
                step(g_.memset(S[name][:], 0.0))
            step(g_.memset(S["sg"][:], -1.0))

        @block.vector
        def _(v):
            n = [0]

            def step(ins):
                n[0] += 1
                ins.then_inc(vec, 1)
                v.wait_ge(vec, n[0])

            def mul(o, a, b):
                step(nc.vector.tensor_tensor(o, a, b, ALU.mult))

            def add(o, a, b):
                step(nc.vector.tensor_tensor(o, a, b, ALU.add))

            def sub(o, a, b):
                step(nc.vector.tensor_tensor(o, a, b, ALU.subtract))

            v.wait_ge(mask_in, 48)
            step(nc.vector.tensor_copy(mf, m8))
            step(nc.vector.tensor_scalar(S["mask_rows"][:], mf, -FAR, FAR, ALU.mult, ALU.add))
            step(nc.vector.tensor_scalar(S["tmask"][:], tm8, 1.0 / H1, None, ALU.mult))
            v.wait_ge(film_in, 48)
            row = S["vf"][J:J + 1, :]
            step(nc.vector.tensor_scalar(row, row, S["mgate"][J:J + 1, :], None, ALU.mult))
            for at in (0, 2 * D):
                step(nc.vector.tensor_scalar(row[:, at:at + D], row[:, at:at + D], 1.0, None, ALU.add))

            def frac(o, x, scratch):
                step(nc.vector.tensor_scalar(scratch, x, MAGIC, -MAGIC, ALU.add, ALU.add))
                sub(o, x, scratch)

            v.wait_ge(par_in, 16 * 9)
            v.wait_ge(iota_made, 17)
            v.wait_ge(act, 1)
            mul(decay[:], ldt[:], are[:])
            mul(turn[:], ldt[:], aim[:])
            step(nc.vector.tensor_scalar(turn[:], turn[:], 0.15915494309189535, None, ALU.mult))
            frac(turn[:], turn[:], g[0])
            step(nc.vector.tensor_scalar(g[1], turn[:], 0.25, None, ALU.add))
            frac(g[2], g[1], g[0])
            nc.vector.tensor_copy(g[3], turn[:]).then_inc(phased, 1)
            v.wait_ge(act, 4)
            mul(g[2], g[2], mag[:])
            mul(g[3], g[3], mag[:])
            step(nc.vector.tensor_scalar(g[2], g[2], -1.0, None, ALU.add))
            mul(den[:], are[:], are[:])
            mul(g[0], aim[:], aim[:])
            add(den[:], den[:], g[0])
            step(nc.vector.reciprocal(den[:], den[:]))
            mul(g[0], cre[:], are[:])
            mul(g[1], cim[:], aim[:])
            add(g[0], g[0], g[1])
            mul(g[4], cim[:], are[:])
            mul(g[5], cre[:], aim[:])
            sub(g[4], g[4], g[5])
            mul(g[0], g[0], den[:])
            mul(g[4], g[4], den[:])
            mul(alpha[:], g[0], g[2])
            mul(g[1], g[4], g[3])
            sub(alpha[:], alpha[:], g[1])
            mul(beta[:], g[0], g[3])
            mul(g[1], g[4], g[2])
            add(beta[:], beta[:], g[1])
            step(nc.vector.tensor_scalar(alpha[:], alpha[:], signA[:], 2.0, ALU.mult, ALU.mult))
            step(nc.vector.tensor_scalar(beta[:], beta[:], signB[:], 2.0, ALU.mult, ALU.mult))

            for q in range(4):
                cols = slice(q * QD, (q + 1) * QD)

                def over(x, m):
                    return x[:, cols].unsqueeze(2).to_broadcast([P, QD, m])

                ti = it_i[:].unsqueeze(1).to_broadcast([P, QD, LI])
                tj = it_j[:].unsqueeze(1).to_broadcast([P, QD, LJ])
                if q:
                    v.wait_ge(taps_filled, q)
                step(nc.vector.tensor_tensor(U[:], over(turn, LI), ti, ALU.mult))
                step(nc.vector.tensor_scalar(U[:], U[:], offA[:], None, ALU.add))
                frac(U[:], U[:], US[:])
                step(nc.vector.tensor_tensor(UE[:], over(decay, LI), ti, ALU.mult))
                step(nc.vector.tensor_tensor(W[:], over(turn, LJ), tj, ALU.mult))
                step(nc.vector.tensor_scalar(WA[:], W[:], offA[:], None, ALU.add))
                frac(WA[:], WA[:], WS[:])
                step(nc.vector.tensor_scalar(WB[:], W[:], offB[:], None, ALU.add))
                frac(WB[:], WB[:], WS[:])
                nc.vector.tensor_tensor(WE[:], over(decay, LJ), tj, ALU.mult).then_inc(phased, 1)
                v.wait_ge(act, 4 + 5 * (q + 1))
                nc.vector.tensor_tensor(U[:], U[:], UE[:], ALU.mult).then_inc(u_made, 1)
                mul(WA[:], WA[:], over(alpha, LJ))
                mul(WB[:], WB[:], over(beta, LJ))
                add(WA[:], WA[:], WB[:])
                nc.vector.tensor_tensor(WA[:], WA[:], WE[:], ALU.mult).then_inc(w_made, 1)

            for r in range(4):
                v.wait_ge(tr_filled, r + 1)
                nc.vector.tensor_copy(
                    kd[:].rearrange("d q (i j) -> d j (q i)", j=LJ)[:, 4 * r:4 * r + 4, :],
                    pt[0:QD, r, :].rearrange("d (j x) -> d j x", j=4)).then_inc(tr_copied, 1)
            for c in range(NT):
                v.wait_ge(kt_filled, c + 1)
                nc.vector.tensor_copy(KT[:, c, :], pt[:, c, 0:D]).then_inc(kt_copied, 1)
            v.wait_ge(skip_in, 16)
            v.wait_ge(kt_copied, NT)
            nc.vector.tensor_tensor(KT[0:1, 0, :], KT[0:1, 0, :], dskip[:], ALU.add).then_inc(kt_copied, 1)
            for j in range(FQ):
                v.wait_ge(kf_filled, j + 1)
                nc.vector.tensor_copy(S["kf"][:, j, 0:2, :], pt[:, j, :].rearrange("p (a d) -> p a d", a=2)).then_inc(kf_copied, 1)
                nc.vector.tensor_copy(S["kf"][:, j, 2, :], pt[:, j, 0:D]).then_inc(kf_copied, 1)

        @block.scalar
        def _(a):
            a.wait_ge(par_in, 16 * 9)
            nc.scalar.activation(ldt[:], ldt[:], ACT.Exp).then_inc(act, 1)
            a.wait_ge(phased, 1)
            nc.scalar.activation(mag[:], decay[:], ACT.Exp).then_inc(act, 1)
            nc.scalar.activation(g[2], g[2], ACT.Sin, scale=TWO_PI).then_inc(act, 1)
            nc.scalar.activation(g[3], g[3], ACT.Sin, scale=TWO_PI).then_inc(act, 1)
            for q in range(4):
                a.wait_ge(phased, q + 2)
                nc.scalar.activation(U[:], U[:], ACT.Sin, scale=TWO_PI).then_inc(act, 1)
                nc.scalar.activation(WA[:], WA[:], ACT.Sin, scale=TWO_PI).then_inc(act, 1)
                nc.scalar.activation(WB[:], WB[:], ACT.Sin, scale=TWO_PI).then_inc(act, 1)
                nc.scalar.activation(UE[:], UE[:], ACT.Exp).then_inc(act, 1)
                nc.scalar.activation(WE[:], WE[:], ACT.Exp).then_inc(act, 1)
            a.wait_ge(taps_filled, 4)
            nc.scalar.copy(kq[:].rearrange("p d j -> p (d j)").rearrange("p (a x) -> p a x", a=2), pk[:]).then_inc(kq_made, 1)

        @block.tensor
        def _(pe):
            for q in range(4):
                pe.wait_ge(u_made, q + 1)
                pe.wait_ge(w_made, q + 1)
                for d in range(QD):
                    half, at = divmod(d * LJ, QD * LJ // 2)
                    last = nc.tensor.matmul(pk[q * LI:(q + 1) * LI, half, at:at + LJ], U[:, d, :], WA[:, d, :],
                                            start=True, stop=True)
                last.then_inc(taps_filled, 1)
            pe.wait_ge(kq_made, 1)
            pe.wait_ge(ident_made, 2)
            for j in range(LJ):
                last = nc.tensor.transpose(pt[0:QD, j // 4, (j % 4) * P:(j % 4 + 1) * P], kq[:, :, j], S["ident"][:])
                if j % 4 == 3:
                    last.then_inc(tr_filled, 1)
            pe.wait_ge(tr_copied, 4)
            for c in range(NT):
                for q in range(4):
                    last = nc.tensor.transpose(pt[:, c, q * QD:(q + 1) * QD], kd[:, q, c * P:(c + 1) * P], S["ident"][0:QD, 0:QD])
                last.then_inc(kt_filled, 1)
            pe.wait_ge(kt_copied, NT + 1)
            pe.wait_ge(w_in, 16)
            for j in range(FQ):
                for part in range(2):
                    for c in range(NT):
                        last = nc.tensor.matmul(pt[:, j, part * D:(part + 1) * D],
                                                S["fd"][:, c, (2 * j + part) * P:(2 * j + part + 1) * P],
                                                KT[:, c, :], start=(c == 0), stop=(c == NT - 1))
                last.then_inc(kf_filled, 1)


LN_ATTN0, LN_MOE0, LN_TEXT, LN_IN, LN_FFN, LN_OUT, LN_EXPERTS, LN_TWICE = range(8)


def layer_uses():
    uses = [("KT",), ("VT",), ("KV1",), ("M", 0), ("M", 1), ("VO", 0), ("VO", 1), ("MM1",), ("VF", 0), ("VF", 1)]
    uses += [("zt", LN_ATTN0, t) for t in range(NT)]
    for s in range(NT + 1):
        uses += [("S", s)] if s < NT else []
        uses += [("PT", s - 1), ("O", s - 1)] if s else []
    uses += [("zt", LN_MOE0, t) for t in range(NT)] + [("LG",)]
    for s in range(NT + 1):
        uses += [("H", s, 0), ("H", s, 1)] if s < NT else []
        uses += [("HT", s - 1, 0), ("HT", s - 1, 1), ("O2", s - 1)] if s else []
    uses += [("zt", LN_TEXT, t) for t in range(NT)] + [("S1", t) for t in range(NT)]
    for t in range(NT):
        uses += [("AT", t), ("FI", t)]
    uses += [("XQ", j) for j in range(FQ)]
    for t in range(NT):
        uses += [("YI", t), ("FO", t)]
    uses += [("zt", LN_FFN, t) for t in range(NT)] + [("GH", c) for c in range(HC)] + [("O3", t) for t in range(NT)]
    uses += [("zt", LN_EXPERTS, t) for t in range(NT)] + [("SC",), ("ST",)]
    return uses


def layer_signals(y):
    tiles = range(NT)
    y.declare("x_loaded", [("x_loaded",)], by=16)
    y.declare("ctx_loaded", [("ctx_loaded",)], by=16)
    y.declare("x3_stored", [("x3_stored",)], base=16, by=16)
    y.declare("table_stored", [("table_stored",)], base=16, by=16)
    y.declare("scores_stored", [("scores_stored",)], base=16, by=16)
    y.declare("mask_rows_made", [("mask_row", 0), ("mask_row", 1), ("tm",)])
    y.declare("stats_made", [("stats", i, t) for i in range(8) for t in tiles])
    y.declare("mean_var_made", [("mean_var", i, t) for i in range(8) for t in tiles])
    y.declare("var_eps_made", [("var_eps", i, t) for i in range(8) for t in tiles])
    y.declare("rstd_made", [("rstd", i, t) for i in range(8) for t in tiles])
    y.declare("normed", [("z", i, t) for i in range(8) for t in tiles])
    y.declare("residual_biased", [("xb",)])
    y.declare("max0_made", [("mx", t) for t in tiles])
    y.declare("exp0_made", [("ex", t) for t in tiles])
    y.declare("sum0_made", [e for t in tiles for e in (("sm", t), ("rs", t))])
    y.declare("probs0_made", [("pr", t) for t in tiles])
    y.declare("gate_chain", [("sg1",), ("sig",)] + [("m8", t) for t in tiles] + [("m8p",)] + [("mr", t) for t in tiles]
             + [("gt",), ("gsum",), ("gmax",), ("grec",), ("grs",), ("gate",)])
    y.declare("top_made", [(k, t, r, h) for t in tiles for r in range(ROUNDS) for k in ("tm8", "tmr") for h in range(H1)])
    y.declare("shifted1_made", [("e1s", t) for t in tiles])
    y.declare("exp1_made", [("e1", t) for t in tiles])
    y.declare("mean1_chain", [(k, t) for t in tiles for k in ("k0", "k1", "k2", "k3", "k4", "am")])
    y.declare("in_gain_made", [e for t in tiles for e in (("ng", t), ("nb", t))])
    y.declare("film_in_scaled", [("xf1", t) for t in tiles])
    y.declare("products_made", [("t1", j) for j in range(FQ)])
    y.declare("spectrum_made", [e for j in range(FQ) for e in (("yc", j), ("ys", j))])
    y.declare("film_out_scaled", [("r1", t) for t in tiles])
    y.declare("text_added", [e for t in tiles for e in (("r", t), ("rb", t))])
    y.declare("out_gain_made", [e for t in tiles for e in (("og", t), ("ob", t))])
    y.declare("x3_made", [("x3", t) for t in tiles])
    y.declare("x4_made", [("x4", t) for t in tiles])
    y.declare("t8_made", [("t8",)])


def layers_block(nc, ctx, S, A, out):
    with ExitStack() as tmp:
        def sb(name, shape, dt=F32):
            return tmp.enter_context(nc.sbuf_tensor(name, shape, dt))

        y = Banks(tmp, nc)
        y.plan(layer_uses(), list(range(PSUM_BANKS)), "layers")
        layer_signals(y)
        at, tick, open_ = y.at, y.tick, y.open_
        ps = tmp.enter_context(nc.psum_tensor("ps", [P, PSUM_BANKS, 512], F32))

        def bank(*use):
            return ps[:, y.bank[use], :]

        x_in, x, xt, z = (sb(n, [P, NT, D]) for n in ("x_in", "x", "x_text", "z"))
        zT = sb("zT", [P, DC, T])
        ctxT = sb("ctxT", [CK, 2, J])
        ktbd, vtbd, k1bd = S["ktbd"], S["vtbd"], S["k1bd"]
        v1T = sb("v1T", [P, DC, J])
        m0 = sb("m0", [P, DC, H0 * J])
        vo = sb("vo", [P, C0, D])
        m1 = sb("m1", [P, DC, H1 * J])
        vf = S["vf"]
        mrow0, mrow1 = sb("mrow0", [1, H0, J], BF16), sb("mrow1", [1, H1, J], BF16)
        tm = sb("tm", [P, NT])
        stats, mv = sb("stats", [P, NT, 6]), sb("mv", [P, NT, 2])
        ve, rstd = sb("ve", [P, NT, 1]), sb("rstd", [P, NT, 1])
        e_buf = sb("e_buf", [P, NT, 512])
        prod = e_buf[:]
        mx, sm, rs = (sb(n, [P, NT, H0]) for n in ("mx", "sm", "rs"))
        pT = sb("pT", [P, 2, 512])
        big = sb("big", [P, 4096])
        h_sb = big[:, 0:2048].rearrange("p (a f) -> p a f", a=2)
        hT = big[:, 2048:4096].rearrange("p (a c t) -> p a c t", a=2, c=HC)
        spec = big[:, 0:2048].rearrange("p (m d) -> p m d", m=2 * FQ)
        s1 = big[:, 2048:3072].rearrange("p (t h j) -> p t h j", t=NT, h=H1)
        e1 = big[:, 3072:4096].rearrange("p (t h j) -> p t h j", t=NT, h=H1)
        gT = big[:].rearrange("p (c t) -> p c t", c=HC)
        sg, zsel = S["sg"], sb("zsel", [P, NT, E0 + KTOP0])
        m8 = sb("m8", [P, NT, 8])
        gate, g4 = sb("gate", [P, NT, E0]), sb("g4", [P, NT, 1])
        work = sb("work", [P, H1, J])
        top, rest = sb("top", [P, NT, H1, 8]), sb("rest", [P, H1, 8])
        k1 = sb("k1", [P, NT, H1])
        am = sb("am", [P, NT, J])
        amT = S["amT"]
        xf, yv, x3 = (sb(n, [P, NT, D]) for n in ("xf", "yv", "x3"))
        r, rb = xf, xt
        r3 = yv
        t8 = sb("t8", [E1, T])
        tb = sb("tb", [P, NT, TABLE_W])
        ident = S["ident"]

        x_h = A["x"].rearrange("b (t p) d -> b p t d", p=P)
        out_h = out.rearrange("b (t p) d -> b p t d", p=P)
        table_h = S["table"].rearrange("(b t p) w -> b p t w", p=P, t=NT)
        scores_h = S["scores"].rearrange("e (b t) -> b e t", b=B)
        ctx_h = A["ctxT"].rearrange("b (k p) j -> b p k j", k=2)

        passed = tmp.enter_context(nc.semaphore("layers_wait_passed"))

        def apart(eng):
            eng.sem_inc(passed, 1)

        block = tmp.enter_context(nc.Block())

        @block.sync
        def _(sp):
            def load(b, before):
                if before is not None:
                    sp.wait_ge(*at(before, "z", LN_ATTN0, NT - 1))
                    apart(sp)
                    sp.wait_ge(*at(before, "xb"))
                apart(sp)
                sp.dma_start(x_in[:], x_h[b]).then_inc(*tick("x_loaded"))
                if before is not None:
                    sp.wait_ge(*at(before, "filled", "KV1"))
                apart(sp)
                sp.dma_start(ctxT[:], ctx_h[b]).then_inc(*tick("ctx_loaded"))

            def store(b):
                sp.wait_ge(*at(b, "t8"))
                apart(sp)
                sp.dma_start(scores_h[b], t8[:]).then_inc(*tick("scores_stored"))
                sp.wait_ge(*at(b, "x4", NT - 1))
                apart(sp)
                sp.dma_start(out_h[b], x3[:]).then_inc(*tick("x3_stored"))
                sp.wait_ge(*at(b, "emptied", "ST"))
                apart(sp)
                sp.wait_ge(*at(b, "z", LN_TWICE, NT - 1))
                apart(sp)
                sp.dma_start(table_h[b], tb[:]).then_inc(*tick("table_stored"))

            for s in ("x3_stored", "table_stored", "scores_stored"):
                sp.sem_inc(y.sems[s], 16)
            load(0, None)
            with sp.Fori(0, B - 1) as b:
                load(b + 1, b)
                store(b)
            store(B - 1)
            sp.wait_ge(*at(B - 1, "x3_stored"))
            sp.wait_ge(*at(B - 1, "table_stored"))
            sp.wait_ge(*at(B - 1, "scores_stored"))

        @block.gpsimd
        def _(g):
            for k in range(PSUM_BANKS):
                g.sem_inc(y.sems[f"layers_bank{k}_emptied"], 1)

            def rstd_of(b, i, t):
                g.wait_ge(*at(b, "mean_var", i, t))
                apart(g)
                nc.gpsimd.tensor_scalar(ve[:, t, :], mv[:, t, 1:2], EPS, None, ALU.add).then_inc(*tick("var_eps", i, t))
                g.wait_ge(*at(b, "var_eps", i, t))
                nc.gpsimd.tensor_tensor(rstd[:, t, :], ve[:, t, :], S["power"][:], ALU.pow).then_inc(*tick("rstd", i, t))

            with g.Fori(0, B) as b:
                for t in range(NT):
                    rstd_of(b, LN_ATTN0, t)
                nc.gpsimd.tensor_tensor(x[:], x_in[:], S["b_o"][:].unsqueeze(1).to_broadcast([P, NT, D]),
                                        ALU.add).then_inc(*tick("xb"))
                for t in range(NT + 1):
                    if t < NT:
                        g.wait_ge(*at(b, "rs", t))
                        nc.gpsimd.tensor_tensor(e_buf[:, t, :].rearrange("p (h j) -> p h j", h=H0),
                                                e_buf[:, t, :].rearrange("p (h j) -> p h j", h=H0),
                                                rs[:, t, :].unsqueeze(2).to_broadcast([P, H0, J]),
                                                ALU.mult).then_inc(*tick("pr", t))
                    if t:
                        rstd_of(b, LN_MOE0, t - 1)
                for t in range(NT):
                    rstd_of(b, LN_TEXT, t)
                for t in range(NT):
                    rstd_of(b, LN_IN, t)
                for t in range(NT):
                    g.wait_ge(*at(b, "z", LN_IN, t))
                    nc.gpsimd.tensor_tensor(z[:, t, :], z[:, t, :], S["g_in"][:], ALU.mult).then_inc(*tick("ng", t))
                    g.wait_ge(*at(b, "ng", t))
                    nc.gpsimd.tensor_tensor(z[:, t, :], z[:, t, :], S["b_in"][:], ALU.add).then_inc(*tick("nb", t))
                for t in range(NT):
                    g.wait_ge(*at(b, "tm8", t, 0, H1 - 1))
                    g.wait_ge(*at(b, "emptied", "S1", t))
                    nc.gpsimd.tensor_tensor(e1[:, t], s1[:, t], top[:, t, :, 0:1].to_broadcast([P, H1, J]),
                                            ALU.subtract).then_inc(*tick("e1s", t))
                for j in range(FQ):
                    g.wait_ge(*at(b, "t1", j))
                    nc.gpsimd.tensor_tensor(spec[:, 2 * j, :], prod[:, 2 * (j % 2), 0:D], prod[:, 2 * (j % 2), D:2 * D],
                                            ALU.subtract).then_inc(*tick("yc", j))
                    g.wait_ge(*at(b, "emptied", "XQ", j))
                    nc.gpsimd.tensor_tensor(spec[:, 2 * j + 1, :], prod[:, 2 * (j % 2) + 1, 0:D],
                                            prod[:, 2 * (j % 2) + 1, D:2 * D], ALU.add).then_inc(*tick("ys", j))
                for t in range(NT):
                    g.wait_ge(*at(b, "emptied", "FO", t))
                    nc.gpsimd.tensor_tensor(r[:, t, :], r[:, t, :], xt[:, t, :], ALU.add).then_inc(*tick("r", t))
                    g.wait_ge(*at(b, "r", t))
                    nc.gpsimd.tensor_tensor(rb[:, t, :], r[:, t, :], S["b2"][:], ALU.add).then_inc(*tick("rb", t))
                    rstd_of(b, LN_FFN, t)
                for t in range(NT):
                    rstd_of(b, LN_OUT, t)
                    g.wait_ge(*at(b, "z", LN_OUT, t))
                    nc.gpsimd.tensor_tensor(z[:, t, :], z[:, t, :], S["g_out"][:], ALU.mult).then_inc(*tick("og", t))
                    g.wait_ge(*at(b, "og", t))
                    nc.gpsimd.tensor_tensor(z[:, t, :], z[:, t, :], S["b_out"][:], ALU.add).then_inc(*tick("ob", t))
                for t in range(NT):
                    rstd_of(b, LN_EXPERTS, t)
                for t in range(NT):
                    g.wait_ge(*at(b, "z", LN_EXPERTS, t))
                    nc.gpsimd.tensor_tensor(x3[:, t, :], x3[:, t, :], z[:, t, :], ALU.add).then_inc(*tick("x4", t))
                    rstd_of(b, LN_TWICE, t)

        @block.vector
        def _(v):
            def stats_of(b, i, t, src):
                nc.vector.bn_stats(stats[:, t, :], src[:, t, :]).then_inc(*tick("stats", i, t))
                v.wait_ge(*at(b, "stats", i, t))
                apart(v)
                nc.vector.bn_aggr(mv[:, t, :], stats[:, t, :]).then_inc(*tick("mean_var", i, t))

            def norm(b, i, t, src, dst):
                v.wait_ge(*at(b, "rstd", i, t))
                nc.vector.tensor_scalar(dst, src[:, t, :], mv[:, t, 0:1], rstd[:, t, :], ALU.subtract,
                                        ALU.mult).then_inc(*tick("z", i, t))

            def heads(ap, h):
                return ap.rearrange("p (h j) -> p h j", h=h)

            with v.Fori(0, B) as b:
                nc.vector.tensor_copy(mrow0[:], S["mask_rows"][:, 0, bass.ds(b * J, J)].unsqueeze(1).to_broadcast([1, H0, J])).then_inc(*tick("mask_row", 0))
                nc.vector.tensor_copy(mrow1[:], S["mask_rows"][:, 1, bass.ds(b * J, J)].unsqueeze(1).to_broadcast([1, H1, J])).then_inc(*tick("mask_row", 1))
                nc.vector.tensor_copy(tm[:], S["tmask"][:, bass.ds(b * NT, NT)]).then_inc(*tick("tm"))
                v.wait_ge(*at(b, "x_loaded"))
                for t in range(NT + 1):
                    if t < NT:
                        stats_of(b, LN_ATTN0, t, x_in)
                    if t:
                        norm(b, LN_ATTN0, t - 1, x_in, z[:, t - 1, :])
                for t in range(NT + 2):
                    if t < NT:
                        v.wait_ge(*at(b, "filled", "S", t))
                        nc.vector.tensor_reduce(mx[:, t, :], heads(bank("S", t), H0), AX, ALU.max).then_inc(*tick("mx", t))
                        v.wait_ge(*at(b, "mx", t))
                        nc.vector.tensor_tensor(heads(e_buf[:, t, :], H0), heads(bank("S", t), H0),
                                                mx[:, t, :].unsqueeze(2).to_broadcast([P, H0, J]),
                                                ALU.subtract).then_inc(*tick("emptied", "S", t))
                    if 0 < t <= NT:
                        v.wait_ge(*at(b, "ex", t - 1))
                        nc.vector.tensor_reduce(sm[:, t - 1, :], heads(e_buf[:, t - 1, :], H0), AX, ALU.add).then_inc(*tick("sm", t - 1))
                        v.wait_ge(*at(b, "sm", t - 1))
                        nc.vector.reciprocal(rs[:, t - 1, :], sm[:, t - 1, :]).then_inc(*tick("rs", t - 1))
                    if t > 1:
                        u = t - 2
                        v.wait_ge(*at(b, "filled", "O", u))
                        v.wait_ge(*at(b, "xb"))
                        nc.vector.tensor_tensor(x[:, u, :], x[:, u, :], bank("O", u)[:, 0:D], ALU.add).then_inc(*tick("emptied", "O", u))
                        v.wait_ge(*at(b, "emptied", "O", u))
                        stats_of(b, LN_MOE0, u, x)
                        if u:
                            norm(b, LN_MOE0, u - 1, x, z[:, u - 1, :])
                norm(b, LN_MOE0, NT - 1, x, z[:, NT - 1, :])
                v.wait_ge(*at(b, "emptied", "LG"))
                nc.vector.tensor_scalar(sg[:, :, 0:E0], sg[:, :, 0:E0], 1.0, None, ALU.add).then_inc(*tick("sg1"))
                v.wait_ge(*at(b, "sg1"))
                nc.vector.reciprocal(sg[:, :, 0:E0], sg[:, :, 0:E0]).then_inc(*tick("sig"))
                v.wait_ge(*at(b, "sig"))
                apart(v)
                for t in range(NT):
                    nc.vector.max(m8[:, t, :], sg[:, t, 0:E0]).then_inc(*tick("m8", t))
                v.wait_ge(*at(b, "m8", NT - 1))
                nc.vector.memset(m8[:, :, KTOP0:8], -1.0).then_inc(*tick("m8p"))
                v.wait_ge(*at(b, "m8p"))
                apart(v)
                for t in range(NT):
                    nc.vector.match_replace(zsel[:, t, :], m8[:, t, :], sg[:, t, :], -2.0).then_inc(*tick("mr", t))
                v.wait_ge(*at(b, "mr", NT - 1))
                nc.vector.scalar_tensor_tensor(gate[:], zsel[:, :, 0:E0], -1.5, sg[:, :, 0:E0], ALU.is_lt, ALU.mult).then_inc(*tick("gt"))
                v.wait_ge(*at(b, "gt"))
                nc.vector.tensor_reduce(g4[:, :, 0], gate[:], AX, ALU.add).then_inc(*tick("gsum"))
                v.wait_ge(*at(b, "gsum"))
                nc.vector.tensor_scalar(g4[:], g4[:], 1e-9, None, ALU.max).then_inc(*tick("gmax"))
                v.wait_ge(*at(b, "gmax"))
                nc.vector.reciprocal(g4[:], g4[:]).then_inc(*tick("grec"))
                v.wait_ge(*at(b, "grec"))
                nc.vector.tensor_scalar(g4[:], g4[:], S["route"][:], None, ALU.mult).then_inc(*tick("grs"))
                v.wait_ge(*at(b, "grs"))
                nc.vector.tensor_tensor(gate[:], gate[:], g4[:].to_broadcast([P, NT, E0]), ALU.mult).then_inc(*tick("gate"))
                v.wait_ge(*at(b, "gate"))
                for t in range(NT + 1):
                    if t < NT:
                        for h in range(2):
                            v.wait_ge(*at(b, "filled", "H", t, h))
                            if t >= 2:
                                v.wait_ge(*at(b, "filled", "HT", t - 2, h))
                            nc.vector.scalar_tensor_tensor(
                                h_sb[:, t % 2, h * 512:(h + 1) * 512].rearrange("p (e f) -> p e f", f=ES),
                                bank("H", t, h).rearrange("p (e f) -> p e f", f=ES), 0.0,
                                gate[:, t, 8 * h:8 * h + 8].unsqueeze(2).to_broadcast([P, 8, ES]),
                                ALU.max, ALU.mult).then_inc(*tick("emptied", "H", t, h))
                    if t:
                        u = t - 1
                        v.wait_ge(*at(b, "filled", "O2", u))
                        nc.vector.tensor_tensor(x[:, u, :], x[:, u, :], bank("O2", u)[:, 0:D], ALU.add).then_inc(*tick("emptied", "O2", u))
                        v.wait_ge(*at(b, "emptied", "O2", u))
                        stats_of(b, LN_TEXT, u, x)
                        if u:
                            norm(b, LN_TEXT, u - 1, x, xt[:, u - 1, :])
                norm(b, LN_TEXT, NT - 1, x, xt[:, NT - 1, :])
                for t in range(NT + 1):
                    if t < NT:
                        v.wait_ge(*at(b, "z", LN_TEXT, t))
                        stats_of(b, LN_IN, t, xt)
                    if t:
                        norm(b, LN_IN, t - 1, xt, z[:, t - 1, :])
                for t in range(NT + 1):
                    if t < NT:
                        v.wait_ge(*at(b, "emptied", "S1", t))
                        apart(v)
                        for n in range(ROUNDS):
                            for h in range(H1):
                                if n:
                                    v.wait_ge(*at(b, "tmr", t, n - 1, h))
                                    apart(v)
                                nc.vector.max(rest[:, h, :] if n else top[:, t, h, :],
                                              work[:, h, :] if n else s1[:, t, h, :]).then_inc(*tick("tm8", t, n, h))
                            for h in range(H1):
                                v.wait_ge(*at(b, "tm8", t, n, h))
                                apart(v)
                                nc.vector.match_replace(work[:, h, :], rest[:, h, :] if n else top[:, t, h, :],
                                                        work[:, h, :] if n else s1[:, t, h, :],
                                                        OUT_OF_RANGE).then_inc(*tick("tmr", t, n, h))
                        v.wait_ge(*at(b, "e1", t))
                        v.wait_ge(*at(b, "tmr", t, ROUNDS - 1, H1 - 1))
                        nc.vector.scalar_tensor_tensor(e1[:, t], work[:], OUT_OF_RANGE / 2, e1[:, t], ALU.is_lt,
                                                       ALU.mult).then_inc(*tick("k0", t))
                        v.wait_ge(*at(b, "k0", t))
                        nc.vector.tensor_reduce(k1[:, t, :], e1[:, t], AX, ALU.add).then_inc(*tick("k1", t))
                        v.wait_ge(*at(b, "k1", t))
                        nc.vector.reciprocal(k1[:, t, :], k1[:, t, :]).then_inc(*tick("k2", t))
                        v.wait_ge(*at(b, "k2", t))
                        nc.vector.tensor_scalar(k1[:, t, :], k1[:, t, :], tm[:, t:t + 1], None, ALU.mult).then_inc(*tick("k3", t))
                        v.wait_ge(*at(b, "k3", t))
                        nc.vector.tensor_tensor(e1[:, t], e1[:, t], k1[:, t, :].unsqueeze(2).to_broadcast([P, H1, J]),
                                                ALU.mult).then_inc(*tick("k4", t))
                        v.wait_ge(*at(b, "k4", t))
                        nc.vector.tensor_reduce(am[:, t, :], e1[:, t].rearrange("p h j -> p j h"), AX, ALU.add).then_inc(*tick("am", t))
                    if t:
                        u = t - 1
                        v.wait_ge(*at(b, "filled", "FI", u))
                        v.wait_ge(*at(b, "nb", u))
                        nc.vector.tensor_tensor(xf[:, u, :], z[:, u, :], bank("FI", u)[:, 0:D], ALU.mult).then_inc(*tick("xf1", u))
                        v.wait_ge(*at(b, "xf1", u))
                        nc.vector.tensor_tensor(xf[:, u, :], xf[:, u, :], bank("FI", u)[:, D:2 * D], ALU.add).then_inc(*tick("emptied", "FI", u))
                for j in range(FQ):
                    v.wait_ge(*at(b, "filled", "XQ", j))
                    if j >= 2:
                        v.wait_ge(*at(b, "ys", j - 2))
                    q = bank("XQ", j).rearrange("p (a d) -> p a d", a=2)
                    nc.vector.tensor_tensor(prod[:, 2 * (j % 2), :].rearrange("p (a d) -> p a d", a=2), q,
                                            S["kf"][:, j, 0:2, :], ALU.mult).then_inc(*tick("t1", j))
                    nc.vector.tensor_tensor(prod[:, 2 * (j % 2) + 1, :].rearrange("p (a d) -> p a d", a=2), q,
                                            S["kf"][:, j, 1:3, :], ALU.mult).then_inc(*tick("emptied", "XQ", j))
                for t in range(NT + 1):
                    if t < NT:
                        v.wait_ge(*at(b, "filled", "FO", t))
                        v.wait_ge(*at(b, "emptied", "YI", t))
                        nc.vector.tensor_tensor(r[:, t, :], yv[:, t, :], bank("FO", t)[:, 0:D], ALU.mult).then_inc(*tick("r1", t))
                        v.wait_ge(*at(b, "r1", t))
                        nc.vector.tensor_tensor(r[:, t, :], r[:, t, :], bank("FO", t)[:, D:2 * D], ALU.add).then_inc(*tick("emptied", "FO", t))
                    if t:
                        u = t - 1
                        v.wait_ge(*at(b, "r", u))
                        stats_of(b, LN_FFN, u, r)
                        if u:
                            norm(b, LN_FFN, u - 1, r, z[:, u - 1, :])
                norm(b, LN_FFN, NT - 1, r, z[:, NT - 1, :])
                v.wait_ge(*y.last(b, "x3_stored"))
                v.wait_ge(*y.last(b, "table_stored"))
                for t in range(NT + 2):
                    if t < NT:
                        v.wait_ge(*at(b, "filled", "O3", t))
                        v.wait_ge(*at(b, "rb", t))
                        nc.vector.tensor_tensor(r3[:, t, :], rb[:, t, :], bank("O3", t)[:, 0:D], ALU.add).then_inc(*tick("emptied", "O3", t))
                        v.wait_ge(*at(b, "emptied", "O3", t))
                        stats_of(b, LN_OUT, t, r3)
                    if 0 < t <= NT:
                        norm(b, LN_OUT, t - 1, r3, z[:, t - 1, :])
                    if t > 1:
                        u = t - 2
                        v.wait_ge(*at(b, "ob", u))
                        nc.vector.tensor_tensor(x3[:, u, :], x[:, u, :], z[:, u, :], ALU.add).then_inc(*tick("x3", u))
                for t in range(NT + 1):
                    if t < NT:
                        v.wait_ge(*at(b, "x3", t))
                        stats_of(b, LN_EXPERTS, t, x3)
                    if t:
                        norm(b, LN_EXPERTS, t - 1, x3, z[:, t - 1, :])
                for t in range(NT + 1):
                    if t < NT:
                        v.wait_ge(*at(b, "z", LN_EXPERTS, t))
                        stats_of(b, LN_TWICE, t, z)
                    if t:
                        norm(b, LN_TWICE, t - 1, z, tb[:, t - 1, 0:D])
                v.wait_ge(*at(b, "emptied", "SC"))
                nc.vector.tensor_scalar(t8[:], t8[:], 1.0, None, ALU.add).then_inc(*tick("t8"))
                v.wait_ge(*at(b, "filled", "ST"))
                nc.vector.tensor_copy(tb[:, :, D:TABLE_W], bank("ST")[:, 0:NT * E1].rearrange("p (t e) -> p t e", t=NT)).then_inc(*tick("emptied", "ST"))

        @block.scalar
        def _(a):
            def evacuate(b, dst, src, *use):
                a.wait_ge(*at(b, "filled", *use))
                nc.scalar.copy(dst, src).then_inc(*tick("emptied", *use))

            def transposed(b, i, t):
                evacuate(b, zT[:, :, t * P:(t + 1) * P], bank("zt", i, t)[:, 0:D].rearrange("p (k n) -> p k n", k=DC), "zt", i, t)

            with a.Fori(0, B) as b:
                for use, dst in (("KT", ktbd), ("VT", vtbd)):
                    a.wait_ge(*at(b, "filled", use))
                    src = bank(use)[:, 0:C0 * J].rearrange("p (c j) -> p c j", c=C0)
                    nc.scalar.copy(dst[0:64, :, 0:J], src[0:64])
                    nc.scalar.copy(dst[64:P, :, J:2 * J], src[64:P]).then_inc(*tick("emptied", use))
                a.wait_ge(*at(b, "filled", "KV1"))
                for h in range(H1):
                    rows = slice(h * DH1, (h + 1) * DH1)
                    nc.scalar.copy(k1bd[rows, h * J:(h + 1) * J], bank("KV1")[rows, 0:J])
                nc.scalar.copy(v1T[:], bank("KV1")[:, J:3 * J].rearrange("p (k j) -> p k j", k=DC)).then_inc(*tick("emptied", "KV1"))
                for k in range(DC):
                    a.wait_ge(*at(b, "filled", "M", k))
                    nc.scalar.mul(m0[:, k, :], bank("M", k), DH0 ** -0.5).then_inc(*tick("emptied", "M", k))
                for k in range(2):
                    evacuate(b, vo[:, 2 * k:2 * k + 2, :], bank("VO", k).rearrange("p (c d) -> p c d", c=2), "VO", k)
                a.wait_ge(*at(b, "filled", "MM1"))
                nc.scalar.mul(m1[:], bank("MM1").rearrange("p (k s) -> p k s", k=DC), DH1 ** -0.5).then_inc(*tick("emptied", "MM1"))
                for k in range(2):
                    a.wait_ge(*at(b, "filled", "VF", k))
                    nc.scalar.mul(vf[0:J, k * 512:(k + 1) * 512], bank("VF", k)[0:J, :], S["mgate"][0:J, :]).then_inc(*tick("emptied", "VF", k))
                for t in range(NT):
                    transposed(b, LN_ATTN0, t)
                for t in range(NT + 1):
                    if t < NT:
                        a.wait_ge(*at(b, "emptied", "S", t))
                        nc.scalar.activation(e_buf[:, t, :], e_buf[:, t, :], ACT.Exp).then_inc(*tick("ex", t))
                    if t:
                        evacuate(b, pT[:, (t - 1) % 2, :], bank("PT", t - 1), "PT", t - 1)
                for t in range(NT):
                    transposed(b, LN_MOE0, t)
                a.wait_ge(*at(b, "filled", "LG"))
                nc.scalar.activation(sg[:, :, 0:E0], bank("LG")[:, 0:NT * E0].rearrange("p (t e) -> p t e", t=NT),
                                     ACT.Exp, scale=-1.0).then_inc(*tick("emptied", "LG"))
                for t in range(NT):
                    for h in range(2):
                        evacuate(b, hT[:, t % 2, 4 * h:4 * h + 4, :], bank("HT", t, h).rearrange("p (c n) -> p c n", c=4), "HT", t, h)
                for t in range(NT):
                    transposed(b, LN_TEXT, t)
                for t in range(NT):
                    evacuate(b, s1[:, t], bank("S1", t)[:, 0:H1 * J].rearrange("p (h j) -> p h j", h=H1), "S1", t)
                for t in range(NT + 1):
                    if t < NT:
                        a.wait_ge(*at(b, "e1s", t))
                        nc.scalar.activation(e1[:, t], e1[:, t], ACT.Exp).then_inc(*tick("e1", t))
                    if t:
                        evacuate(b, amT[0:J, (t - 1) * P:t * P], bank("AT", t - 1)[0:J, 0:P], "AT", t - 1)
                for t in range(NT):
                    evacuate(b, yv[:, t, :], bank("YI", t)[:, 0:D], "YI", t)
                for t in range(NT):
                    a.wait_ge(*at(b, "filled", "zt", LN_FFN, t))
                    for k in range(DC):
                        last = nc.scalar.activation(zT[:, k, t * P:(t + 1) * P], bank("zt", LN_FFN, t)[:, k * P:(k + 1) * P],
                                                    ACT.Identity, bias=S["b_ffn"][:, k:k + 1], scale=S["g_ffn"][:, k:k + 1])
                    last.then_inc(*tick("emptied", "zt", LN_FFN, t))
                for c in range(HC):
                    a.wait_ge(*at(b, "filled", "GH", c))
                    nc.scalar.activation(gT[:, c, :], bank("GH", c), ACT.Gelu, bias=S["b1"][:, c:c + 1]).then_inc(*tick("emptied", "GH", c))
                for t in range(NT):
                    transposed(b, LN_EXPERTS, t)
                a.wait_ge(*at(b, "filled", "SC"))
                a.wait_ge(*y.last(b, "scores_stored"))
                nc.scalar.activation(t8[:], bank("SC")[0:E1, :], ACT.Tanh).then_inc(*tick("emptied", "SC"))

        @block.tensor
        def _(pe):
            def product(b, *use, parts):
                pe.wait_ge(*open_(b, *use))
                for o, l, r_, start, stop in parts:
                    last = nc.tensor.matmul(o, l, r_, start=start, stop=stop)
                last.then_inc(*tick("filled", *use))

            def transposes(b, *use, parts):
                pe.wait_ge(*open_(b, *use))
                for o, i in parts:
                    last = nc.tensor.transpose(o, i, ident[:])
                last.then_inc(*tick("filled", *use))

            def contract(o, pairs):
                n = len(pairs)
                return [(o, l, r_, k == 0, k == n - 1) for k, (l, r_) in enumerate(pairs)]

            def transpose_norm(b, i, t, src):
                transposes(b, "zt", i, t, parts=[(bank("zt", i, t)[:, k * P:(k + 1) * P], src[:, t, k * P:(k + 1) * P]) for k in range(DC)])

            with pe.Fori(0, B) as b:
                pe.wait_ge(*at(b, "ctx_loaded"))
                for use, w in (("KT", S["wk"]), ("VT", S["wv"])):
                    o = bank(use)
                    product(b, use, parts=[p for c in range(C0) for p in contract(
                        o[:, c * J:(c + 1) * J], [(w[:, k, c * P:(c + 1) * P], ctxT[:, k, :]) for k in range(2)])])
                o = bank("KV1")
                product(b, "KV1", parts=contract(o[:, 0:J], [(S["wk1"][:, k, :], ctxT[:, k, :]) for k in range(2)])
                        + [p for c in range(DC) for p in contract(
                            o[:, (c + 1) * J:(c + 2) * J], [(S["wv1"][:, k, c * P:(c + 1) * P], ctxT[:, k, :]) for k in range(2)])])
                pe.wait_ge(*at(b, "emptied", "KT"))
                for k in range(DC):
                    product(b, "M", k, parts=[p for c in range(C0) for p in contract(
                        bank("M", k)[:, c * P:(c + 1) * P], [(S["wqT"][:, c, k * P:(k + 1) * P], ktbd[:, c, :])])])
                pe.wait_ge(*at(b, "emptied", "VT"))
                for k in range(2):
                    product(b, "VO", k, parts=[p for c in range(2) for p in contract(
                        bank("VO", k)[:, c * D:(c + 1) * D], [(vtbd[:, 2 * k + c, :], S["wo"][:, 2 * k + c, :])])])
                pe.wait_ge(*at(b, "emptied", "KV1"))
                product(b, "MM1", parts=[p for k in range(DC) for p in contract(
                    bank("MM1")[:, k * D:(k + 1) * D], [(S["wq1T"][:, k * P:(k + 1) * P], k1bd[:])])])
                for k in range(2):
                    product(b, "VF", k, parts=contract(bank("VF", k)[0:J, :], [
                        (v1T[:, c, :], S["wfilm"][:, c, k * 512:(k + 1) * 512]) for c in range(DC)]))
                for t in range(NT):
                    pe.wait_ge(*at(b, "z", LN_ATTN0, t))
                    transpose_norm(b, LN_ATTN0, t, z)
                pe.wait_ge(*at(b, "emptied", "M", 1))
                pe.wait_ge(*at(b, "mask_row", 0))
                for s in range(NT + 1):
                    if s < NT:
                        pe.wait_ge(*at(b, "emptied", "zt", LN_ATTN0, s))
                        product(b, "S", s, parts=contract(bank("S", s), [
                            (S["ones_bf"][:], mrow0[:].rearrange("o h j -> o (h j)"))] + [
                            (zT[:, k, s * P:(s + 1) * P], m0[:, k, :]) for k in range(DC)]))
                    if s:
                        t = s - 1
                        pe.wait_ge(*at(b, "pr", t))
                        transposes(b, "PT", t, parts=[(bank("PT", t)[:, c * P:(c + 1) * P], e_buf[:, t, c * P:(c + 1) * P]) for c in range(C0)])
                        pe.wait_ge(*at(b, "emptied", "VO", 1))
                        pe.wait_ge(*at(b, "emptied", "PT", t))
                        product(b, "O", t, parts=contract(bank("O", t)[:, 0:D], [
                            (pT[:, t % 2, c * P:(c + 1) * P], vo[:, c, :]) for c in range(C0)]))
                for t in range(NT):
                    pe.wait_ge(*at(b, "z", LN_MOE0, t))
                    transpose_norm(b, LN_MOE0, t, z)
                pe.wait_ge(*at(b, "emptied", "zt", LN_MOE0, NT - 1))
                product(b, "LG", parts=[p for t in range(NT) for p in contract(bank("LG")[:, t * E0:(t + 1) * E0], [
                    (zT[:, k, t * P:(t + 1) * P], S["sel"][:, k, :]) for k in range(DC)])])
                for s in range(NT + 1):
                    if s < NT:
                        for h in range(2):
                            product(b, "H", s, h, parts=contract(bank("H", s, h), [
                                (zT[:, k, s * P:(s + 1) * P], S["keys"][:, k, h * 512:(h + 1) * 512]) for k in range(DC)]))
                    if s:
                        t = s - 1
                        for h in range(2):
                            pe.wait_ge(*at(b, "emptied", "H", t, h))
                            transposes(b, "HT", t, h, parts=[
                                (bank("HT", t, h)[:, c * P:(c + 1) * P], h_sb[:, t % 2, (4 * h + c) * P:(4 * h + c + 1) * P]) for c in range(4)])
                        pe.wait_ge(*at(b, "emptied", "HT", t, 1))
                        product(b, "O2", t, parts=contract(bank("O2", t)[:, 0:D], [
                            (hT[:, t % 2, c, :], S["values"][:, c, :]) for c in range(HC)]))
                for t in range(NT):
                    pe.wait_ge(*at(b, "z", LN_TEXT, t))
                    transpose_norm(b, LN_TEXT, t, xt)
                for t in range(NT):
                    pe.wait_ge(*at(b, "emptied", "zt", LN_TEXT, t))
                    if t == 0:
                        pe.wait_ge(*at(b, "emptied", "MM1"))
                        pe.wait_ge(*at(b, "mask_row", 1))
                    product(b, "S1", t, parts=contract(bank("S1", t)[:, 0:H1 * J], [
                        (S["ones_bf"][:], mrow1[:].rearrange("o h j -> o (h j)"))] + [
                        (zT[:, k, t * P:(t + 1) * P], m1[:, k, :]) for k in range(DC)]))
                for t in range(NT):
                    pe.wait_ge(*at(b, "am", t))
                    pe.wait_ge(*open_(b, "AT", t))
                    apart(pe)
                    nc.tensor.transpose(bank("AT", t)[0:J, 0:P], am[:, t, :], ident[:]).then_inc(*tick("filled", "AT", t))
                    pe.wait_ge(*at(b, "emptied", "AT", t))
                    if t == 0:
                        pe.wait_ge(*at(b, "emptied", "VF", 1))
                    product(b, "FI", t, parts=contract(bank("FI", t), [(amT[:, t * P:(t + 1) * P], vf[:, 0:2 * D])]))
                pe.wait_ge(*at(b, "emptied", "FI", NT - 1))
                for j in range(FQ):
                    product(b, "XQ", j, parts=[p for part in range(2) for p in contract(
                        bank("XQ", j)[:, part * D:(part + 1) * D],
                        [(S["fd"][:, t, (2 * j + part) * P:(2 * j + part + 1) * P], xf[:, t, :]) for t in range(NT)])])
                pe.wait_ge(*at(b, "ys", FQ - 1))
                for t in range(NT):
                    product(b, "YI", t, parts=contract(bank("YI", t)[:, 0:D], [
                        (S["gi"][:, m, t * P:(t + 1) * P], spec[:, m, :]) for m in range(2 * FQ)]))
                    product(b, "FO", t, parts=contract(bank("FO", t), [(amT[:, t * P:(t + 1) * P], vf[:, 2 * D:4 * D])]))
                for t in range(NT):
                    pe.wait_ge(*at(b, "z", LN_FFN, t))
                    transpose_norm(b, LN_FFN, t, z)
                pe.wait_ge(*at(b, "emptied", "zt", LN_FFN, NT - 1))
                for c in range(HC):
                    product(b, "GH", c, parts=contract(bank("GH", c), [
                        (S["w1"][:, k, c * P:(c + 1) * P], zT[:, k, :]) for k in range(DC)]))
                for t in range(NT):
                    pe.wait_ge(*at(b, "emptied", "GH", HC - 1))
                    product(b, "O3", t, parts=contract(bank("O3", t)[:, 0:D], [
                        (gT[:, c, t * P:(t + 1) * P], S["w2"][:, c, :]) for c in range(HC)]))
                for t in range(NT):
                    pe.wait_ge(*at(b, "z", LN_EXPERTS, t))
                    transpose_norm(b, LN_EXPERTS, t, z)
                pe.wait_ge(*at(b, "emptied", "zt", LN_EXPERTS, NT - 1))
                product(b, "SC", parts=contract(bank("SC")[0:E1, :], [(S["gate_w"][:, k, :], zT[:, k, :]) for k in range(DC)]))
                pe.wait_ge(*at(b, "t8"))
                pe.wait_ge(*open_(b, "ST"))
                apart(pe)
                for t in range(NT):
                    last = nc.tensor.transpose(bank("ST")[:, t * E1:(t + 1) * E1], t8[:, t * P:(t + 1) * P], ident[0:E1, 0:E1])
                last.then_inc(*tick("filled", "ST"))


STEPS = 26
HI, LO = 32, 16
BLK = P // E1
BW = N // BLK


def experts_signals(y):
    pair, chunks = range(2), range(CC)
    y.declare("indices_picked", [("idx", s) for s in pair])
    y.declare("rows0_gathered", [("rows", 0)], by=16 * CC)
    y.declare("rows1_gathered", [("rows", 1)], by=16 * CC)
    y.declare("rows_scattered", [("added", s) for s in pair], by=16 * CC)
    y.declare("expert0_loaded", [("loaded", 0)], by=64)
    y.declare("expert1_loaded", [("loaded", 1)], by=64)
    y.declare("weights_picked", [e for s in pair for e in (("wcol", s), ("whalf", s))])
    y.declare("outputs_weighted", [("ow", s, c) for s in pair for c in chunks])


def experts_block(nc, ctx, S, A, out):
    with ExitStack() as tmp:
        def sb(name, shape, dt=F32):
            return tmp.enter_context(nc.sbuf_tensor(f"experts_{name}", shape, dt))

        def sem(name):
            return tmp.enter_context(nc.semaphore(f"choose_{name}"))

        y = Banks(tmp, nc)
        uses = []
        for s in range(2):
            uses += [("zt", s, c) for c in range(CC)] + [("G", s, m) for m in range(HC)] + [("O", s, c) for c in range(CC)]
        y.plan(uses, list(range(PSUM_BANKS)), "experts")
        experts_signals(y)
        at, tick, open_ = y.at, y.tick, y.open_
        ps = tmp.enter_context(nc.psum_tensor("experts_ps", [P, PSUM_BANKS, 512], F32))

        def bank(*use):
            return ps[:, y.bank[use], :]

        ident = S["ident"]
        same, lower = sb("same", [P, P]), sb("lower", [P, P])
        sc, gt, eq, run, sel, ones = (sb(n, [P, BW]) for n in ("sc", "gt", "eq", "run", "sel", "ones"))
        lo, cand, cnt, step_, up = (sb(n, [P, 1]) for n in ("lo", "cand", "cnt", "step", "up"))
        cols = sb("cols", [P, 8])
        slot = sb("slot", [P, 2, P])
        hi, lw = sb("hi", [P, 2 * P]), sb("lw", [P, 2 * P])
        hi_b, lw_b = sb("hi_b", [P, 2 * P], BF16), sb("lw_b", [P, 2 * P], BF16)
        iota_h, iota_l = sb("iota_h", [P, HI], BF16), sb("iota_l", [P, LO], BF16)
        pay_p, pay_g = sb("pay_p", [P, 1]), sb("pay_g", [P, 2, E1, BLK], BF16)
        one_hi = sb("one_hi", [P, 2 * P, HI], BF16)
        one_lo = sb("one_lo", [P, 2 * P, 2, LO], BF16)
        ids_f, ids = sb("ids_f", [HI, E1, LO]), sb("ids", [HI, E1, LO], I32)
        idx_all = sb("idx_all", [P, E1, CC], I32)
        idx = [sb(f"idx{s}", [P, CC], I32) for s in range(2)]
        rows = [sb(f"rows{s}", [P, CC, TABLE_W]) for s in range(2)]
        o = [sb(f"o{s}", [P, CC, D]) for s in range(2)]
        fc1, fc2 = [sb(f"fc1_{s}", [P, DC, HID]) for s in range(2)], [sb(f"fc2_{s}", [P, HC, D]) for s in range(2)]
        b1, b2 = [sb(f"b1_{s}", [P, HC]) for s in range(2)], [sb(f"b2_{s}", [P, D]) for s in range(2)]
        gamma, beta = sb("gamma", [P, DC]), sb("beta", [P, DC])
        yT = [sb(f"yT{s}", [P, DC, CAP]) for s in range(2)]
        hT = [sb(f"hT{s}", [P, HC, CAP]) for s in range(2)]
        wt = sb("wt", [P, 2, CC])

        c_in, aff_in, iota_made, vec = sem("in"), sem("affine_in"), sem("iota_made"), sem("vec_step")
        counted, summed, slot_made, slot_filled = sem("counted"), sem("summed"), sem("slot_made"), sem("slot_filled")
        onehot_made, list_filled, ids_made, ids_out, ids_in = (sem(n) for n in ("onehot_made", "list_filled", "ids_made", "ids_out", "ids_in"))

        list_h = S["list"]
        out_rows = out.rearrange("b t d -> (b t) d")

        passed = sem("wait_passed")

        def apart(eng):
            eng.sem_inc(passed, 1)

        block = tmp.enter_context(nc.Block())

        def load_expert(sp, e, s):
            sem_, _ = tick("loaded", s)
            apart(sp)
            sp.dma_start(fc1[s][:], A["fc1T"].rearrange("e (k p) f -> e p k f", p=P)[e]).then_inc(sem_, 16)
            sp.dma_start(fc2[s][:], A["fc2T"].rearrange("e (c p) d -> e p c d", p=P)[e]).then_inc(sem_, 16)
            sp.dma_start(b1[s][:], A["e_b1"].rearrange("p e c -> e p c")[e]).then_inc(sem_, 16)
            sp.dma_start(b2[s][:], A["e_b2"][e].partition_broadcast(P)).then_inc(sem_, 16)

        @block.sync
        def _(sp):
            sp.dma_start(sc[:], S["scores"].rearrange("e (k j) -> (e k) j", j=BW)).then_inc(c_in, 16)
            sp.dma_start(same[:], A["same_expert"]).then_inc(c_in, 16)
            sp.dma_start(lower[:], A["lower_block"]).then_inc(c_in, 16)
            sp.dma_start(gamma[:], A["e_gamma"]).then_inc(aff_in, 16)
            sp.dma_start(beta[:], A["e_beta"]).then_inc(aff_in, 16)
            for s in range(2):
                load_expert(sp, s, s)
            sp.wait_ge(ids_made, 1)
            sp.dma_start(list_h.rearrange("e (h l) -> h e l", l=LO), ids[:]).then_inc(ids_out, 16)
            sp.wait_ge(ids_out, 16)
            sp.dma_start(idx_all[:], list_h.rearrange("e (p c) -> p e c", c=CC)).then_inc(ids_in, 16)
            with sp.Fori(0, E1 // 2 - 1) as b:
                for s in range(2):
                    sp.wait_ge(*at(b, "filled", "O", s, CC - 1))
                    apart(sp)
                    sp.wait_ge(*at(b, "ow", s, CC - 1))
                    load_expert(sp, b * 2 + (2 + s), s)

        @block.gpsimd
        def _(g):
            for k in range(PSUM_BANKS):
                g.sem_inc(y.sems[f"experts_bank{k}_emptied"], 1)
            g.iota(iota_h[:], [[1, HI]], base=0, channel_multiplier=0, allow_small_or_imprecise_dtypes=True).then_inc(iota_made, 1)
            g.iota(iota_l[:], [[1, LO]], base=0, channel_multiplier=0, allow_small_or_imprecise_dtypes=True).then_inc(iota_made, 1)
            g.iota(pay_p[:], [[0, 1]], base=0, channel_multiplier=1, allow_small_or_imprecise_dtypes=True).then_inc(iota_made, 1)
            g.iota(pay_g[:], [[P, 2], [0, E1], [BW, BLK]], base=0, channel_multiplier=0, allow_small_or_imprecise_dtypes=True).then_inc(iota_made, 1)
            g.memset(ones[:], 1.0).then_inc(iota_made, 1)
            g.memset(lo[:], -1.0).then_inc(iota_made, 1)
            g.memset(step_[:], 2.0).then_inc(iota_made, 1)

            def gather(e, b, s, before):
                if before:
                    g.wait_ge(*at(b - 1, "ow", s, CC - 1))
                    g.wait_ge(*at(b - 1, "added", s))
                    apart(g)
                nc.gpsimd.tensor_copy(idx[s][:], idx_all[:].rearrange("p e c -> p (e c)")[:, e * CC:(e + 1) * CC] if isinstance(e, int)
                                      else idx_all[:].rearrange("p e c -> p (e c)")[:, bass.ds(e * CC, CC)]).then_inc(*tick("idx", s))
                g.wait_ge(*at(b, "idx", s))
                sem_, _ = tick("rows", s)
                apart(g)
                for c in range(CC):
                    g.indirect_dma_start(rows[s][:, c, :], None, S["table"],
                                         bass.IndirectOffsetOnAxis(ap=idx[s][:, c:c + 1], axis=0)).then_inc(sem_, 16)

            def scatter(b, s, first=False):
                g.wait_ge(*at(b, "ow", s, CC - 1))
                sem_, total = at(b, "added", s)
                if not first:
                    g.wait_ge(sem_, total - 16 * CC)
                tick("added", s)
                apart(g)
                for c in range(CC):
                    g.indirect_dma_start(out_rows, bass.IndirectOffsetOnAxis(ap=idx[s][:, c:c + 1], axis=0),
                                         o[s][:, c, :], None, compute_op=ALU.add).then_inc(sem_, 16)

            g.wait_ge(ids_in, 16)
            gather(0, 0, 0, False)
            gather(1, 0, 1, False)
            scatter(0, 0, first=True)
            with g.Fori(1, E1 // 2) as b:
                gather(b * 2, b, 0, True)
                scatter(b - 1, 1)
                gather(b * 2 + 1, b, 1, True)
                scatter(b, 0)
            scatter(E1 // 2 - 1, 1)
            g.wait_ge(*at(E1 // 2 - 1, "added", 1))

        @block.vector
        def _(v):
            n = [0]

            def step(ins):
                n[0] += 1
                ins.then_inc(vec, 1)
                v.wait_ge(vec, n[0])

            v.wait_ge(iota_made, 7)
            v.wait_ge(c_in, 48)
            with v.Fori(0, STEPS) as k:
                nc.vector.tensor_tensor(cand[:], lo[:], step_[:], ALU.add).then_inc(vec, 1)
                v.wait_ge(vec, k * 4 + 1)
                nc.vector.tensor_scalar(gt[:], sc[:], cand[:], 0.0, ALU.is_ge, ALU.add, accum_out=cnt[:]).then_inc(counted, 1)
                v.wait_ge(summed, k + 1)
                nc.vector.tensor_scalar(up[:], ps[:, 0, 0:1], CAP - 0.5, step_[:], ALU.is_ge, ALU.mult).then_inc(vec, 1)
                v.wait_ge(vec, k * 4 + 2)
                nc.vector.tensor_tensor(lo[:], lo[:], up[:], ALU.add).then_inc(vec, 1)
                nc.vector.tensor_scalar(step_[:], step_[:], 0.5, None, ALU.mult).then_inc(vec, 1)
                v.wait_ge(vec, k * 4 + 4)
            n[0] = 4 * STEPS
            step(nc.vector.tensor_scalar(gt[:], sc[:], lo[:], 0.0, ALU.is_gt, ALU.add, accum_out=cols[:, 0:1]))
            step(nc.vector.tensor_scalar(eq[:], sc[:], lo[:], 0.0, ALU.is_equal, ALU.add, accum_out=cols[:, 1:2]))
            nc.vector.tensor_tensor_scan(run[:], ones[:], eq[:], 0.0, ALU.mult, ALU.add).then_inc(counted, 1)
            v.wait_ge(summed, STEPS + 1)
            step(nc.vector.tensor_scalar(cols[:, 2:3], ps[:, 0, 0:1], -1.0, float(CAP), ALU.mult, ALU.add))
            step(nc.vector.tensor_tensor(cols[:, 2:3], cols[:, 2:3], ps[:, 0, 1:2], ALU.subtract))
            v.wait_ge(counted, STEPS + 1)
            step(nc.vector.scalar_tensor_tensor(run[:], run[:], cols[:, 2:3], eq[:], ALU.is_le, ALU.mult))
            step(nc.vector.scalar_tensor_tensor(sel[:], gt[:], 1.0, run[:], ALU.mult, ALU.add, accum_out=cols[:, 3:4]))
            nc.vector.tensor_tensor_scan(run[:], ones[:], sel[:], 0.0, ALU.mult, ALU.add).then_inc(counted, 1)
            v.wait_ge(summed, STEPS + 2)
            v.wait_ge(counted, STEPS + 2)
            step(nc.vector.tensor_copy(cols[:, 4:5], ps[:, 0, 0:1]))
            step(nc.vector.scalar_tensor_tensor(run[:], run[:], cols[:, 4:5], sel[:], ALU.add, ALU.mult))
            nc.vector.tensor_scalar(run[:], run[:], -1.0, None, ALU.add).then_inc(slot_made, 1)
            v.wait_ge(slot_filled, 1)
            step(nc.vector.tensor_copy(slot[:], ps[:, 1, 0:2 * P].rearrange("p (a x) -> p a x", a=2)))
            flat = slot[:].rearrange("p a x -> p (a x)")
            step(nc.vector.tensor_scalar(hi[:], flat, 1.0 / LO, -(LO - 1) / (2.0 * LO), ALU.mult, ALU.add))
            step(nc.vector.tensor_scalar(hi[:], hi[:], MAGIC, -MAGIC, ALU.add, ALU.add))
            step(nc.vector.scalar_tensor_tensor(lw[:], hi[:], -float(LO), flat, ALU.mult, ALU.add))
            step(nc.vector.tensor_copy(hi_b[:], hi[:]))
            step(nc.vector.tensor_copy(lw_b[:], lw[:]))
            nc.vector.tensor_tensor(one_hi[:], hi_b[:].unsqueeze(2).to_broadcast([P, 2 * P, HI]),
                                    iota_h[:].unsqueeze(1).to_broadcast([P, 2 * P, HI]), ALU.is_equal).then_inc(onehot_made, 1)
            step(nc.vector.tensor_tensor(one_lo[:, :, 1, :], lw_b[:].unsqueeze(2).to_broadcast([P, 2 * P, LO]),
                                         iota_l[:].unsqueeze(1).to_broadcast([P, 2 * P, LO]), ALU.is_equal))
            step(nc.vector.tensor_scalar(one_lo[:, :, 0, :], one_lo[:, :, 1, :], pay_p[:], None, ALU.mult))
            nc.vector.tensor_tensor(one_lo[:, :, 1, :], one_lo[:, :, 1, :],
                                    pay_g[:].rearrange("p a e k -> p (a e k)").unsqueeze(2).to_broadcast([P, 2 * P, LO]),
                                    ALU.mult).then_inc(onehot_made, 1)
            v.wait_ge(list_filled, 1)
            pair = ps[0:HI, 2, 0:E1 * 2 * LO].rearrange("h (e a l) -> h e a l", e=E1, a=2)
            step(nc.vector.tensor_copy(ids_f[:], pair[:, :, 0, :]))
            step(nc.vector.tensor_tensor(ids_f[:], ids_f[:], pair[:, :, 1, :], ALU.add))
            nc.vector.tensor_copy(ids[:], ids_f[:]).then_inc(ids_made, 1)

            with v.Fori(0, E1 // 2) as b:
                for s in range(2):
                    v.wait_ge(*at(b, "rows", s))
                    nc.vector.tensor_copy(wt[:, s, :], rows[s][:, :, bass.ds(b * 2 + (D + s), 1)].rearrange("p c o -> p (c o)")).then_inc(*tick("wcol", s))
                    v.wait_ge(*at(b, "wcol", s))
                    nc.vector.tensor_scalar(wt[:, s, :], wt[:, s, :], 0.5, None, ALU.mult).then_inc(*tick("whalf", s))
                    v.wait_ge(*at(b, "whalf", s))
                    v.wait_ge(aff_in, 32)
                    v.wait_ge(*at(b, "loaded", s))
                    for c in range(CC + 1):
                        if c < CC:
                            v.wait_ge(*at(b, "filled", "O", s, c))
                            nc.vector.tensor_tensor(o[s][:, c, :], bank("O", s, c)[:, 0:D], b2[s][:], ALU.add).then_inc(*tick("emptied", "O", s, c))
                        if c:
                            v.wait_ge(*at(b, "emptied", "O", s, c - 1))
                            nc.vector.tensor_scalar(o[s][:, c - 1, :], o[s][:, c - 1, :], wt[:, s, c - 1:c], None, ALU.mult).then_inc(*tick("ow", s, c - 1))

        @block.scalar
        def _(a):
            a.wait_ge(aff_in, 32)
            with a.Fori(0, E1 // 2) as b:
                for s in range(2):
                    for c in range(CC):
                        a.wait_ge(*at(b, "filled", "zt", s, c))
                        for k in range(DC):
                            last = nc.scalar.activation(yT[s][:, k, c * P:(c + 1) * P], bank("zt", s, c)[:, k * P:(k + 1) * P],
                                                        ACT.Identity, bias=beta[:, k:k + 1], scale=gamma[:, k:k + 1])
                        last.then_inc(*tick("emptied", "zt", s, c))
                    a.wait_ge(*at(b, "loaded", s))
                    for m in range(HC):
                        a.wait_ge(*at(b, "filled", "G", s, m))
                        nc.scalar.activation(hT[s][:, m, :], bank("G", s, m), ACT.Gelu_apprx_tanh, bias=b1[s][:, m:m + 1]).then_inc(*tick("emptied", "G", s, m))

        @block.tensor
        def _(pe):
            pe.wait_ge(c_in, 48)
            with pe.Fori(0, STEPS) as k:
                pe.wait_ge(counted, k + 1)
                nc.tensor.matmul(ps[:, 0, 0:1], same[:], cnt[:], start=True, stop=True).then_inc(summed, 1)
            pe.wait_ge(counted, STEPS + 1)
            nc.tensor.matmul(ps[:, 0, 0:1], same[:], cols[:, 0:1], start=True, stop=True)
            nc.tensor.matmul(ps[:, 0, 1:2], lower[:], cols[:, 1:2], start=True, stop=True).then_inc(summed, 1)
            pe.wait_ge(counted, STEPS + 2)
            nc.tensor.matmul(ps[:, 0, 0:1], lower[:], cols[:, 3:4], start=True, stop=True).then_inc(summed, 1)
            pe.wait_ge(slot_made, 1)
            for a_ in range(2):
                last = nc.tensor.transpose(ps[:, 1, a_ * P:(a_ + 1) * P], run[:, a_ * P:(a_ + 1) * P], ident[:])
            last.then_inc(slot_filled, 1)
            pe.wait_ge(onehot_made, 2)
            for e in range(E1):
                for k in range(2 * BLK):
                    group = (k % 2) * P + e * BLK + k // 2
                    last = nc.tensor.matmul(ps[0:HI, 2, e * 2 * LO:(e + 1) * 2 * LO], one_hi[:, group, :],
                                            one_lo[:, group].rearrange("p a l -> p (a l)"), start=(k == 0), stop=(k == 2 * BLK - 1))
            last.then_inc(list_filled, 1)
            pe.wait_ge(ids_made, 1)

            with pe.Fori(0, E1 // 2) as b:
                for s in range(2):
                    pe.wait_ge(*at(b, "rows", s))
                    for c in range(CC):
                        pe.wait_ge(*open_(b, "zt", s, c))
                        for k in range(DC):
                            last = nc.tensor.transpose(bank("zt", s, c)[:, k * P:(k + 1) * P], rows[s][:, c, k * P:(k + 1) * P], ident[:])
                        last.then_inc(*tick("filled", "zt", s, c))
                    pe.wait_ge(*at(b, "loaded", s))
                    pe.wait_ge(*at(b, "emptied", "zt", s, CC - 1))
                    for m in range(HC):
                        pe.wait_ge(*open_(b, "G", s, m))
                        for k in range(DC):
                            last = nc.tensor.matmul(bank("G", s, m), fc1[s][:, k, m * P:(m + 1) * P], yT[s][:, k, :], start=(k == 0), stop=(k == DC - 1))
                        last.then_inc(*tick("filled", "G", s, m))
                    pe.wait_ge(*at(b, "emptied", "G", s, HC - 1))
                    for c in range(CC):
                        pe.wait_ge(*open_(b, "O", s, c))
                        for m in range(HC):
                            last = nc.tensor.matmul(bank("O", s, c)[:, 0:D], hT[s][:, m, c * P:(c + 1) * P], fc2[s][:, m, :], start=(m == 0), stop=(m == HC - 1))
                        last.then_inc(*tick("filled", "O", s, c))


def build(nc, A, out):
    with ExitStack() as ctx:
        def sb(name, shape, dt=F32):
            return ctx.enter_context(nc.sbuf_tensor(name, shape, dt))

        table = nc.dram_tensor("expert_table", [N, TABLE_W], F32, kind="Internal").ap()
        scores = nc.dram_tensor("expert_scores", [E1, N], F32, kind="Internal").ap()
        lists = nc.dram_tensor("expert_lists", [E1, CAP], I32, kind="Internal").ap()
        S = {"table": table, "scores": scores, "list": lists}
        S["ident"] = sb("ident", [P, P])
        with ExitStack() as weights:
            def wb(name, shape, dt=F32):
                S[name] = weights.enter_context(nc.sbuf_tensor(name, shape, dt))
                return S[name]

            chunked = {
                "wqT": ("L0_WqT", C0, P), "wk": ("L0_Wk", 2, CK), "wv": ("L0_Wv", 2, CK), "wo": ("L0_Wo", C0, P),
                "wk1": ("L1_Wk", 2, CK), "wv1": ("L1_Wv", 2, CK), "sel": ("sel", DC, P), "keys": ("keys", DC, P),
                "values": ("values", HC, P), "w1": ("W1", DC, P), "w2": ("W2", HC, P), "gate_w": ("gate_w", DC, P),
                "gi": ("dft_out", 2 * FQ, P),
            }
            S["weight_loads"] = []
            for name, (src, c, p) in chunked.items():
                t = wb(name, [p, c, A[src].shape[1]])
                S["weight_loads"].append((t[:], A[src].rearrange("(c p) n -> p c n", p=p)))
            wb("fd", [P, NT, 2 * T])
            wb("wq1T", [P, D])
            S["weight_loads"].append((S["wq1T"][:], A["L1_WqT"]))
            wb("wfilm", [P, DC, 4 * D])
            S["weight_loads"].append((S["wfilm"][:, :, 0:2 * D], A["film_in"].rearrange("(c p) n -> p c n", p=P)))
            S["weight_loads"].append((S["wfilm"][:, :, 2 * D:4 * D], A["film_out"].rearrange("(c p) n -> p c n", p=P)))
            for name in ("b_o", "g_in", "b_in", "g_out", "b_out", "b2"):
                wb(name, [P, D])
                S["weight_loads"].append((S[name][:], A[name].partition_broadcast(P)))
            wb("route", [P, 1])
            S["weight_loads"].append((S["route"][:], A["route"].partition_broadcast(P)))
            for name, c in (("g_ffn", DC), ("b_ffn", DC), ("b1", HC)):
                wb(name, [P, c])
                S["weight_loads"].append((S[name][:], A[name]))
            wb("kf", [P, FQ, 3, D])
            wb("mgate", [P, 1])
            wb("vf", [J + 1, 4 * D])
            wb("amT", [J + 1, T])
            wb("mask_rows", [1, 2, B * J], BF16)
            wb("tmask", [P, B * NT])
            wb("power", [P, 1])
            wb("ones_bf", [1, P], BF16)
            wb("ktbd", [P, C0, P])
            wb("vtbd", [P, C0, P])
            wb("k1bd", [P, H1 * J])
            wb("sg", [P, NT, E0 + KTOP0])
            setup_block(nc, ctx, S, A, None)
            layers_block(nc, ctx, S, A, out)
        experts_block(nc, ctx, S, A, out)


def kernel(**inputs):
    import numpy as np
    import concourse.bacc as bacc
    from concourse.bass_utils import run_bass_kernel_spmd

    i = {k: np.asarray(v) for k, v in inputs.items()}
    t = np.arange(T)[:, None]
    f = np.arange(T)[None, :] + 0.5
    angle = 2.0 * np.pi * t * f / (2 * T)

    def parts(fn_c, fn_s):
        return np.stack([fn_c.reshape(T, FQ, P), fn_s.reshape(T, FQ, P)], axis=2)

    forward = parts(np.cos(angle), np.sin(angle)).reshape(T, 2 * T).astype(np.float32)
    back = (parts(np.cos(angle), np.sin(angle)) / T).transpose(1, 2, 3, 0).reshape(2 * T, T).astype(np.float32)
    arrays = {
        "x": i["x"], "ctxT": i["ctx_768"].transpose(0, 2, 1),
        "mask_k0": i["mask_BxS2_bk0"].reshape(1, -1).view(np.uint32),
        "mask_k1": i["mask_BxS2_bf1"].reshape(1, -1).view(np.uint32),
        "mask_t": np.ascontiguousarray(i["mask_BxS_bf1"].reshape(B * NT, P).T).view(np.uint32),
        "L0_WqT": i["L0_xattn_W_q"].T, "L0_Wk": i["L0_xattn_W_k"], "L0_Wv": i["L0_xattn_W_v"], "L0_Wo": i["L0_xattn_W_o"],
        "b_o": i["L0_xattn_b_o"], "sel": i["L0_ffn_expert_sel"].T,
        "keys": i["L0_ffn_keys"].transpose(1, 0, 2).reshape(D, HID), "values": i["L0_ffn_values"].reshape(HID, D),
        "route": i["L0_ffn_route_scale"],
        "L1_WqT": i["L1_xattn_Wq"].T, "L1_Wk": i["L1_xattn_Wk"], "L1_Wv": i["L1_xattn_Wv"],
        "film_in": i["L1_xattn_W_film_in"], "film_out": i["L1_xattn_W_film_out"],
        "b_film_in": i["L1_xattn_b_film_in"].reshape(1, -1), "b_film_out": i["L1_xattn_b_film_out"].reshape(1, -1),
        "g_in": i["L1_xattn_g_norm_in"], "b_in": i["L1_xattn_b_norm_in"],
        "g_out": i["L1_xattn_g_norm_out"], "b_out": i["L1_xattn_b_norm_out"],
        "g_ffn": i["L1_xattn_g_ffn"].reshape(DC, P).T, "b_ffn": i["L1_xattn_b_ffn"].reshape(DC, P).T,
        "W1": i["L1_xattn_W1"], "b1": i["L1_xattn_b1"].reshape(HC, P).T, "W2": i["L1_xattn_W2"], "b2": i["L1_xattn_b2"],
        "log_dt": i["L1_xattn_log_dt"], "A_reT": i["L1_xattn_A_re"].T, "A_imT": i["L1_xattn_A_im"].T,
        "C_reT": i["L1_xattn_C_re"].T, "C_imT": i["L1_xattn_C_im"].T, "D_skip": i["L1_xattn_D_skip"].reshape(1, -1),
        "mod_gate": i["L1_xattn_mod_gate"].reshape(1),
        "gate_w": i["L1_ffn_gate_w"].T,
        "e_gamma": i["L1_ffn_ln_gamma"].reshape(DC, P).T, "e_beta": i["L1_ffn_ln_beta"].reshape(DC, P).T,
        "fc1T": i["L1_ffn_fc1s"].transpose(0, 2, 1), "e_b1": i["L1_ffn_b1s"].reshape(E1, HC, P).transpose(2, 0, 1),
        "fc2T": i["L1_ffn_fc2s"].transpose(0, 2, 1), "e_b2": i["L1_ffn_b2s"],
        "same_expert": np.kron(np.eye(E1), np.ones((BLK, BLK))).astype(np.float32),
        "lower_block": np.kron(np.eye(E1), np.triu(np.ones((BLK, BLK)), 1)).astype(np.float32),
        "dft_in": forward, "dft_out": back,
    }
    nc = bacc.Bacc("TRN2", target_bir_lowering=False, num_devices=1)
    given, A = {}, {}
    for name, a in arrays.items():
        a = np.ascontiguousarray(a)
        given[f"in_{name}"] = a
        A[name] = nc.dram_tensor(f"in_{name}", a.shape, mybir.dt.from_np(a.dtype), kind="ExternalInput").ap()
    out = nc.dram_tensor("out_x", [B, T, D], F32, kind="ExternalOutput").ap()
    build(nc, A, out)
    r = run_bass_kernel_spmd(nc, [given], core_ids=[0])
    return r.results[0]["out_x"]
```

```python
from contextlib import ExitStack

import concourse.bass as bass
from concourse import mybir

F32 = mybir.dt.float32
BF16 = mybir.dt.bfloat16
I32 = mybir.dt.int32
U8 = mybir.dt.uint8
U32 = mybir.dt.uint32
ALU = mybir.AluOpType
ACT = mybir.ActivationFunctionType
AX = mybir.AxisListType.X

P = 128
B, T, D = 8, 512, 256
NT = T // P
DC = D // P
N = B * T
J, CD = 64, 192
CK = CD // 2
H0, DH0 = 8, 64
H1, DH1 = 4, 32
C0 = H0 * DH0 // P
E0, ES = 16, 64
HID = 1024
HC = HID // P
KTOP0 = 4
ROUNDS = 4
NS = 64
FQ = 4
LI, LJ = 32, 16
E1, CAP = 8, N // 8
CC = CAP // P
EPS = 1e-5
FAR = -1e30
OUT_OF_RANGE = -3e38
MAGIC = 1.5 * 2.0 ** 23
TWO_PI = 6.283184
TABLE_W = D + E1
PSUM_BANKS = 8


class Tally:

    def __init__(self, ctx, nc):
        self.ctx, self.nc = ctx, nc
        self.sems, self.place, self.per, self.base, self.by, self.next = {}, {}, {}, {}, {}, {}
        self.bank, self.before = {}, {}

    def declare(self, sem, events, base=0, by=1):
        self.sems[sem] = self.ctx.enter_context(self.nc.semaphore(sem))
        self.per[sem], self.base[sem], self.by[sem], self.next[sem] = len(events), base, by, 0
        for n, e in enumerate(events):
            assert e not in self.place, e
            self.place[e] = (sem, n)

    def at(self, b, *event):
        sem, n = self.place[event]
        by = self.by[sem]
        fixed = self.base[sem] + (n + 1) * by
        return self.sems[sem], (fixed if isinstance(b, int) and b == 0 else b * (self.per[sem] * by) + fixed)

    def last(self, b, *event):
        sem, n = self.place[event]
        fixed = self.base[sem] + (n + 1 - self.per[sem]) * self.by[sem]
        assert fixed > 0
        return self.sems[sem], b * (self.per[sem] * self.by[sem]) + fixed

    def tick(self, *event):
        sem, n = self.place[event]
        if event[0] == "emptied":
            return self.sems[sem], 1
        assert n == self.next[sem] % self.per[sem], (event, self.next[sem])
        self.next[sem] += 1
        return self.sems[sem], self.by[sem]


class Banks(Tally):

    def plan(self, uses, banks, tag):
        filled, emptied = {k: [] for k in banks}, {k: [] for k in banks}
        for n, u in enumerate(uses):
            k = banks[n % len(banks)]
            self.bank[u] = k
            self.before[u] = len(emptied[k])
            filled[k].append(("filled", *u))
            emptied[k].append(("emptied", *u))
        for k in banks:
            self.declare(f"{tag}_bank{k}_filled", filled[k])
            self.declare(f"{tag}_bank{k}_emptied", emptied[k], base=1)
        self.tag = tag

    def open_(self, b, *use):
        sem = f"{self.tag}_bank{self.bank[use]}_emptied"
        return self.sems[sem], b * self.per[sem] + (self.base[sem] + self.before[use])


def setup_block(nc, ctx, S, A, tally):
    with ExitStack() as tmp:
        def sb(name, shape, dt=F32):
            return tmp.enter_context(nc.sbuf_tensor(f"setup_{name}", shape, dt))

        def sem(name):
            return tmp.enter_context(nc.semaphore(name))

        QD = D // 4
        are, aim, cre, cim, ldt = (sb(n, [P, D]) for n in ("are", "aim", "cre", "cim", "ldt"))
        decay, turn, mag, den = (sb(n, [P, D]) for n in ("decay", "turn", "mag", "den"))
        alpha, beta = sb("alpha", [P, D]), sb("beta", [P, D])
        offA, offB, signA, signB = (sb(n, [P, 1]) for n in ("offA", "offB", "signA", "signB"))
        it_i, it_j = sb("it_i", [P, LI]), sb("it_j", [P, LJ])
        Us, UEs = ([sb(f"{n}{k}", [P, QD, LI]) for k in range(2)] for n in ("U", "UE"))
        US = sb("US", [P, QD, LI])
        sinA, sinB = sb("sinA", [P, 1]), sb("sinB", [P, 1])
        U, UE = Us[0], UEs[0]
        g = [UE[:].rearrange("p d i -> p (d i)")[:, k * D:(k + 1) * D] for k in range(6)]
        mf = US[0:1].rearrange("p d i -> p (d i)")[:, 0:2 * B * J].rearrange("p (a s) -> p a s", a=2)
        W, WS = sb("W", [P, QD, LJ]), sb("WS", [P, QD, LJ])
        WAs, WBs, WEs = ([sb(f"{n}{k}", [P, QD, LJ]) for k in range(2)] for n in ("WA", "WB", "WE"))
        kq = sb("kq", [P, QD, LJ])
        kd = sb("kd", [QD, 4, T])
        KT = sb("KTaps", [P, NT, D])
        dskip = sb("dskip", [1, D])
        m8w = sb("m8", [1, 2, B * J // 4], U32)
        m8 = m8w[:].bitcast(U8)
        tm8w = sb("tm8", [P, B * NT // 4], U32)
        tm8 = tm8w[:].bitcast(U8)
        pk = tmp.enter_context(nc.psum_tensor("pk", [P, 2, QD * LJ // 2], F32))
        pt = tmp.enter_context(nc.psum_tensor("pt", [P, 4, 512], F32))

        par_in, mask_in, skip_in = sem("par_in"), sem("mask_in"), sem("skip_in")
        iota_made, vec, act = sem("iota_made"), sem("vec_step"), sem("act_step")
        u_made, w_made, taps_filled, kq_made = sem("u_made"), sem("w_made"), sem("taps_filled"), sem("kq_made")
        tr_filled, tr_copied, film_in = sem("tr_filled"), sem("tr_copied"), sem("film_in")
        kt_filled, kt_copied, kf_filled = sem("kt_filled"), sem("kt_copied"), sem("kf_filled")
        w_in, ident_made = sem("w_in"), sem("ident_made")
        phased, coefficients_made, exponents_made = sem("phased"), sem("coefficients_made"), sem("exponents_made")

        block = tmp.enter_context(nc.Block())

        @block.sync
        def _(sp):
            for half in (0, NS):
                for dst, src in ((are, A["A_reT"]), (aim, A["A_imT"]), (cre, A["C_reT"]), (cim, A["C_imT"])):
                    sp.dma_start(dst[half:half + NS, :], src).then_inc(par_in, 16)
            sp.dma_start(ldt[:], A["log_dt"].partition_broadcast(P)).then_inc(par_in, 16)
            sp.dma_start(S["fd"][:], A["dft_in"].rearrange("(c p) f -> p c f", p=P)).then_inc(w_in, 16)
            sp.dma_start(dskip[:], A["D_skip"]).then_inc(skip_in, 16)
            sp.dma_start(m8w[:, 0, :], A["mask_k0"]).then_inc(mask_in, 16)
            sp.dma_start(m8w[:, 1, :], A["mask_k1"]).then_inc(mask_in, 16)
            sp.dma_start(tm8w[:], A["mask_t"]).then_inc(mask_in, 16)
            sp.dma_start(S["mgate"][:], A["mod_gate"].partition_broadcast(P)).then_inc(film_in, 16)
            sp.dma_start(S["vf"][J:J + 1, 0:2 * D], A["b_film_in"]).then_inc(film_in, 16)
            sp.dma_start(S["vf"][J:J + 1, 2 * D:4 * D], A["b_film_out"]).then_inc(film_in, 16)
            n = 0
            for dst, src in S["weight_loads"]:
                sp.dma_start(dst, src).then_inc(w_in, 16)
                n += 1
            sp.wait_ge(w_in, 16 * (n + 1))

        @block.gpsimd
        def _(g_):
            ident = S["ident"]
            g_.memset(ident[:], 0.0).then_inc(ident_made, 1)
            g_.wait_ge(ident_made, 1)
            g_.affine_select(out=ident[:], in_=ident[:], compare_op=ALU.not_equal, fill=1.0, base=0,
                             pattern=[[-1, P]], channel_multiplier=1).then_inc(ident_made, 1)
            made = [0]

            def step(ins):
                made[0] += 1
                ins.then_inc(iota_made, 1)
                g_.wait_ge(iota_made, made[0])

            g_.wait_ge(ident_made, 2)
            step(g_.iota(it_i[:], [[LJ, LI]], base=0, channel_multiplier=0, allow_small_or_imprecise_dtypes=True))
            step(g_.iota(it_j[:], [[1, LJ]], base=0, channel_multiplier=0, allow_small_or_imprecise_dtypes=True))
            for tile, first, second in ((offA, 0.25, 0.0), (offB, 0.0, 0.25), (signA, 1.0, -1.0), (signB, -1.0, -1.0)):
                step(g_.memset(tile[0:NS, :], first))
                step(g_.memset(tile[NS:P, :], second))
            step(g_.memset(S["power"][:], -0.5))
            step(g_.memset(S["ones_bf"][:], 1.0))
            step(g_.memset(S["amT"][J:J + 1, :], 1.0))
            for name in ("ktbd", "vtbd", "k1bd"):
                step(g_.memset(S[name][:], 0.0))
            step(g_.memset(S["sg"][:], -1.0))
            for q in range(4):
                if q == 0:
                    g_.wait_ge(coefficients_made, 1)
                if q >= 2:
                    g_.wait_ge(taps_filled, q - 1)
                    g_.wait_ge(w_made, q - 1)
                k = q % 2
                for o, it, m in ((UEs[k], it_i, LI), (WEs[k], it_j, LJ)):
                    g_.tensor_tensor(o[:], decay[:, q * QD:(q + 1) * QD].unsqueeze(2).to_broadcast([P, QD, m]),
                                     it[:].unsqueeze(1).to_broadcast([P, QD, m]), ALU.mult).then_inc(exponents_made, 1)

        @block.vector
        def _(v):
            n = [0]

            def step(ins):
                n[0] += 1
                ins.then_inc(vec, 1)
                v.wait_ge(vec, n[0])

            def mul(o, a, b):
                step(nc.vector.tensor_tensor(o, a, b, ALU.mult))

            def add(o, a, b):
                step(nc.vector.tensor_tensor(o, a, b, ALU.add))

            def sub(o, a, b):
                step(nc.vector.tensor_tensor(o, a, b, ALU.subtract))

            v.wait_ge(mask_in, 48)
            step(nc.vector.tensor_copy(mf, m8))
            step(nc.vector.tensor_scalar(S["mask_rows"][:], mf, -FAR, FAR, ALU.mult, ALU.add))
            step(nc.vector.tensor_scalar(S["tmask"][:], tm8, 1.0 / H1, None, ALU.mult))
            v.wait_ge(film_in, 48)
            row = S["vf"][J:J + 1, :]
            step(nc.vector.tensor_scalar(row, row, S["mgate"][J:J + 1, :], None, ALU.mult))
            for at in (0, 2 * D):
                step(nc.vector.tensor_scalar(row[:, at:at + D], row[:, at:at + D], 1.0, None, ALU.add))

            def frac(o, x, scratch):
                step(nc.vector.tensor_scalar(scratch, x, MAGIC, -MAGIC, ALU.add, ALU.add))
                sub(o, x, scratch)

            v.wait_ge(par_in, 16 * 9)
            v.wait_ge(iota_made, 17)
            v.wait_ge(act, 1)
            mul(decay[:], ldt[:], are[:])
            mul(turn[:], ldt[:], aim[:])
            step(nc.vector.tensor_scalar(turn[:], turn[:], 0.15915494309189535, None, ALU.mult))
            frac(turn[:], turn[:], g[0])
            step(nc.vector.tensor_scalar(g[1], turn[:], 0.25, None, ALU.add))
            frac(g[2], g[1], g[0])
            nc.vector.tensor_copy(g[3], turn[:]).then_inc(phased, 1)
            v.wait_ge(act, 4)
            mul(g[2], g[2], mag[:])
            mul(g[3], g[3], mag[:])
            step(nc.vector.tensor_scalar(g[2], g[2], -1.0, None, ALU.add))
            mul(den[:], are[:], are[:])
            mul(g[0], aim[:], aim[:])
            add(den[:], den[:], g[0])
            step(nc.vector.reciprocal(den[:], den[:]))
            mul(g[0], cre[:], are[:])
            mul(g[1], cim[:], aim[:])
            add(g[0], g[0], g[1])
            mul(g[4], cim[:], are[:])
            mul(g[5], cre[:], aim[:])
            sub(g[4], g[4], g[5])
            mul(g[0], g[0], den[:])
            mul(g[4], g[4], den[:])
            mul(alpha[:], g[0], g[2])
            mul(g[1], g[4], g[3])
            sub(alpha[:], alpha[:], g[1])
            mul(beta[:], g[0], g[3])
            mul(g[1], g[4], g[2])
            add(beta[:], beta[:], g[1])
            step(nc.vector.tensor_scalar(alpha[:], alpha[:], signA[:], 2.0, ALU.mult, ALU.mult))
            step(nc.vector.tensor_scalar(beta[:], beta[:], signB[:], 2.0, ALU.mult, ALU.mult))
            for o, off in ((sinA, offA), (sinB, offB)):
                step(nc.vector.tensor_scalar(o[:], off[:], TWO_PI, None, ALU.mult))
            v.sem_inc(coefficients_made, 1)

            def over(x, q, m):
                return x[:, q * QD:(q + 1) * QD].unsqueeze(2).to_broadcast([P, QD, m])

            def whole_less(o, x, off, scratch):
                step(nc.vector.tensor_scalar(scratch, x, off, MAGIC, ALU.add, ALU.add))
                return nc.vector.scalar_tensor_tensor(o, scratch, -MAGIC, x, ALU.add, ALU.subtract)

            def phases(q):
                k = q % 2
                if q >= 2:
                    v.wait_ge(taps_filled, q - 1)
                step(nc.vector.tensor_tensor(Us[k][:], over(turn, q, LI), it_i[:].unsqueeze(1).to_broadcast([P, QD, LI]), ALU.mult))
                step(whole_less(Us[k][:], Us[k][:], offA[:], US[:]))
                step(nc.vector.tensor_tensor(W[:], over(turn, q, LJ), it_j[:].unsqueeze(1).to_broadcast([P, QD, LJ]), ALU.mult))
                step(whole_less(WAs[k][:], W[:], offA[:], WS[:]))
                whole_less(WBs[k][:], W[:], offB[:], WS[:]).then_inc(phased, 1)

            def powers(q):
                k = q % 2
                WA, WB = WAs[k], WBs[k]
                v.wait_ge(act, 4 + 5 * (q + 1))
                nc.vector.tensor_tensor(Us[k][:], Us[k][:], UEs[k][:], ALU.mult).then_inc(u_made, 1)
                mul(WA[:], WA[:], over(alpha, q, LJ))
                mul(WB[:], WB[:], over(beta, q, LJ))
                add(WA[:], WA[:], WB[:])
                nc.vector.tensor_tensor(WA[:], WA[:], WEs[k][:], ALU.mult).then_inc(w_made, 1)

            for q in (0, 2):
                phases(q)
                v.wait_ge(phased, q + 2)
                phases(q + 1)
                powers(q)
                powers(q + 1)
                v.wait_ge(phased, q + 3)

            for r in range(4):
                v.wait_ge(tr_filled, r + 1)
                nc.vector.tensor_copy(
                    kd[:].rearrange("d q (i j) -> d j (q i)", j=LJ)[:, 4 * r:4 * r + 4, :],
                    pt[0:QD, r, :].rearrange("d (j x) -> d j x", j=4)).then_inc(tr_copied, 1)
            for c in range(NT):
                v.wait_ge(kt_filled, c + 1)
                nc.vector.tensor_copy(KT[:, c, :], pt[:, c, 0:D]).then_inc(kt_copied, 1)
            v.wait_ge(skip_in, 16)
            v.wait_ge(kt_copied, NT)
            nc.vector.tensor_tensor(KT[0:1, 0, :], KT[0:1, 0, :], dskip[:], ALU.add).then_inc(kt_copied, 1)
            v.wait_ge(kf_filled, NT)
            low = U[:].rearrange("p d i -> p (d i)").rearrange("p (m x) -> p m x", m=4)
            kept = US[:].rearrange("p d i -> p (d i)")[:, 0:1024].rearrange("p (m x) -> p m x", m=2)
            step(nc.vector.tensor_copy(kept, pt[:, 2:4, :]))
            qs = [pt[:, 0, :], pt[:, 1, :], kept[:, 0, :], kept[:, 1, :]]
            add(low[:, 0, :], qs[0], qs[2])
            sub(low[:, 1, :], qs[0], qs[2])
            add(low[:, 2, :], qs[1], qs[3])
            sub(low[:, 3, 0:D], qs[1][:, D:2 * D], qs[3][:, D:2 * D])
            sub(low[:, 3, D:2 * D], qs[3][:, 0:D], qs[1][:, 0:D])
            for j, combine, o, e in ((0, add, 0, 2), (1, sub, 1, 3), (2, sub, 0, 2), (3, add, 1, 3)):
                o, e = (low[:, m, :].rearrange("p (a d) -> p a d", a=2) for m in (o, e))
                combine(S["kf"][:, j, 0:2, :], o, e)
                step(nc.vector.tensor_copy(S["kf"][:, j, 2, :], S["kf"][:, j, 0, :]))

        @block.scalar
        def _(a):
            a.wait_ge(par_in, 16 * 9)
            nc.scalar.activation(ldt[:], ldt[:], ACT.Exp).then_inc(act, 1)
            a.wait_ge(phased, 1)
            nc.scalar.activation(mag[:], decay[:], ACT.Exp).then_inc(act, 1)
            nc.scalar.activation(g[2], g[2], ACT.Sin, scale=TWO_PI).then_inc(act, 1)
            nc.scalar.activation(g[3], g[3], ACT.Sin, scale=TWO_PI).then_inc(act, 1)
            for q in range(4):
                k = q % 2
                a.wait_ge(phased, q + 2)
                nc.scalar.activation(Us[k][:], Us[k][:], ACT.Sin, scale=-TWO_PI, bias=sinA[:]).then_inc(act, 1)
                nc.scalar.activation(WAs[k][:], WAs[k][:], ACT.Sin, scale=-TWO_PI, bias=sinA[:]).then_inc(act, 1)
                nc.scalar.activation(WBs[k][:], WBs[k][:], ACT.Sin, scale=-TWO_PI, bias=sinB[:]).then_inc(act, 1)
                a.wait_ge(exponents_made, 2 * q + 2)
                nc.scalar.activation(UEs[k][:], UEs[k][:], ACT.Exp).then_inc(act, 1)
                nc.scalar.activation(WEs[k][:], WEs[k][:], ACT.Exp).then_inc(act, 1)
            a.wait_ge(taps_filled, 4)
            nc.scalar.copy(kq[:].rearrange("p d j -> p (d j)").rearrange("p (a x) -> p a x", a=2), pk[:]).then_inc(kq_made, 1)

        @block.tensor
        def _(pe):
            for q in range(4):
                pe.wait_ge(u_made, q + 1)
                pe.wait_ge(w_made, q + 1)
                for d in range(QD):
                    half, at = divmod(d * LJ, QD * LJ // 2)
                    last = nc.tensor.matmul(pk[q * LI:(q + 1) * LI, half, at:at + LJ], Us[q % 2][:, d, :], WAs[q % 2][:, d, :],
                                            start=True, stop=True)
                last.then_inc(taps_filled, 1)
            pe.wait_ge(kq_made, 1)
            pe.wait_ge(ident_made, 2)
            for j in range(LJ):
                last = nc.tensor.transpose(pt[0:QD, j // 4, (j % 4) * P:(j % 4 + 1) * P], kq[:, :, j], S["ident"][:])
                if j % 4 == 3:
                    last.then_inc(tr_filled, 1)
            pe.wait_ge(tr_copied, 4)
            for c in range(NT):
                for q in range(4):
                    last = nc.tensor.transpose(pt[:, c, q * QD:(q + 1) * QD], kd[:, q, :].rearrange("d (p c) -> d c p", c=NT)[:, c, :], S["ident"][0:QD, 0:QD])
                last.then_inc(kt_filled, 1)
            pe.wait_ge(kt_copied, NT + 1)
            pe.wait_ge(w_in, 16)
            for t in range(NT):
                for part in range(2):
                    last = nc.tensor.matmul(pt[:, t, part * D:(part + 1) * D], S["fd"][:, t, part * P:(part + 1) * P],
                                            KT[:, t, :], start=True, stop=True)
                last.then_inc(kf_filled, 1)


LN_ATTN0, LN_MOE0, LN_TEXT, LN_IN, LN_FFN, LN_OUT, LN_EXPERTS, LN_TWICE = range(8)
FIRST, SECOND = range(2)
ATTEND, MLP, SECOND_LAYER = range(3)
NORMS = {FIRST: (LN_ATTN0, LN_MOE0), SECOND: (LN_TEXT, LN_IN, LN_FFN, LN_OUT, LN_EXPERTS, LN_TWICE)}
PHASE = {i: p for p, norms in NORMS.items() for i in norms}

ORDER = [
    (MLP, "mlp", 0), (SECOND_LAYER, "text"), (SECOND_LAYER, "text_scores"), (MLP, "mlp", 1),
    (SECOND_LAYER, "pick", 0), (MLP, "mlp", 2), (SECOND_LAYER, "pick", 1), (MLP, "mlp", 3),
    (SECOND_LAYER, "pick", 2), (MLP, "mlp", 4), (SECOND_LAYER, "pick", 3), (SECOND_LAYER, "pick", 4),
    (MLP, "mlp", 5), (SECOND_LAYER, "pick", 5), (SECOND_LAYER, "transform"), (ATTEND, "keys"), (ATTEND, "norm"),
    (SECOND_LAYER, "spectrum"), (ATTEND, "attend", 0), (ATTEND, "attend", 1), (SECOND_LAYER, "spectrum_back"),
    (SECOND_LAYER, "back", 0), (SECOND_LAYER, "back", 1), (SECOND_LAYER, "back", 2), (SECOND_LAYER, "back", 3),
    (ATTEND, "attend", 2), (ATTEND, "attend", 3), (ATTEND, "attend", 4), (SECOND_LAYER, "back", 4),
    (SECOND_LAYER, "ffn"), (SECOND_LAYER, "gelu", 0), (SECOND_LAYER, "gelu", 1), (SECOND_LAYER, "gelu", 2),
    (ATTEND, "attend", 5), (SECOND_LAYER, "gelu", 3), (ATTEND, "route"), (ATTEND, "gates"),
    (SECOND_LAYER, "ffn_out", 0), (SECOND_LAYER, "ffn_out", 1), (SECOND_LAYER, "ffn_out", 2),
    (SECOND_LAYER, "ffn_out", 3), (SECOND_LAYER, "ffn_out", 4), (SECOND_LAYER, "ffn_out", 5),
    (SECOND_LAYER, "scores"), (SECOND_LAYER, "table"),
]


def take_stages(stages, *batches):
    for phase, name, *t in ORDER:
        b = batches[phase]
        if b is not None and name in stages:
            stages[name](b, *t)


def layer_uses(phase):
    if phase == FIRST:
        uses = [("KT",), ("VT",), ("M", 0), ("M", 1), ("VO", 0), ("VO", 1)] + [("zt", LN_ATTN0, t) for t in range(NT)]
        for s in range(NT + 1):
            uses += [("S", s)] if s < NT else []
            uses += [("PT", s - 1), ("O", s - 1)] if s else []
        uses += [("zt", LN_MOE0, t) for t in range(NT)] + [("LG",)]
        for s in range(NT + 1):
            uses += [("H", s, 0), ("H", s, 1)] if s < NT else []
            uses += [("HT", s - 1, 0), ("HT", s - 1, 1), ("O2", s - 1)] if s else []
        return uses
    uses = [("KV1",), ("MM1",), ("VF", 0), ("VF", 1)]
    uses += [("zt", LN_TEXT, t) for t in range(NT)] + [("S1", t) for t in range(NT)]
    for t in range(NT):
        uses += [("AT", t), ("FI", t)]
    uses += [("Q", t) for t in range(NT)]
    for t in range(NT):
        uses += [("YI", t), ("FO", t)]
    uses += [("zt", LN_FFN, t) for t in range(NT)] + [("GH", c) for c in range(HC)] + [("O3", t) for t in range(NT)]
    uses += [("zt", LN_EXPERTS, t) for t in range(NT)] + [("SC",), ("ST",)]
    return uses


def layer_signals(y):
    tiles = range(NT)
    y.declare("x_loaded", [("x_loaded",)], by=16)
    y.declare("ctx0_loaded", [("ctx0_loaded",)], by=16)
    y.declare("ctx1_loaded", [("ctx1_loaded",)], by=16)
    y.declare("x3_stored", [("x3_stored",)], base=16, by=16)
    y.declare("table_stored", [("table_stored",)], base=16, by=16)
    y.declare("scores_stored", [("scores_stored",)], base=16, by=16)
    y.declare("mask0_made", [("mask_row", 0)])
    y.declare("mask1_made", [("mask_row", 1), ("tm",)])
    for p, norms in NORMS.items():
        for name, event in (("stats_made", "stats"), ("mean_var_made", "mean_var"), ("var_eps_made", "var_eps"),
                            ("rstd_made", "rstd"), ("normed", "z")):
            y.declare(f"{name}{p}", [(event, i, t) for i in norms for t in tiles])
    y.declare("residual_biased", [("xb",)])
    y.declare("residual_taken", [("xc",)])
    y.declare("max0_made", [("mx", t) for t in tiles])
    y.declare("exp0_made", [("ex", t) for t in tiles])
    y.declare("sum0_made", [e for t in tiles for e in (("sm", t), ("rs", t))])
    y.declare("probs0_made", [("pr", t) for t in tiles])
    y.declare("gate_chain", [("sg1",), ("sig",)] + [("m8", t) for t in tiles] + [("m8p",)] + [("mr", t) for t in tiles]
             + [("gt",), ("gsum",), ("gmax",), ("grec",), ("grs",), ("gate",)])
    y.declare("top_made", [(k, t, r, h) for t in tiles for r in range(ROUNDS) for k in ("tm8", "tmr") for h in range(H1)])
    y.declare("shifted1_made", [("e1s", t) for t in tiles])
    y.declare("exp1_made", [("e1", t) for t in tiles])
    y.declare("mean1_chain", [(k, t) for t in tiles for k in ("k0", "k1", "k2", "k3", "k4", "am")])
    y.declare("in_gain_made", [e for t in tiles for e in (("ng", t), ("nb", t))])
    y.declare("film_in_scaled", [("xf1", t) for t in tiles])
    y.declare("transform_steps", [("fa",), ("fb",), ("fd1",), ("A0",), ("A2",)])
    y.declare("odd_sums_made", [("A1",), ("A3",)])
    y.declare("products_made", [(k, j) for j in range(FQ) for k in ("t1", "t2")])
    y.declare("spectrum_made", [e for j in range(FQ) for e in (("yc", j), ("ys", j))])
    y.declare("even_back_made", [("ga",), ("gb",), ("R0",), ("R2",)])
    y.declare("odd_back_made", [("gc",), ("gd1",), ("gd2",), ("R1",), ("R3",)])
    y.declare("film_out_scaled", [("r1", t) for t in tiles])
    y.declare("text_added", [e for t in tiles for e in (("r", t), ("rb", t))])
    y.declare("out_gain_made", [e for t in tiles for e in (("og", t),)])
    y.declare("x3_made", [("x3", t) for t in tiles])
    y.declare("x4_made", [("x4", t) for t in tiles])
    y.declare("t8_made", [("t8",)])



def layers_block(nc, ctx, S, A, out):
    with ExitStack() as tmp:
        def sb(name, shape, dt=F32):
            return tmp.enter_context(nc.sbuf_tensor(name, shape, dt))

        y = Banks(tmp, nc)
        half = PSUM_BANKS // 2
        for phase in (FIRST, SECOND):
            y.plan(layer_uses(phase), list(range(phase * half, (phase + 1) * half)), "layers")
        layer_signals(y)
        at, tick, open_ = y.at, y.tick, y.open_
        ps = tmp.enter_context(nc.psum_tensor("ps", [P, PSUM_BANKS, 512], F32))

        def bank(*use):
            return ps[:, y.bank[use], :]

        x, ctx0, ctx1 = S["x"], S["ctx_first"], S["ctx_second"]
        x1, z0 = sb("x_first", [P, NT, D]), sb("z_first", [P, NT, D])
        zT0 = sb("zT_first", [P, DC, T])
        ktbd, vtbd = S["ktbd"], S["vtbd"]
        m0, vo = sb("m0", [P, DC, H0 * J]), sb("vo", [P, C0, D])
        mrow0 = sb("mrow0", [1, H0, J], BF16)
        e_buf = sb("e_buf", [P, NT, 512])
        h_sb = e_buf[:].rearrange("p (a t) f -> p a (t f)", a=2)
        mx, sm, rs = (sb(n, [P, NT, H0]) for n in ("mx", "sm", "rs"))
        hT = sb("hT", [P, 2, HC, P])
        pT = hT[:, 0].rearrange("p (a c) t -> p a (c t)", a=2)
        sg, zsel = S["sg"], sb("zsel", [P, NT, E0 + KTOP0])
        m8 = sb("m8", [P, NT, 8])
        gate, g4 = sb("gate", [P, NT, E0]), sb("g4", [P, NT, 1])
        xc, xt, z1 = (sb(n, [P, NT, D]) for n in ("x_kept", "x_text", "z_second"))
        zT1 = sb("zT_second", [P, DC, T])
        k1bd, vf, amT = S["k1bd"], S["vf"], S["amT"]
        v1T = sb("v1T", [P, DC, J])
        m1 = sb("m1", [P, DC, H1 * J])
        mrow1 = sb("mrow1", [1, H1, J], BF16)
        tm = sb("tm", [P, NT])
        big = sb("big", [P, 4096])
        s1 = big[:, 2048:3072].rearrange("p (t h j) -> p t h j", t=NT, h=H1)
        e1 = big[:, 3072:4096].rearrange("p (t h j) -> p t h j", t=NT, h=H1)
        low = big[:, 0:2048].rearrange("p (m x) -> p m x", m=4)
        high = big[:, 2048:4096].rearrange("p (m x) -> p m x", m=4)
        gT = big[:].rearrange("p (c t) -> p c t", c=HC)
        work = sb("work", [P, H1, J])
        top, rest = sb("top", [P, NT, H1, 8]), sb("rest", [P, H1, 8])
        k1 = sb("k1", [P, NT, H1])
        am = sb("am", [P, NT, J])
        xf, yv, x3 = (sb(n, [P, NT, D]) for n in ("xf", "yv", "x3"))
        r, rb = xf, xt
        r3 = yv
        t8 = sb("t8", [E1, T])
        tb = sb("tb", [P, NT, TABLE_W])
        prod = [tb[:].rearrange("p t w -> p (t w)")[:, 0:1024].rearrange("p (m x) -> p m x", m=2),
                yv[:].rearrange("p t d -> p (t d)").rearrange("p (m x) -> p m x", m=2)]
        stats, mv, ve, rstd = ([sb(f"{n}{p}", [P, NT, w]) for p in NORMS] for n, w in (
            ("stats", 6), ("mv", 2), ("ve", 1), ("rstd", 1)))
        ident = S["ident"]

        x_h = A["x"].rearrange("b (p t) d -> b p t d", t=NT)
        out_h = out.rearrange("b (p t) d -> b p t d", t=NT)
        table_h = S["table"].rearrange("(b p t) w -> b p t w", p=P, t=NT)
        scores_h = S["scores"].rearrange("e (b t) -> b e t", b=B)
        ctx_h = A["ctxT"].rearrange("b (k p) j -> b p k j", k=2)
        t8_tiles = t8[:].rearrange("e (p t) -> e t p", t=NT)

        passed = tmp.enter_context(nc.semaphore("layers_wait_passed"))

        def apart(eng):
            eng.sem_inc(passed, 1)

        block = tmp.enter_context(nc.Block())

        @block.sync
        def _(sp):
            def load_first(b, done):
                sp.wait_ge(*at(done, "filled", "VT"))
                apart(sp)
                sp.dma_start(ctx0[:], ctx_h[b]).then_inc(*tick("ctx0_loaded"))
                sp.wait_ge(*at(done, "emptied", "O2", NT - 1))
                apart(sp)
                sp.dma_start(x[:], x_h[b]).then_inc(*tick("x_loaded"))

            def load_second(b, done):
                sp.wait_ge(*at(done, "filled", "KV1"))
                apart(sp)
                sp.dma_start(ctx1[:], ctx_h[b]).then_inc(*tick("ctx1_loaded"))

            def store(b):
                sp.wait_ge(*at(b, "t8"))
                apart(sp)
                sp.dma_start(scores_h[b], t8[:]).then_inc(*tick("scores_stored"))
                sp.wait_ge(*at(b, "x4", NT - 1))
                apart(sp)
                sp.dma_start(out_h[b], x3[:]).then_inc(*tick("x3_stored"))
                sp.wait_ge(*at(b, "emptied", "ST"))
                apart(sp)
                sp.wait_ge(*at(b, "z", LN_TWICE, NT - 1))
                apart(sp)
                sp.dma_start(table_h[b], tb[:]).then_inc(*tick("table_stored"))

            for s in ("x3_stored", "table_stored", "scores_stored"):
                sp.sem_inc(y.sems[s], 16)
            for s in ("x_loaded", "ctx0_loaded", "ctx1_loaded"):
                tick(s)
                sp.sem_inc(y.sems[s], 16)
            load_first(1, 0)
            with sp.Fori(0, B - 2) as b:
                load_second(b + 1, b)
                load_first(b + 2, b + 1)
                store(b)
            load_second(B - 1, B - 2)
            store(B - 2)
            store(B - 1)
            sp.wait_ge(*at(B - 1, "x3_stored"))
            sp.wait_ge(*at(B - 1, "table_stored"))
            sp.wait_ge(*at(B - 1, "scores_stored"))

        def trips(eng, stages):
            take_stages(stages, 0, None, None)
            take_stages(stages, 1, 0, None)
            with eng.Fori(0, B - 2) as b:
                take_stages(stages, b + 2, b + 1, b)
            take_stages(stages, None, B - 1, B - 2)
            take_stages(stages, None, None, B - 1)

        @block.gpsimd
        def _(g):
            for k in range(PSUM_BANKS):
                g.sem_inc(y.sems[f"layers_bank{k}_emptied"], 1)

            def rstd_of(b, i, t):
                p = PHASE[i]
                g.wait_ge(*at(b, "mean_var", i, t))
                apart(g)
                nc.gpsimd.tensor_scalar(ve[p][:, t, :], mv[p][:, t, 1:2], EPS, None, ALU.add).then_inc(*tick("var_eps", i, t))
                g.wait_ge(*at(b, "var_eps", i, t))
                nc.gpsimd.tensor_tensor(rstd[p][:, t, :], ve[p][:, t, :], S["power"][:], ALU.pow).then_inc(*tick("rstd", i, t))

            def norm_first(b):
                for t in range(NT):
                    rstd_of(b, LN_ATTN0, t)
                g.wait_ge(*at(b, "z", LN_ATTN0, NT - 1))
                nc.gpsimd.tensor_tensor(x[:], x[:], S["b_o"][:].unsqueeze(1).to_broadcast([P, NT, D]),
                                        ALU.add).then_inc(*tick("xb"))

            def attend(b, t):
                if 0 < t <= NT:
                    u = t - 1
                    g.wait_ge(*at(b, "rs", u))
                    nc.gpsimd.tensor_tensor(e_buf[:, u, :].rearrange("p (h j) -> p h j", h=H0),
                                            e_buf[:, u, :].rearrange("p (h j) -> p h j", h=H0),
                                            rs[:, u, :].unsqueeze(2).to_broadcast([P, H0, J]),
                                            ALU.mult).then_inc(*tick("pr", u))
                if t > 1:
                    rstd_of(b, LN_MOE0, t - 2)

            def text(b):
                g.wait_ge(*at(b, "emptied", "O2", NT - 1))
                nc.gpsimd.tensor_tensor(xc[:], x1[:], S["b_out"][:].unsqueeze(1).to_broadcast([P, NT, D]),
                                        ALU.add).then_inc(*tick("xc"))
                for t in range(NT):
                    rstd_of(b, LN_TEXT, t)
                for t in range(NT):
                    rstd_of(b, LN_IN, t)

            def pick(b, t):
                if t < NT:
                    g.wait_ge(*at(b, "z", LN_IN, t))
                    nc.gpsimd.tensor_tensor(z1[:, t, :], z1[:, t, :], S["g_in"][:], ALU.mult).then_inc(*tick("ng", t))
                    g.wait_ge(*at(b, "ng", t))
                    nc.gpsimd.tensor_tensor(z1[:, t, :], z1[:, t, :], S["b_in"][:], ALU.add).then_inc(*tick("nb", t))
                    g.wait_ge(*at(b, "tm8", t, 0, H1 - 1))
                    g.wait_ge(*at(b, "emptied", "S1", t))
                    nc.gpsimd.tensor_tensor(e1[:, t], s1[:, t], top[:, t, :, 0:1].to_broadcast([P, H1, J]),
                                            ALU.subtract).then_inc(*tick("e1s", t))

            def spectrum(b):
                g.wait_ge(*at(b, "emptied", "Q", 1))
                nc.gpsimd.tensor_tensor(high[:, 1, :], low[:, 1, :], low[:, 3, :], ALU.subtract).then_inc(*tick("A1"))
                nc.gpsimd.tensor_tensor(high[:, 3, :], low[:, 1, :], low[:, 3, :], ALU.add).then_inc(*tick("A3"))
                g.wait_ge(*at(b, "A3"))
                for j in range(FQ):
                    g.wait_ge(*at(b, "t2", j))
                    nc.gpsimd.tensor_tensor(low[:, j, 0:D], prod[j % 2][:, 0, 0:D], prod[j % 2][:, 0, D:2 * D],
                                            ALU.subtract).then_inc(*tick("yc", j))
                    nc.gpsimd.tensor_tensor(low[:, j, D:2 * D], prod[j % 2][:, 1, 0:D],
                                            prod[j % 2][:, 1, D:2 * D], ALU.add).then_inc(*tick("ys", j))

            def spectrum_back(b):
                g.wait_ge(*at(b, "ys", FQ - 1))
                nc.gpsimd.tensor_tensor(high[:, 1, :], low[:, 0, :], low[:, 2, :], ALU.subtract).then_inc(*tick("gc"))
                nc.gpsimd.tensor_tensor(high[:, 3, 0:D], low[:, 1, D:2 * D], low[:, 3, D:2 * D], ALU.subtract).then_inc(*tick("gd1"))
                nc.gpsimd.tensor_tensor(high[:, 3, D:2 * D], low[:, 3, 0:D], low[:, 1, 0:D], ALU.subtract).then_inc(*tick("gd2"))
                g.wait_ge(*at(b, "gb"))
                g.wait_ge(*at(b, "gd2"))
                nc.gpsimd.tensor_tensor(low[:, 1, :], high[:, 1, :], high[:, 3, :], ALU.add).then_inc(*tick("R1"))
                nc.gpsimd.tensor_tensor(low[:, 3, :], high[:, 1, :], high[:, 3, :], ALU.subtract).then_inc(*tick("R3"))

            def back(b, t):
                if t < NT:
                    g.wait_ge(*at(b, "emptied", "FO", t))
                    nc.gpsimd.tensor_tensor(r[:, t, :], r[:, t, :], xt[:, t, :], ALU.add).then_inc(*tick("r", t))
                    g.wait_ge(*at(b, "r", t))
                    nc.gpsimd.tensor_tensor(rb[:, t, :], r[:, t, :], S["b2"][:], ALU.add).then_inc(*tick("rb", t))
                if t:
                    rstd_of(b, LN_FFN, t - 1)

            def ffn_out(b, t):
                if t < NT:
                    rstd_of(b, LN_OUT, t)
                if 0 < t <= NT:
                    g.wait_ge(*at(b, "z", LN_OUT, t - 1))
                    nc.gpsimd.tensor_tensor(z1[:, t - 1, :], z1[:, t - 1, :], S["g_out"][:], ALU.mult).then_inc(*tick("og", t - 1))

            def scores(b):
                for t in range(NT):
                    rstd_of(b, LN_EXPERTS, t)

            def table(b):
                for t in range(NT):
                    g.wait_ge(*at(b, "z", LN_EXPERTS, t))
                    nc.gpsimd.tensor_tensor(x3[:, t, :], x3[:, t, :], z1[:, t, :], ALU.add).then_inc(*tick("x4", t))
                    rstd_of(b, LN_TWICE, t)

            trips(g, {"norm": norm_first, "attend": attend, "text": text, "pick": pick, "spectrum": spectrum,
                      "spectrum_back": spectrum_back, "back": back, "ffn_out": ffn_out, "scores": scores, "table": table})

        @block.vector
        def _(v):
            def stats_of(b, i, t, src):
                p = PHASE[i]
                nc.vector.bn_stats(stats[p][:, t, :], src[:, t, :]).then_inc(*tick("stats", i, t))
                v.wait_ge(*at(b, "stats", i, t))
                apart(v)
                nc.vector.bn_aggr(mv[p][:, t, :], stats[p][:, t, :]).then_inc(*tick("mean_var", i, t))

            def norm(b, i, t, src, dst):
                p = PHASE[i]
                v.wait_ge(*at(b, "rstd", i, t))
                nc.vector.tensor_scalar(dst, src[:, t, :], mv[p][:, t, 0:1], rstd[p][:, t, :], ALU.subtract,
                                        ALU.mult).then_inc(*tick("z", i, t))

            def heads(ap, h):
                return ap.rearrange("p (h j) -> p h j", h=h)

            def norm_first(b):
                nc.vector.tensor_copy(mrow0[:], S["mask_rows"][:, 0, bass.ds(b * J, J)].unsqueeze(1).to_broadcast([1, H0, J])).then_inc(*tick("mask_row", 0))
                v.wait_ge(*at(b, "x_loaded"))
                for t in range(NT + 1):
                    if t < NT:
                        stats_of(b, LN_ATTN0, t, x)
                    if t:
                        norm(b, LN_ATTN0, t - 1, x, z0[:, t - 1, :])

            def attend(b, t):
                if 0 < t <= NT:
                    v.wait_ge(*at(b, "ex", t - 1))
                    nc.vector.tensor_reduce(sm[:, t - 1, :], heads(e_buf[:, t - 1, :], H0), AX, ALU.add).then_inc(*tick("sm", t - 1))
                    v.wait_ge(*at(b, "sm", t - 1))
                    nc.vector.reciprocal(rs[:, t - 1, :], sm[:, t - 1, :]).then_inc(*tick("rs", t - 1))
                if t < NT:
                    v.wait_ge(*at(b, "filled", "S", t))
                    nc.vector.tensor_reduce(mx[:, t, :], heads(bank("S", t), H0), AX, ALU.max).then_inc(*tick("mx", t))
                    v.wait_ge(*at(b, "mx", t))
                    nc.vector.tensor_tensor(heads(e_buf[:, t, :], H0), heads(bank("S", t), H0),
                                            mx[:, t, :].unsqueeze(2).to_broadcast([P, H0, J]),
                                            ALU.subtract).then_inc(*tick("emptied", "S", t))
                if t > 1:
                    u = t - 2
                    v.wait_ge(*at(b, "filled", "O", u))
                    v.wait_ge(*at(b, "xb"))
                    nc.vector.tensor_tensor(x[:, u, :], x[:, u, :], bank("O", u)[:, 0:D], ALU.add).then_inc(*tick("emptied", "O", u))
                    v.wait_ge(*at(b, "emptied", "O", u))
                    stats_of(b, LN_MOE0, u, x)
                    if u:
                        norm(b, LN_MOE0, u - 1, x, z0[:, u - 1, :])

            def route(b):
                norm(b, LN_MOE0, NT - 1, x, z0[:, NT - 1, :])

            def gates(b):
                v.wait_ge(*at(b, "emptied", "LG"))
                nc.vector.tensor_scalar(sg[:, :, 0:E0], sg[:, :, 0:E0], 1.0, None, ALU.add).then_inc(*tick("sg1"))
                v.wait_ge(*at(b, "sg1"))
                nc.vector.reciprocal(sg[:, :, 0:E0], sg[:, :, 0:E0]).then_inc(*tick("sig"))
                v.wait_ge(*at(b, "sig"))
                apart(v)
                for t in range(NT):
                    nc.vector.max(m8[:, t, :], sg[:, t, 0:E0]).then_inc(*tick("m8", t))
                v.wait_ge(*at(b, "m8", NT - 1))
                nc.vector.memset(m8[:, :, KTOP0:8], -1.0).then_inc(*tick("m8p"))
                v.wait_ge(*at(b, "m8p"))
                apart(v)
                for t in range(NT):
                    nc.vector.match_replace(zsel[:, t, :], m8[:, t, :], sg[:, t, :], -2.0).then_inc(*tick("mr", t))
                v.wait_ge(*at(b, "mr", NT - 1))
                nc.vector.scalar_tensor_tensor(gate[:], zsel[:, :, 0:E0], -1.5, sg[:, :, 0:E0], ALU.is_lt, ALU.mult).then_inc(*tick("gt"))
                v.wait_ge(*at(b, "gt"))
                nc.vector.tensor_reduce(g4[:, :, 0], gate[:], AX, ALU.add).then_inc(*tick("gsum"))
                v.wait_ge(*at(b, "gsum"))
                nc.vector.tensor_scalar(g4[:], g4[:], 1e-9, None, ALU.max).then_inc(*tick("gmax"))
                v.wait_ge(*at(b, "gmax"))
                nc.vector.reciprocal(g4[:], g4[:]).then_inc(*tick("grec"))
                v.wait_ge(*at(b, "grec"))
                nc.vector.tensor_scalar(g4[:], g4[:], S["route"][:], None, ALU.mult).then_inc(*tick("grs"))
                v.wait_ge(*at(b, "grs"))
                nc.vector.tensor_tensor(gate[:], gate[:], g4[:].to_broadcast([P, NT, E0]), ALU.mult).then_inc(*tick("gate"))
                v.wait_ge(*at(b, "gate"))

            def mlp(b, t):
                if t > 1:
                    u = t - 2
                    v.wait_ge(*at(b, "filled", "O2", u))
                    if not isinstance(b, int) or b:
                        v.wait_ge(*at(b - 1, "xc"))
                    nc.vector.tensor_tensor(x1[:, u, :], x[:, u, :], bank("O2", u)[:, 0:D], ALU.add).then_inc(*tick("emptied", "O2", u))
                if t < NT:
                    for h in range(2):
                        v.wait_ge(*at(b, "filled", "H", t, h))
                        if t == 0:
                            v.wait_ge(*at(b, "filled", "PT", NT - 1))
                        else:
                            if t >= 2:
                                v.wait_ge(*at(b, "filled", "HT", t - 2, h))
                        nc.vector.scalar_tensor_tensor(
                            h_sb[:, t % 2, h * 512:(h + 1) * 512].rearrange("p (e f) -> p e f", f=ES),
                            bank("H", t, h).rearrange("p (e f) -> p e f", f=ES), 0.0,
                            gate[:, t, 8 * h:8 * h + 8].unsqueeze(2).to_broadcast([P, 8, ES]),
                            ALU.max, ALU.mult).then_inc(*tick("emptied", "H", t, h))

            def text(b):
                nc.vector.tensor_copy(mrow1[:], S["mask_rows"][:, 1, bass.ds(b * J, J)].unsqueeze(1).to_broadcast([1, H1, J])).then_inc(*tick("mask_row", 1))
                nc.vector.tensor_copy(tm[:], S["tmask"][:, bass.ds(b * NT, NT)]).then_inc(*tick("tm"))
                v.wait_ge(*at(b, "emptied", "O2", NT - 1))
                for t in range(NT + 1):
                    if t < NT:
                        stats_of(b, LN_TEXT, t, x1)
                    if t:
                        norm(b, LN_TEXT, t - 1, x1, xt[:, t - 1, :])
                for t in range(NT + 1):
                    if t < NT:
                        v.wait_ge(*at(b, "z", LN_TEXT, t))
                        stats_of(b, LN_IN, t, xt)
                    if t:
                        norm(b, LN_IN, t - 1, xt, z1[:, t - 1, :])

            def pick(b, t):
                if t < NT:
                    v.wait_ge(*at(b, "emptied", "S1", t))
                    apart(v)
                    for n in range(ROUNDS):
                        for h in range(H1):
                            if n:
                                v.wait_ge(*at(b, "tmr", t, n - 1, h))
                                apart(v)
                            nc.vector.max(rest[:, h, :] if n else top[:, t, h, :],
                                          work[:, h, :] if n else s1[:, t, h, :]).then_inc(*tick("tm8", t, n, h))
                        for h in range(H1):
                            v.wait_ge(*at(b, "tm8", t, n, h))
                            apart(v)
                            nc.vector.match_replace(work[:, h, :], rest[:, h, :] if n else top[:, t, h, :],
                                                    work[:, h, :] if n else s1[:, t, h, :],
                                                    OUT_OF_RANGE).then_inc(*tick("tmr", t, n, h))
                    v.wait_ge(*at(b, "e1", t))
                    v.wait_ge(*at(b, "tmr", t, ROUNDS - 1, H1 - 1))
                    nc.vector.scalar_tensor_tensor(e1[:, t], work[:], OUT_OF_RANGE / 2, e1[:, t], ALU.is_lt,
                                                   ALU.mult).then_inc(*tick("k0", t))
                    v.wait_ge(*at(b, "k0", t))
                    nc.vector.tensor_reduce(k1[:, t, :], e1[:, t], AX, ALU.add).then_inc(*tick("k1", t))
                    v.wait_ge(*at(b, "k1", t))
                    nc.vector.reciprocal(k1[:, t, :], k1[:, t, :]).then_inc(*tick("k2", t))
                    v.wait_ge(*at(b, "k2", t))
                    nc.vector.tensor_scalar(k1[:, t, :], k1[:, t, :], tm[:, t:t + 1], None, ALU.mult).then_inc(*tick("k3", t))
                    v.wait_ge(*at(b, "k3", t))
                    nc.vector.tensor_tensor(e1[:, t], e1[:, t], k1[:, t, :].unsqueeze(2).to_broadcast([P, H1, J]),
                                            ALU.mult).then_inc(*tick("k4", t))
                    v.wait_ge(*at(b, "k4", t))
                    nc.vector.tensor_reduce(am[:, t, :], e1[:, t].rearrange("p h j -> p j h"), AX, ALU.add).then_inc(*tick("am", t))
                if t > 1:
                    u = t - 2
                    v.wait_ge(*at(b, "filled", "FI", u))
                    v.wait_ge(*at(b, "nb", u))
                    nc.vector.tensor_tensor(xf[:, u, :], z1[:, u, :], bank("FI", u)[:, 0:D], ALU.mult).then_inc(*tick("xf1", u))
                    v.wait_ge(*at(b, "xf1", u))
                    nc.vector.tensor_tensor(xf[:, u, :], xf[:, u, :], bank("FI", u)[:, D:2 * D], ALU.add).then_inc(*tick("emptied", "FI", u))

            def spectrum(b):
                for t in range(2):
                    v.wait_ge(*at(b, "filled", "Q", t))
                    v.wait_ge(*at(b, "emptied", "Q", 2 + t))
                q = [bank("Q", 0), bank("Q", 1), high[:, 2, :], high[:, 3, :]]
                nc.vector.tensor_tensor(low[:, 0, :], q[0], q[2], ALU.add).then_inc(*tick("fa"))
                nc.vector.tensor_tensor(low[:, 1, :], q[0], q[2], ALU.subtract).then_inc(*tick("emptied", "Q", 0))
                nc.vector.tensor_tensor(low[:, 2, :], q[1], q[3], ALU.add).then_inc(*tick("fb"))
                nc.vector.tensor_tensor(low[:, 3, 0:D], q[1][:, D:2 * D], q[3][:, D:2 * D], ALU.subtract).then_inc(*tick("fd1"))
                nc.vector.tensor_tensor(low[:, 3, D:2 * D], q[3][:, 0:D], q[1][:, 0:D], ALU.subtract).then_inc(*tick("emptied", "Q", 1))
                v.wait_ge(*at(b, "fb"))
                nc.vector.tensor_tensor(high[:, 0, :], low[:, 0, :], low[:, 2, :], ALU.add).then_inc(*tick("A0"))
                nc.vector.tensor_tensor(high[:, 2, :], low[:, 0, :], low[:, 2, :], ALU.subtract).then_inc(*tick("A2"))
                v.wait_ge(*y.last(b, "table_stored"))
                made = [("A0",), ("A1",), ("A2",), ("A3",)]
                for j in range(FQ):
                    v.wait_ge(*at(b, *made[j]))
                    v.wait_ge(*at(b, "A2"))
                    if j >= 2:
                        v.wait_ge(*at(b, "ys", j - 2))
                    a = high[:, j, :].rearrange("p (a d) -> p a d", a=2)
                    for m, k in enumerate(("t1", "t2")):
                        nc.vector.tensor_tensor(prod[j % 2][:, m, :].rearrange("p (a d) -> p a d", a=2), a,
                                                S["kf"][:, j, m:m + 2, :], ALU.mult).then_inc(*tick(k, j))

            def spectrum_back(b):
                v.wait_ge(*at(b, "ys", FQ - 1))
                nc.vector.tensor_tensor(high[:, 0, :], low[:, 0, :], low[:, 2, :], ALU.add).then_inc(*tick("ga"))
                nc.vector.tensor_tensor(high[:, 2, :], low[:, 1, :], low[:, 3, :], ALU.add).then_inc(*tick("gb"))
                v.wait_ge(*at(b, "gb"))
                v.wait_ge(*at(b, "gd2"))
                nc.vector.tensor_tensor(low[:, 0, :], high[:, 0, :], high[:, 2, :], ALU.add).then_inc(*tick("R0"))
                nc.vector.tensor_tensor(low[:, 2, :], high[:, 0, :], high[:, 2, :], ALU.subtract).then_inc(*tick("R2"))

            def back(b, t):
                if t < NT:
                    v.wait_ge(*at(b, "filled", "FO", t))
                    v.wait_ge(*at(b, "emptied", "YI", t))
                    nc.vector.tensor_tensor(r[:, t, :], yv[:, t, :], bank("FO", t)[:, 0:D], ALU.mult).then_inc(*tick("r1", t))
                    v.wait_ge(*at(b, "r1", t))
                    nc.vector.tensor_tensor(r[:, t, :], r[:, t, :], bank("FO", t)[:, D:2 * D], ALU.add).then_inc(*tick("emptied", "FO", t))
                if t:
                    u = t - 1
                    v.wait_ge(*at(b, "r", u))
                    stats_of(b, LN_FFN, u, r)
                    if u:
                        norm(b, LN_FFN, u - 1, r, z1[:, u - 1, :])

            def ffn(b):
                norm(b, LN_FFN, NT - 1, r, z1[:, NT - 1, :])

            def ffn_out(b, t):
                if t == 0:
                    v.wait_ge(*y.last(b, "x3_stored"))
                if t < NT:
                    v.wait_ge(*at(b, "filled", "O3", t))
                    v.wait_ge(*at(b, "rb", t))
                    nc.vector.tensor_tensor(r3[:, t, :], rb[:, t, :], bank("O3", t)[:, 0:D], ALU.add).then_inc(*tick("emptied", "O3", t))
                    v.wait_ge(*at(b, "emptied", "O3", t))
                    stats_of(b, LN_OUT, t, r3)
                if 0 < t <= NT:
                    norm(b, LN_OUT, t - 1, r3, z1[:, t - 1, :])
                if t > 1:
                    u = t - 2
                    v.wait_ge(*at(b, "og", u))
                    nc.vector.tensor_tensor(x3[:, u, :], xc[:, u, :], z1[:, u, :], ALU.add).then_inc(*tick("x3", u))

            def scores(b):
                for t in range(NT + 1):
                    if t < NT:
                        v.wait_ge(*at(b, "x3", t))
                        stats_of(b, LN_EXPERTS, t, x3)
                    if t:
                        norm(b, LN_EXPERTS, t - 1, x3, z1[:, t - 1, :])

            def table(b):
                for t in range(NT + 1):
                    if t < NT:
                        v.wait_ge(*at(b, "z", LN_EXPERTS, t))
                        stats_of(b, LN_TWICE, t, z1)
                    if t:
                        norm(b, LN_TWICE, t - 1, z1, tb[:, t - 1, 0:D])
                v.wait_ge(*at(b, "emptied", "SC"))
                nc.vector.tensor_scalar(t8[:], t8[:], 1.0, None, ALU.add).then_inc(*tick("t8"))
                v.wait_ge(*at(b, "filled", "ST"))
                nc.vector.tensor_copy(tb[:, :, D:TABLE_W], bank("ST")[:, 0:NT * E1].rearrange("p (t e) -> p t e", t=NT)).then_inc(*tick("emptied", "ST"))

            trips(v, {"norm": norm_first, "attend": attend, "route": route, "mlp": mlp, "text": text, "pick": pick,
                      "gates": gates, "spectrum": spectrum, "spectrum_back": spectrum_back, "back": back, "ffn": ffn,
                      "ffn_out": ffn_out, "scores": scores, "table": table})

        @block.scalar
        def _(a):
            def evacuate(b, dst, src, *use):
                a.wait_ge(*at(b, "filled", *use))
                nc.scalar.copy(dst, src).then_inc(*tick("emptied", *use))

            def transposed(b, i, t):
                zT = (zT0, zT1)[PHASE[i]]
                evacuate(b, zT[:, :, t * P:(t + 1) * P], bank("zt", i, t)[:, 0:D].rearrange("p (k n) -> p k n", k=DC), "zt", i, t)

            def keys(b):
                for use, dst in (("KT", ktbd), ("VT", vtbd)):
                    a.wait_ge(*at(b, "filled", use))
                    src = bank(use)[:, 0:C0 * J].rearrange("p (c j) -> p c j", c=C0)
                    nc.scalar.copy(dst[0:64, :, 0:J], src[0:64])
                    nc.scalar.copy(dst[64:P, :, J:2 * J], src[64:P]).then_inc(*tick("emptied", use))
                for k in range(DC):
                    a.wait_ge(*at(b, "filled", "M", k))
                    nc.scalar.mul(m0[:, k, :], bank("M", k), DH0 ** -0.5).then_inc(*tick("emptied", "M", k))
                for k in range(2):
                    evacuate(b, vo[:, 2 * k:2 * k + 2, :], bank("VO", k).rearrange("p (c d) -> p c d", c=2), "VO", k)

            def norm_first(b):
                for t in range(NT):
                    transposed(b, LN_ATTN0, t)

            def attend(b, t):
                if t < NT:
                    a.wait_ge(*at(b, "emptied", "S", t))
                    nc.scalar.activation(e_buf[:, t, :], e_buf[:, t, :], ACT.Exp).then_inc(*tick("ex", t))
                if 0 < t <= NT:
                    evacuate(b, pT[:, (t - 1) % 2, :], bank("PT", t - 1), "PT", t - 1)

            def route(b):
                for t in range(NT):
                    transposed(b, LN_MOE0, t)
                a.wait_ge(*at(b, "filled", "LG"))
                nc.scalar.activation(sg[:, :, 0:E0], bank("LG")[:, 0:NT * E0].rearrange("p (t e) -> p t e", t=NT),
                                     ACT.Exp, scale=-1.0).then_inc(*tick("emptied", "LG"))

            def mlp(b, t):
                if 0 < t <= NT:
                    for h in range(2):
                        evacuate(b, hT[:, (t - 1) % 2, 4 * h:4 * h + 4, :], bank("HT", t - 1, h).rearrange("p (c n) -> p c n", c=4), "HT", t - 1, h)

            def text(b):
                a.wait_ge(*at(b, "filled", "KV1"))
                for h in range(H1):
                    rows = slice(h * DH1, (h + 1) * DH1)
                    nc.scalar.copy(k1bd[rows, h * J:(h + 1) * J], bank("KV1")[rows, 0:J])
                nc.scalar.copy(v1T[:], bank("KV1")[:, J:3 * J].rearrange("p (k j) -> p k j", k=DC)).then_inc(*tick("emptied", "KV1"))
                a.wait_ge(*at(b, "filled", "MM1"))
                nc.scalar.mul(m1[:], bank("MM1").rearrange("p (k s) -> p k s", k=DC), DH1 ** -0.5).then_inc(*tick("emptied", "MM1"))
                for k in range(2):
                    a.wait_ge(*at(b, "filled", "VF", k))
                    nc.scalar.mul(vf[0:J, k * 512:(k + 1) * 512], bank("VF", k)[0:J, :], S["mgate"][0:J, :]).then_inc(*tick("emptied", "VF", k))

            def text_scores(b):
                for t in range(NT):
                    transposed(b, LN_TEXT, t)
                for t in range(NT):
                    evacuate(b, s1[:, t], bank("S1", t)[:, 0:H1 * J].rearrange("p (h j) -> p h j", h=H1), "S1", t)

            def pick(b, t):
                if 0 < t <= NT:
                    evacuate(b, amT[0:J, (t - 1) * P:t * P], bank("AT", t - 1)[0:J, 0:P], "AT", t - 1)
                if t < NT:
                    a.wait_ge(*at(b, "e1s", t))
                    nc.scalar.activation(e1[:, t], e1[:, t], ACT.Exp).then_inc(*tick("e1", t))

            def transform(b):
                for t in (2, 3):
                    evacuate(b, high[:, t, :], bank("Q", t), "Q", t)

            def back(b, t):
                if t < NT:
                    evacuate(b, yv[:, t, :], bank("YI", t)[:, 0:D], "YI", t)

            def ffn(b):
                for t in range(NT):
                    a.wait_ge(*at(b, "filled", "zt", LN_FFN, t))
                    for k in range(DC):
                        last = nc.scalar.activation(zT1[:, k, t * P:(t + 1) * P], bank("zt", LN_FFN, t)[:, k * P:(k + 1) * P],
                                                    ACT.Identity, bias=S["b_ffn"][:, k:k + 1], scale=S["g_ffn"][:, k:k + 1])
                    last.then_inc(*tick("emptied", "zt", LN_FFN, t))

            def gelu(b, pair):
                for c in (2 * pair, 2 * pair + 1):
                    a.wait_ge(*at(b, "filled", "GH", c))
                    nc.scalar.activation(gT[:, c, :], bank("GH", c), ACT.Gelu, bias=S["b1"][:, c:c + 1]).then_inc(*tick("emptied", "GH", c))

            def scores(b):
                for t in range(NT):
                    transposed(b, LN_EXPERTS, t)
                a.wait_ge(*at(b, "filled", "SC"))
                a.wait_ge(*y.last(b, "scores_stored"))
                nc.scalar.activation(t8_tiles, bank("SC")[0:E1, :].rearrange("e (t p) -> e t p", t=NT), ACT.Tanh).then_inc(*tick("emptied", "SC"))

            trips(a, {"keys": keys, "norm": norm_first, "attend": attend, "route": route, "mlp": mlp, "text": text,
                      "text_scores": text_scores, "pick": pick, "transform": transform, "back": back, "ffn": ffn,
                      "gelu": gelu, "scores": scores})

        @block.tensor
        def _(pe):
            def product(b, *use, parts):
                pe.wait_ge(*open_(b, *use))
                for o, l, r_, start, stop in parts:
                    last = nc.tensor.matmul(o, l, r_, start=start, stop=stop)
                last.then_inc(*tick("filled", *use))

            def transposes(b, *use, parts):
                pe.wait_ge(*open_(b, *use))
                for o, i in parts:
                    last = nc.tensor.transpose(o, i, ident[:])
                last.then_inc(*tick("filled", *use))

            def contract(o, pairs):
                n = len(pairs)
                return [(o, l, r_, k == 0, k == n - 1) for k, (l, r_) in enumerate(pairs)]

            def transpose_norm(b, i, t, src):
                transposes(b, "zt", i, t, parts=[(bank("zt", i, t)[:, k * P:(k + 1) * P], src[:, t, k * P:(k + 1) * P]) for k in range(DC)])

            def keys(b):
                pe.wait_ge(*at(b, "ctx0_loaded"))
                for use, w in (("KT", S["wk"]), ("VT", S["wv"])):
                    o = bank(use)
                    product(b, use, parts=[p for c in range(C0) for p in contract(
                        o[:, c * J:(c + 1) * J], [(w[:, k, c * P:(c + 1) * P], ctx0[:, k, :]) for k in range(2)])])
                pe.wait_ge(*at(b, "emptied", "KT"))
                for k in range(DC):
                    product(b, "M", k, parts=[p for c in range(C0) for p in contract(
                        bank("M", k)[:, c * P:(c + 1) * P], [(S["wqT"][:, c, k * P:(k + 1) * P], ktbd[:, c, :])])])
                pe.wait_ge(*at(b, "emptied", "VT"))
                for k in range(2):
                    product(b, "VO", k, parts=[p for c in range(2) for p in contract(
                        bank("VO", k)[:, c * D:(c + 1) * D], [(vtbd[:, 2 * k + c, :], S["wo"][:, 2 * k + c, :])])])

            def norm_first(b):
                for t in range(NT):
                    pe.wait_ge(*at(b, "z", LN_ATTN0, t))
                    transpose_norm(b, LN_ATTN0, t, z0)

            def attend(b, s):
                if s == 0:
                    pe.wait_ge(*at(b, "emptied", "M", 1))
                    pe.wait_ge(*at(b, "mask_row", 0))
                if s < NT:
                    pe.wait_ge(*at(b, "emptied", "zt", LN_ATTN0, s))
                    product(b, "S", s, parts=contract(bank("S", s), [
                        (S["ones_bf"][:], mrow0[:].rearrange("o h j -> o (h j)"))] + [
                        (zT0[:, k, s * P:(s + 1) * P], m0[:, k, :]) for k in range(DC)]))
                if 0 < s <= NT:
                    t = s - 1
                    pe.wait_ge(*at(b, "pr", t))
                    transposes(b, "PT", t, parts=[(bank("PT", t)[:, c * P:(c + 1) * P], e_buf[:, t, c * P:(c + 1) * P]) for c in range(C0)])
                    pe.wait_ge(*at(b, "emptied", "VO", 1))
                    pe.wait_ge(*at(b, "emptied", "PT", t))
                    product(b, "O", t, parts=contract(bank("O", t)[:, 0:D], [
                        (pT[:, t % 2, c * P:(c + 1) * P], vo[:, c, :]) for c in range(C0)]))

            def route(b):
                for t in range(NT):
                    pe.wait_ge(*at(b, "z", LN_MOE0, t))
                    transpose_norm(b, LN_MOE0, t, z0)
                pe.wait_ge(*at(b, "emptied", "zt", LN_MOE0, NT - 1))
                product(b, "LG", parts=[p for t in range(NT) for p in contract(bank("LG")[:, t * E0:(t + 1) * E0], [
                    (zT0[:, k, t * P:(t + 1) * P], S["sel"][:, k, :]) for k in range(DC)])])

            def mlp(b, s):
                if s < NT:
                    for h in range(2):
                        product(b, "H", s, h, parts=contract(bank("H", s, h), [
                            (zT0[:, k, s * P:(s + 1) * P], S["keys"][:, k, h * 512:(h + 1) * 512]) for k in range(DC)]))
                if 0 < s <= NT:
                    t = s - 1
                    for h in range(2):
                        pe.wait_ge(*at(b, "emptied", "H", t, h))
                        transposes(b, "HT", t, h, parts=[
                            (bank("HT", t, h)[:, c * P:(c + 1) * P], h_sb[:, t % 2, (4 * h + c) * P:(4 * h + c + 1) * P]) for c in range(4)])
                    pe.wait_ge(*at(b, "emptied", "HT", t, 1))
                    product(b, "O2", t, parts=contract(bank("O2", t)[:, 0:D], [
                        (hT[:, t % 2, c, :], S["values"][:, c, :]) for c in range(HC)]))

            def text(b):
                pe.wait_ge(*at(b, "ctx1_loaded"))
                o = bank("KV1")
                product(b, "KV1", parts=contract(o[:, 0:J], [(S["wk1"][:, k, :], ctx1[:, k, :]) for k in range(2)])
                        + [p for c in range(DC) for p in contract(
                            o[:, (c + 1) * J:(c + 2) * J], [(S["wv1"][:, k, c * P:(c + 1) * P], ctx1[:, k, :]) for k in range(2)])])
                pe.wait_ge(*at(b, "emptied", "KV1"))
                product(b, "MM1", parts=[p for k in range(DC) for p in contract(
                    bank("MM1")[:, k * D:(k + 1) * D], [(S["wq1T"][:, k * P:(k + 1) * P], k1bd[:])])])
                for k in range(2):
                    product(b, "VF", k, parts=contract(bank("VF", k)[0:J, :], [
                        (v1T[:, c, :], S["wfilm"][:, c, k * 512:(k + 1) * 512]) for c in range(DC)]))

            def text_scores(b):
                for t in range(NT):
                    pe.wait_ge(*at(b, "z", LN_TEXT, t))
                    transpose_norm(b, LN_TEXT, t, xt)
                for t in range(NT):
                    pe.wait_ge(*at(b, "emptied", "zt", LN_TEXT, t))
                    if t == 0:
                        pe.wait_ge(*at(b, "emptied", "MM1"))
                        pe.wait_ge(*at(b, "mask_row", 1))
                    product(b, "S1", t, parts=contract(bank("S1", t)[:, 0:H1 * J], [
                        (S["ones_bf"][:], mrow1[:].rearrange("o h j -> o (h j)"))] + [
                        (zT1[:, k, t * P:(t + 1) * P], m1[:, k, :]) for k in range(DC)]))

            def pick(b, s):
                if 0 < s <= NT:
                    t = s - 1
                    pe.wait_ge(*at(b, "am", t))
                    pe.wait_ge(*open_(b, "AT", t))
                    apart(pe)
                    nc.tensor.transpose(bank("AT", t)[0:J, 0:P], am[:, t, :], ident[:]).then_inc(*tick("filled", "AT", t))
                    pe.wait_ge(*at(b, "emptied", "AT", t))
                    if t == 0:
                        pe.wait_ge(*at(b, "emptied", "VF", 1))
                    product(b, "FI", t, parts=contract(bank("FI", t), [(amT[:, t * P:(t + 1) * P], vf[:, 0:2 * D])]))

            def transform(b):
                pe.wait_ge(*at(b, "emptied", "FI", NT - 1))
                for t in range(NT):
                    product(b, "Q", t, parts=[(bank("Q", t)[:, part * D:(part + 1) * D], S["fd"][:, t, part * P:(part + 1) * P],
                                               xf[:, t, :], True, True) for part in range(2)])

            def back(b, t):
                made = [("R0",), ("R1",), ("R2",), ("R3",)]
                if t < NT:
                    pe.wait_ge(*at(b, *made[t]))
                    product(b, "YI", t, parts=contract(bank("YI", t)[:, 0:D], [
                        (S["gi"][:, t, part * P:(part + 1) * P], low[:, t, part * D:(part + 1) * D]) for part in range(2)]))
                    product(b, "FO", t, parts=contract(bank("FO", t), [(amT[:, t * P:(t + 1) * P], vf[:, 2 * D:4 * D])]))

            def ffn(b):
                for t in range(NT):
                    pe.wait_ge(*at(b, "z", LN_FFN, t))
                    transpose_norm(b, LN_FFN, t, z1)
                pe.wait_ge(*at(b, "emptied", "zt", LN_FFN, NT - 1))

            def gelu(b, pair):
                for c in (2 * pair, 2 * pair + 1):
                    product(b, "GH", c, parts=contract(bank("GH", c), [
                        (S["w1"][:, k, c * P:(c + 1) * P], zT1[:, k, :]) for k in range(DC)]))

            def ffn_out(b, t):
                if t < NT:
                    pe.wait_ge(*at(b, "emptied", "GH", HC - 1))
                    product(b, "O3", t, parts=contract(bank("O3", t)[:, 0:D], [
                        (gT[:, c, t * P:(t + 1) * P], S["w2"][:, c, :]) for c in range(HC)]))

            def scores(b):
                for t in range(NT):
                    pe.wait_ge(*at(b, "z", LN_EXPERTS, t))
                    transpose_norm(b, LN_EXPERTS, t, z1)
                pe.wait_ge(*at(b, "emptied", "zt", LN_EXPERTS, NT - 1))
                product(b, "SC", parts=contract(bank("SC")[0:E1, :], [(S["gate_w"][:, k, :], zT1[:, k, :]) for k in range(DC)]))

            def table(b):
                pe.wait_ge(*at(b, "t8"))
                pe.wait_ge(*open_(b, "ST"))
                apart(pe)
                for t in range(NT):
                    last = nc.tensor.transpose(bank("ST")[:, t * E1:(t + 1) * E1], t8_tiles[:, t, :], ident[0:E1, 0:E1])
                last.then_inc(*tick("filled", "ST"))

            trips(pe, {"keys": keys, "norm": norm_first, "attend": attend, "route": route, "mlp": mlp, "text": text,
                       "text_scores": text_scores, "pick": pick, "transform": transform, "back": back, "ffn": ffn,
                       "gelu": gelu, "ffn_out": ffn_out, "scores": scores, "table": table})


WAYS = 4
STEPS = 13
COUNTS = STEPS * (WAYS - 1)
HI, LO = 32, 16
BLK = P // E1
BW = N // BLK


def experts_signals(y):
    pair, chunks = range(2), range(CC)
    y.declare("indices_picked", [("idx", s) for s in pair])
    y.declare("rows0_gathered", [("rows", 0)], by=16 * CC)
    y.declare("rows1_gathered", [("rows", 1)], by=16 * CC)
    y.declare("rows_scattered", [("added", s) for s in pair], by=16 * CC)
    y.declare("expert0_loaded", [("loaded", 0)], by=64)
    y.declare("expert1_loaded", [("loaded", 1)], by=64)
    y.declare("weights_picked", [e for s in pair for e in (("wcol", s), ("whalf", s))])
    y.declare("outputs_weighted", [("ow", s, c) for s in pair for c in chunks])


def experts_block(nc, ctx, S, A, out):
    with ExitStack() as tmp:
        def sb(name, shape, dt=F32):
            return tmp.enter_context(nc.sbuf_tensor(f"experts_{name}", shape, dt))

        def sem(name):
            return tmp.enter_context(nc.semaphore(f"choose_{name}"))

        y = Banks(tmp, nc)
        uses = []
        for s in range(2):
            uses += [("zt", s, c) for c in range(CC)] + [("G", s, m) for m in range(HC)] + [("O", s, c) for c in range(CC)]
        y.plan(uses, list(range(PSUM_BANKS)), "experts")
        experts_signals(y)
        at, tick, open_ = y.at, y.tick, y.open_
        ps = tmp.enter_context(nc.psum_tensor("experts_ps", [P, PSUM_BANKS, 512], F32))

        def bank(*use):
            return ps[:, y.bank[use], :]

        ident = S["ident"]
        same, lower = sb("same", [P, P]), sb("lower", [P, P])
        sc, gt, eq, run, sel, ones = (sb(n, [P, BW]) for n in ("sc", "gt", "eq", "run", "sel", "ones"))
        lo, step_, passed_n = (sb(n, [P, 1]) for n in ("lo", "step", "candidates_passed"))
        cand, cnt, up, which = (sb(n, [P, WAYS - 1]) for n in ("cand", "cnt", "up", "which"))
        cols = sb("cols", [P, 8])
        slot = sb("slot", [P, 2, P])
        hi, lw = sb("hi", [P, 2 * P]), sb("lw", [P, 2 * P])
        hi_b, lw_b = sb("hi_b", [P, 2 * P], BF16), sb("lw_b", [P, 2 * P], BF16)
        iota_h, iota_l = sb("iota_h", [P, HI], BF16), sb("iota_l", [P, LO], BF16)
        pay_p, pay_g = sb("pay_p", [P, 1]), sb("pay_g", [P, 2, E1, BLK], BF16)
        one_hi = sb("one_hi", [P, 2 * P, HI], BF16)
        one_lo = sb("one_lo", [P, 2 * P, 2, LO], BF16)
        ids_f, ids = sb("ids_f", [HI, E1, LO]), sb("ids", [HI, E1, LO], I32)
        idx_all = sb("idx_all", [P, E1, CC], I32)
        idx = [sb(f"idx{s}", [P, CC], I32) for s in range(2)]
        rows = [sb(f"rows{s}", [P, CC, TABLE_W]) for s in range(2)]
        o = [sb(f"o{s}", [P, CC, D]) for s in range(2)]
        fc1, fc2 = [sb(f"fc1_{s}", [P, DC, HID]) for s in range(2)], [sb(f"fc2_{s}", [P, HC, D]) for s in range(2)]
        b1, b2 = [sb(f"b1_{s}", [P, HC]) for s in range(2)], [sb(f"b2_{s}", [P, D]) for s in range(2)]
        gamma, beta = sb("gamma", [P, DC]), sb("beta", [P, DC])
        yT = [sb(f"yT{s}", [P, DC, CAP]) for s in range(2)]
        hT = [sb(f"hT{s}", [P, HC, CAP]) for s in range(2)]
        wt = sb("wt", [P, 2, CC])

        c_in, aff_in, iota_made, vec = sem("in"), sem("affine_in"), sem("iota_made"), sem("vec_step")
        counted, summed, slot_made, slot_filled = sem("counted"), sem("summed"), sem("slot_made"), sem("slot_filled")
        onehot_made, list_filled, ids_made, ids_out, ids_in = (sem(n) for n in ("onehot_made", "list_filled", "ids_made", "ids_out", "ids_in"))

        low_made, groups_made = sem("low_made"), sem("groups_made")

        list_h = S["list"]
        out_rows = out.rearrange("b t d -> (b t) d")

        passed = sem("wait_passed")

        def apart(eng):
            eng.sem_inc(passed, 1)

        block = tmp.enter_context(nc.Block())

        def load_expert(sp, e, s):
            sem_, _ = tick("loaded", s)
            apart(sp)
            sp.dma_start(fc1[s][:], A["fc1T"].rearrange("e (k p) f -> e p k f", p=P)[e]).then_inc(sem_, 16)
            sp.dma_start(fc2[s][:], A["fc2T"].rearrange("e (c p) d -> e p c d", p=P)[e]).then_inc(sem_, 16)
            sp.dma_start(b1[s][:], A["e_b1"].rearrange("p e c -> e p c")[e]).then_inc(sem_, 16)
            sp.dma_start(b2[s][:], A["e_b2"][e].partition_broadcast(P)).then_inc(sem_, 16)

        @block.sync
        def _(sp):
            sp.dma_start(sc[:], S["scores"].rearrange("e (k j) -> (e k) j", j=BW)).then_inc(c_in, 16)
            sp.dma_start(same[:], A["same_expert"]).then_inc(c_in, 16)
            sp.dma_start(lower[:], A["lower_block"]).then_inc(c_in, 16)
            sp.dma_start(gamma[:], A["e_gamma"]).then_inc(aff_in, 16)
            sp.dma_start(beta[:], A["e_beta"]).then_inc(aff_in, 16)
            for s in range(2):
                load_expert(sp, s, s)
            sp.wait_ge(ids_made, 1)
            sp.dma_start(list_h.rearrange("e (h l) -> h e l", l=LO), ids[:]).then_inc(ids_out, 16)
            sp.wait_ge(ids_out, 16)
            sp.dma_start(idx_all[:], list_h.rearrange("e (p c) -> p e c", c=CC)).then_inc(ids_in, 16)
            with sp.Fori(0, E1 // 2 - 1) as b:
                for s in range(2):
                    sp.wait_ge(*at(b, "filled", "O", s, CC - 1))
                    apart(sp)
                    sp.wait_ge(*at(b, "ow", s, CC - 1))
                    load_expert(sp, b * 2 + (2 + s), s)

        @block.gpsimd
        def _(g):
            for k in range(PSUM_BANKS):
                g.sem_inc(y.sems[f"experts_bank{k}_emptied"], 1)
            g.iota(iota_h[:], [[1, HI]], base=0, channel_multiplier=0, allow_small_or_imprecise_dtypes=True).then_inc(iota_made, 1)
            g.iota(iota_l[:], [[1, LO]], base=0, channel_multiplier=0, allow_small_or_imprecise_dtypes=True).then_inc(iota_made, 1)
            g.iota(pay_p[:], [[0, 1]], base=0, channel_multiplier=1, allow_small_or_imprecise_dtypes=True).then_inc(iota_made, 1)
            g.iota(pay_g[:], [[P, 2], [0, E1], [BW, BLK]], base=0, channel_multiplier=0, allow_small_or_imprecise_dtypes=True).then_inc(iota_made, 1)
            g.memset(ones[:], 1.0).then_inc(iota_made, 1)
            g.memset(lo[:], -1.0).then_inc(iota_made, 1)
            g.memset(step_[:], 1.0).then_inc(iota_made, 1)
            g.iota(which[:], [[1, WAYS - 1]], base=1, channel_multiplier=0, allow_small_or_imprecise_dtypes=True).then_inc(iota_made, 1)
            g.wait_ge(low_made, 1)
            nc.gpsimd.tensor_tensor(one_lo[:, :, 1, :], one_lo[:, :, 0, :],
                                    pay_g[:].rearrange("p a e k -> p (a e k)").unsqueeze(2).to_broadcast([P, 2 * P, LO]),
                                    ALU.mult).then_inc(groups_made, 1)

            def gather(e, b, s, before):
                if before:
                    g.wait_ge(*at(b - 1, "ow", s, CC - 1))
                    g.wait_ge(*at(b - 1, "added", s))
                    apart(g)
                nc.gpsimd.tensor_copy(idx[s][:], idx_all[:].rearrange("p e c -> p (e c)")[:, e * CC:(e + 1) * CC] if isinstance(e, int)
                                      else idx_all[:].rearrange("p e c -> p (e c)")[:, bass.ds(e * CC, CC)]).then_inc(*tick("idx", s))
                g.wait_ge(*at(b, "idx", s))
                sem_, _ = tick("rows", s)
                apart(g)
                for c in range(CC):
                    g.indirect_dma_start(rows[s][:, c, :], None, S["table"],
                                         bass.IndirectOffsetOnAxis(ap=idx[s][:, c:c + 1], axis=0)).then_inc(sem_, 16)

            def scatter(b, s, first=False):
                g.wait_ge(*at(b, "ow", s, CC - 1))
                sem_, total = at(b, "added", s)
                if not first:
                    g.wait_ge(sem_, total - 16 * CC)
                tick("added", s)
                apart(g)
                for c in range(CC):
                    g.indirect_dma_start(out_rows, bass.IndirectOffsetOnAxis(ap=idx[s][:, c:c + 1], axis=0),
                                         o[s][:, c, :], None, compute_op=ALU.add).then_inc(sem_, 16)

            g.wait_ge(ids_in, 16)
            gather(0, 0, 0, False)
            gather(1, 0, 1, False)
            scatter(0, 0, first=True)
            with g.Fori(1, E1 // 2) as b:
                gather(b * 2, b, 0, True)
                scatter(b - 1, 1)
                gather(b * 2 + 1, b, 1, True)
                scatter(b, 0)
            scatter(E1 // 2 - 1, 1)
            g.wait_ge(*at(E1 // 2 - 1, "added", 1))

        @block.vector
        def _(v):
            n = [0]

            def step(ins):
                n[0] += 1
                ins.then_inc(vec, 1)
                v.wait_ge(vec, n[0])

            v.wait_ge(iota_made, 8)
            v.wait_ge(c_in, 48)
            with v.Fori(0, STEPS) as k:
                nc.vector.tensor_scalar(cand[:], which[:], step_[:], lo[:], ALU.mult, ALU.add).then_inc(vec, 1)
                v.wait_ge(vec, k * 4 + 1)
                for n_, hits in enumerate((gt, eq, run)):
                    nc.vector.tensor_scalar(hits[:], sc[:], cand[:, n_:n_ + 1], 0.0, ALU.is_ge, ALU.add,
                                            accum_out=cnt[:, n_:n_ + 1]).then_inc(counted, 1)
                v.wait_ge(summed, k + 1)
                nc.vector.tensor_scalar(up[:], ps[:, 0, 0:WAYS - 1], CAP - 0.5, 0.0, ALU.is_ge, ALU.add, accum_out=passed_n[:]).then_inc(vec, 1)
                v.wait_ge(vec, k * 4 + 2)
                nc.vector.scalar_tensor_tensor(lo[:], passed_n[:], step_[:], lo[:], ALU.mult, ALU.add).then_inc(vec, 1)
                v.wait_ge(vec, k * 4 + 3)
                nc.vector.tensor_scalar(step_[:], step_[:], 1.0 / WAYS, None, ALU.mult).then_inc(vec, 1)
                v.wait_ge(vec, k * 4 + 4)
            n[0] = 4 * STEPS
            step(nc.vector.tensor_scalar(gt[:], sc[:], lo[:], 0.0, ALU.is_gt, ALU.add, accum_out=cols[:, 0:1]))
            step(nc.vector.tensor_scalar(eq[:], sc[:], lo[:], 0.0, ALU.is_equal, ALU.add, accum_out=cols[:, 1:2]))
            nc.vector.tensor_tensor_scan(run[:], ones[:], eq[:], 0.0, ALU.mult, ALU.add).then_inc(counted, 1)
            v.wait_ge(summed, STEPS + 1)
            step(nc.vector.tensor_scalar(cols[:, 2:3], ps[:, 0, 0:1], -1.0, float(CAP), ALU.mult, ALU.add))
            step(nc.vector.tensor_tensor(cols[:, 2:3], cols[:, 2:3], ps[:, 0, 1:2], ALU.subtract))
            v.wait_ge(counted, COUNTS + 1)
            step(nc.vector.scalar_tensor_tensor(run[:], run[:], cols[:, 2:3], eq[:], ALU.is_le, ALU.mult))
            step(nc.vector.scalar_tensor_tensor(sel[:], gt[:], 1.0, run[:], ALU.mult, ALU.add, accum_out=cols[:, 3:4]))
            nc.vector.tensor_tensor_scan(run[:], ones[:], sel[:], 0.0, ALU.mult, ALU.add).then_inc(counted, 1)
            v.wait_ge(summed, STEPS + 2)
            v.wait_ge(counted, COUNTS + 2)
            step(nc.vector.tensor_copy(cols[:, 4:5], ps[:, 0, 0:1]))
            step(nc.vector.scalar_tensor_tensor(run[:], run[:], cols[:, 4:5], sel[:], ALU.add, ALU.mult))
            nc.vector.tensor_scalar(run[:], run[:], -1.0, None, ALU.add).then_inc(slot_made, 1)
            v.wait_ge(slot_filled, 1)
            step(nc.vector.tensor_copy(slot[:], ps[:, 1, 0:2 * P].rearrange("p (a x) -> p a x", a=2)))
            flat = slot[:].rearrange("p a x -> p (a x)")
            step(nc.vector.tensor_scalar(hi[:], flat, 1.0 / LO, -(LO - 1) / (2.0 * LO), ALU.mult, ALU.add))
            step(nc.vector.tensor_scalar(hi[:], hi[:], MAGIC, -MAGIC, ALU.add, ALU.add))
            step(nc.vector.scalar_tensor_tensor(lw[:], hi[:], -float(LO), flat, ALU.mult, ALU.add))
            step(nc.vector.tensor_copy(hi_b[:], hi[:]))
            step(nc.vector.tensor_copy(lw_b[:], lw[:]))
            nc.vector.tensor_tensor(one_lo[:, :, 0, :], lw_b[:].unsqueeze(2).to_broadcast([P, 2 * P, LO]),
                                    iota_l[:].unsqueeze(1).to_broadcast([P, 2 * P, LO]), ALU.is_equal).then_inc(low_made, 1)
            nc.vector.tensor_tensor(one_hi[:], hi_b[:].unsqueeze(2).to_broadcast([P, 2 * P, HI]),
                                    iota_h[:].unsqueeze(1).to_broadcast([P, 2 * P, HI]), ALU.is_equal).then_inc(onehot_made, 1)
            v.wait_ge(low_made, 1)
            v.wait_ge(groups_made, 1)
            nc.vector.tensor_scalar(one_lo[:, :, 0, :], one_lo[:, :, 0, :], pay_p[:], None, ALU.mult).then_inc(onehot_made, 1)
            v.wait_ge(list_filled, 1)
            pair = ps[0:HI, 2, 0:E1 * 2 * LO].rearrange("h (e a l) -> h e a l", e=E1, a=2)
            step(nc.vector.tensor_copy(ids_f[:], pair[:, :, 0, :]))
            step(nc.vector.tensor_tensor(ids_f[:], ids_f[:], pair[:, :, 1, :], ALU.add))
            nc.vector.tensor_copy(ids[:], ids_f[:]).then_inc(ids_made, 1)

            with v.Fori(0, E1 // 2) as b:
                for s in range(2):
                    v.wait_ge(*at(b, "rows", s))
                    nc.vector.tensor_copy(wt[:, s, :], rows[s][:, :, bass.ds(b * 2 + (D + s), 1)].rearrange("p c o -> p (c o)")).then_inc(*tick("wcol", s))
                    v.wait_ge(*at(b, "wcol", s))
                    nc.vector.tensor_scalar(wt[:, s, :], wt[:, s, :], 0.5, None, ALU.mult).then_inc(*tick("whalf", s))
                    v.wait_ge(*at(b, "whalf", s))
                    v.wait_ge(aff_in, 32)
                    v.wait_ge(*at(b, "loaded", s))
                    for c in range(CC + 1):
                        if c < CC:
                            v.wait_ge(*at(b, "filled", "O", s, c))
                            nc.vector.tensor_tensor(o[s][:, c, :], bank("O", s, c)[:, 0:D], b2[s][:], ALU.add).then_inc(*tick("emptied", "O", s, c))
                        if c:
                            v.wait_ge(*at(b, "emptied", "O", s, c - 1))
                            nc.vector.tensor_scalar(o[s][:, c - 1, :], o[s][:, c - 1, :], wt[:, s, c - 1:c], None, ALU.mult).then_inc(*tick("ow", s, c - 1))

        @block.scalar
        def _(a):
            a.wait_ge(aff_in, 32)
            with a.Fori(0, E1 // 2) as b:
                for s in range(2):
                    for c in range(CC):
                        a.wait_ge(*at(b, "filled", "zt", s, c))
                        for k in range(DC):
                            last = nc.scalar.activation(yT[s][:, k, c * P:(c + 1) * P], bank("zt", s, c)[:, k * P:(k + 1) * P],
                                                        ACT.Identity, bias=beta[:, k:k + 1], scale=gamma[:, k:k + 1])
                        last.then_inc(*tick("emptied", "zt", s, c))
                    a.wait_ge(*at(b, "loaded", s))
                    for m in range(HC):
                        a.wait_ge(*at(b, "filled", "G", s, m))
                        nc.scalar.activation(hT[s][:, m, :], bank("G", s, m), ACT.Gelu_apprx_tanh, bias=b1[s][:, m:m + 1]).then_inc(*tick("emptied", "G", s, m))

        @block.tensor
        def _(pe):
            pe.wait_ge(c_in, 48)
            with pe.Fori(0, STEPS) as k:
                pe.wait_ge(counted, k * (WAYS - 1) + (WAYS - 1))
                nc.tensor.matmul(ps[:, 0, 0:WAYS - 1], same[:], cnt[:], start=True, stop=True).then_inc(summed, 1)
            pe.wait_ge(counted, COUNTS + 1)
            nc.tensor.matmul(ps[:, 0, 0:1], same[:], cols[:, 0:1], start=True, stop=True)
            nc.tensor.matmul(ps[:, 0, 1:2], lower[:], cols[:, 1:2], start=True, stop=True).then_inc(summed, 1)
            pe.wait_ge(counted, COUNTS + 2)
            nc.tensor.matmul(ps[:, 0, 0:1], lower[:], cols[:, 3:4], start=True, stop=True).then_inc(summed, 1)
            pe.wait_ge(slot_made, 1)
            for a_ in range(2):
                last = nc.tensor.transpose(ps[:, 1, a_ * P:(a_ + 1) * P], run[:, a_ * P:(a_ + 1) * P], ident[:])
            last.then_inc(slot_filled, 1)
            pe.wait_ge(onehot_made, 2)
            for e in range(E1):
                for k in range(2 * BLK):
                    group = (k % 2) * P + e * BLK + k // 2
                    last = nc.tensor.matmul(ps[0:HI, 2, e * 2 * LO:(e + 1) * 2 * LO], one_hi[:, group, :],
                                            one_lo[:, group].rearrange("p a l -> p (a l)"), start=(k == 0), stop=(k == 2 * BLK - 1))
            last.then_inc(list_filled, 1)
            pe.wait_ge(ids_made, 1)

            with pe.Fori(0, E1 // 2) as b:
                for s in range(2):
                    pe.wait_ge(*at(b, "rows", s))
                    for c in range(CC):
                        pe.wait_ge(*open_(b, "zt", s, c))
                        for k in range(DC):
                            last = nc.tensor.transpose(bank("zt", s, c)[:, k * P:(k + 1) * P], rows[s][:, c, k * P:(k + 1) * P], ident[:])
                        last.then_inc(*tick("filled", "zt", s, c))
                    pe.wait_ge(*at(b, "loaded", s))
                    pe.wait_ge(*at(b, "emptied", "zt", s, CC - 1))
                    for m in range(HC):
                        pe.wait_ge(*open_(b, "G", s, m))
                        for k in range(DC):
                            last = nc.tensor.matmul(bank("G", s, m), fc1[s][:, k, m * P:(m + 1) * P], yT[s][:, k, :], start=(k == 0), stop=(k == DC - 1))
                        last.then_inc(*tick("filled", "G", s, m))
                    pe.wait_ge(*at(b, "emptied", "G", s, HC - 1))
                    for c in range(CC):
                        pe.wait_ge(*open_(b, "O", s, c))
                        for m in range(HC):
                            last = nc.tensor.matmul(bank("O", s, c)[:, 0:D], hT[s][:, m, c * P:(c + 1) * P], fc2[s][:, m, :], start=(m == 0), stop=(m == HC - 1))
                        last.then_inc(*tick("filled", "O", s, c))


def build(nc, A, out):
    with ExitStack() as ctx:
        def sb(name, shape, dt=F32):
            return ctx.enter_context(nc.sbuf_tensor(name, shape, dt))

        table = nc.dram_tensor("expert_table", [N, TABLE_W], F32, kind="Internal").ap()
        scores = nc.dram_tensor("expert_scores", [E1, N], F32, kind="Internal").ap()
        lists = nc.dram_tensor("expert_lists", [E1, CAP], I32, kind="Internal").ap()
        S = {"table": table, "scores": scores, "list": lists}
        S["ident"] = sb("ident", [P, P])
        with ExitStack() as weights:
            def wb(name, shape, dt=F32):
                S[name] = weights.enter_context(nc.sbuf_tensor(name, shape, dt))
                return S[name]

            chunked = {
                "wqT": ("L0_WqT", C0, P), "wk": ("L0_Wk", 2, CK), "wv": ("L0_Wv", 2, CK), "wo": ("L0_Wo", C0, P),
                "wk1": ("L1_Wk", 2, CK), "wv1": ("L1_Wv", 2, CK), "sel": ("sel", DC, P), "keys": ("keys", DC, P),
                "values": ("values", HC, P), "w1": ("W1", DC, P), "w2": ("W2", HC, P), "gate_w": ("gate_w", DC, P),
                "gi": ("dft_out", NT, P),
            }
            S["weight_loads"] = []
            for name, (src, c, p) in chunked.items():
                t = wb(name, [p, c, A[src].shape[1]])
                S["weight_loads"].append((t[:], A[src].rearrange("(c p) n -> p c n", p=p)))
            wb("fd", [P, NT, 2 * P])
            wb("wq1T", [P, D])
            S["weight_loads"].append((S["wq1T"][:], A["L1_WqT"]))
            wb("wfilm", [P, DC, 4 * D])
            S["weight_loads"].append((S["wfilm"][:, :, 0:2 * D], A["film_in"].rearrange("(c p) n -> p c n", p=P)))
            S["weight_loads"].append((S["wfilm"][:, :, 2 * D:4 * D], A["film_out"].rearrange("(c p) n -> p c n", p=P)))
            for name in ("b_o", "g_in", "b_in", "g_out", "b_out", "b2"):
                wb(name, [P, D])
                S["weight_loads"].append((S[name][:], A[name].partition_broadcast(P)))
            wb("route", [P, 1])
            S["weight_loads"].append((S["route"][:], A["route"].partition_broadcast(P)))
            for name, c in (("g_ffn", DC), ("b_ffn", DC), ("b1", HC)):
                wb(name, [P, c])
                S["weight_loads"].append((S[name][:], A[name]))
            wb("kf", [P, FQ, 3, D])
            wb("x", [P, NT, D])
            wb("ctx_first", [CK, 2, J])
            wb("ctx_second", [CK, 2, J])
            S["weight_loads"].append((S["x"][:], A["x"].rearrange("b (p t) d -> b p t d", t=NT)[0]))
            for name in ("ctx_first", "ctx_second"):
                S["weight_loads"].append((S[name][:], A["ctxT"].rearrange("b (k p) j -> b p k j", k=2)[0]))
            wb("mgate", [P, 1])
            wb("vf", [J + 1, 4 * D])
            wb("amT", [J + 1, T])
            wb("mask_rows", [1, 2, B * J], BF16)
            wb("tmask", [P, B * NT])
            wb("power", [P, 1])
            wb("ones_bf", [1, P], BF16)
            wb("ktbd", [P, C0, P])
            wb("vtbd", [P, C0, P])
            wb("k1bd", [P, H1 * J])
            wb("sg", [P, NT, E0 + KTOP0])
            setup_block(nc, ctx, S, A, None)
            layers_block(nc, ctx, S, A, out)
        experts_block(nc, ctx, S, A, out)


def kernel(**inputs):
    import numpy as np
    import concourse.bacc as bacc
    from concourse.bass_utils import run_bass_kernel_spmd

    i = {k: np.asarray(v) for k, v in inputs.items()}
    token = NT * np.arange(P)[None, :, None] + np.arange(NT)[:, None, None]
    angle = 2.0 * np.pi * token * (np.arange(P) + 0.5) / (2 * T)
    forward = np.concatenate([np.cos(angle), np.sin(angle)], axis=2).reshape(T, 2 * P).astype(np.float32)
    turned = angle.transpose(0, 2, 1)
    back = (np.concatenate([np.cos(turned), np.sin(turned)], axis=2) / T).reshape(NT * P, 2 * P).astype(np.float32)
    arrays = {
        "x": i["x"], "ctxT": i["ctx_768"].transpose(0, 2, 1),
        "mask_k0": i["mask_BxS2_bk0"].reshape(1, -1).view(np.uint32),
        "mask_k1": i["mask_BxS2_bf1"].reshape(1, -1).view(np.uint32),
        "mask_t": np.ascontiguousarray(i["mask_BxS_bf1"].reshape(B, P, NT).transpose(1, 0, 2).reshape(P, B * NT)).view(np.uint32),
        "L0_WqT": i["L0_xattn_W_q"].T, "L0_Wk": i["L0_xattn_W_k"], "L0_Wv": i["L0_xattn_W_v"], "L0_Wo": i["L0_xattn_W_o"],
        "b_o": i["L0_xattn_b_o"], "sel": i["L0_ffn_expert_sel"].T,
        "keys": i["L0_ffn_keys"].transpose(1, 0, 2).reshape(D, HID), "values": i["L0_ffn_values"].reshape(HID, D),
        "route": i["L0_ffn_route_scale"],
        "L1_WqT": i["L1_xattn_Wq"].T, "L1_Wk": i["L1_xattn_Wk"], "L1_Wv": i["L1_xattn_Wv"],
        "film_in": i["L1_xattn_W_film_in"], "film_out": i["L1_xattn_W_film_out"],
        "b_film_in": i["L1_xattn_b_film_in"].reshape(1, -1), "b_film_out": i["L1_xattn_b_film_out"].reshape(1, -1),
        "g_in": i["L1_xattn_g_norm_in"], "b_in": i["L1_xattn_b_norm_in"],
        "g_out": i["L1_xattn_g_norm_out"], "b_out": i["L1_xattn_b_norm_out"],
        "g_ffn": i["L1_xattn_g_ffn"].reshape(DC, P).T, "b_ffn": i["L1_xattn_b_ffn"].reshape(DC, P).T,
        "W1": i["L1_xattn_W1"], "b1": i["L1_xattn_b1"].reshape(HC, P).T, "W2": i["L1_xattn_W2"], "b2": i["L1_xattn_b2"],
        "log_dt": i["L1_xattn_log_dt"], "A_reT": i["L1_xattn_A_re"].T, "A_imT": i["L1_xattn_A_im"].T,
        "C_reT": i["L1_xattn_C_re"].T, "C_imT": i["L1_xattn_C_im"].T, "D_skip": i["L1_xattn_D_skip"].reshape(1, -1),
        "mod_gate": i["L1_xattn_mod_gate"].reshape(1),
        "gate_w": i["L1_ffn_gate_w"].T,
        "e_gamma": i["L1_ffn_ln_gamma"].reshape(DC, P).T, "e_beta": i["L1_ffn_ln_beta"].reshape(DC, P).T,
        "fc1T": i["L1_ffn_fc1s"].transpose(0, 2, 1), "e_b1": i["L1_ffn_b1s"].reshape(E1, HC, P).transpose(2, 0, 1),
        "fc2T": i["L1_ffn_fc2s"].transpose(0, 2, 1), "e_b2": i["L1_ffn_b2s"],
        "same_expert": np.kron(np.eye(E1), np.ones((BLK, BLK))).astype(np.float32),
        "lower_block": np.kron(np.eye(E1), np.triu(np.ones((BLK, BLK)), 1)).astype(np.float32),
        "dft_in": forward, "dft_out": back,
    }
    nc = bacc.Bacc("TRN2", target_bir_lowering=False, num_devices=1)
    given, A = {}, {}
    for name, a in arrays.items():
        a = np.ascontiguousarray(a)
        given[f"in_{name}"] = a
        A[name] = nc.dram_tensor(f"in_{name}", a.shape, mybir.dt.from_np(a.dtype), kind="ExternalInput").ap()
    out = nc.dram_tensor("out_x", [B, T, D], F32, kind="ExternalOutput").ap()
    build(nc, A, out)
    r = run_bass_kernel_spmd(nc, [given], core_ids=[0])
    return r.results[0]["out_x"]
```
